# Optimizing a Trainium2 kernel written in Bass

```python
import numpy as np
import jax
import jax.numpy as jnp

def _softmax(x, axis=-1):
    return jax.nn.softmax(x, axis=axis)

def _gelu(x):
    return jax.nn.gelu(x, approximate=True)

def _silu(x):
    return jax.nn.silu(x)

def _sigmoid(x):
    return jax.nn.sigmoid(x)

def _layernorm(x, axis=-1, eps=1e-05):
    m = jnp.mean(x, axis=axis, keepdims=True)
    v = jnp.var(x, axis=axis, keepdims=True)
    return (x - m) / jnp.sqrt(v + eps)

def _scatter_add(tgt, idx, src, axis=0):
    return tgt.at[idx].add(src)

def _segment_sum(src, seg, n):
    return jax.ops.segment_sum(src, seg, n)
kernel_name = 'mk_decoder_postln_d1_seqx_r4_871be3'

def setup_inputs(seed: int=0):
    np.random.seed(seed)
    _w = jnp.asarray

    def _rec_inputs():
        import jax
        import jax.numpy as jnp
        _rk = jax.random.key(seed)
        x = -0.0001033 + 0.9999 * jax.random.normal(jax.random.fold_in(_rk, 1), (4, 1024, 256), jnp.float32)
        _lenS = 1024 - jax.random.randint(jax.random.fold_in(_rk, 7), (4,), 0, max(1, 1024 // 4) + 1, jnp.int32)
        _lenS2 = 154 - jax.random.randint(jax.random.fold_in(_rk, 8), (4,), 0, max(1, 154 // 4) + 1, jnp.int32)
        _ctx_1024P = jax.random.normal(jax.random.fold_in(_rk, 11), (4, 16, 256), jnp.float32)
        _ctx_1024c = jax.random.dirichlet(jax.random.fold_in(_rk, 511), 0.3 * jnp.ones((16,), jnp.float32), (4, 154))
        _ctx_1024t = jnp.einsum('bsk,bkd->bsd', _ctx_1024c, _ctx_1024P)
        _ctx_1024t = _ctx_1024t * jax.lax.rsqrt(jnp.mean(jnp.square(_ctx_1024t)) + 1e-12) * 0.953939
        ctx_1024 = -0.000292821 + 1.00034 * (_ctx_1024t + 0.3 * jax.random.normal(jax.random.fold_in(_rk, 611), (4, 154, 256), jnp.float32))
        return (x, ctx_1024)
    x, ctx_1024 = _rec_inputs()

    def _L0_attn_setup():
        import jax, jax.numpy as jnp
        import numpy as np
        HEAD_SIZE = 64
        key = jax.random.key(seed)
        ks = jax.random.split(key, 5)
        B, N, D, H, E, O = (2, 512, 256, 16, HEAD_SIZE, 256)
        return {'query': jax.random.normal(ks[0], (B, N, D), dtype=jnp.float32), 'Wq': jax.random.normal(ks[1], (H, D, E), dtype=jnp.float32) / np.sqrt(D), 'Wk': jax.random.normal(ks[2], (H, D, E), dtype=jnp.float32) / np.sqrt(D), 'Wv': jax.random.normal(ks[3], (H, D, E), dtype=jnp.float32) / np.sqrt(D), 'Wp': jax.random.normal(ks[4], (H * E, O), dtype=jnp.float32) / np.sqrt(H * E), 'bp': jnp.zeros((O,), dtype=jnp.float32)}
    _L0_attn_all = _L0_attn_setup()
    _L0_attn_in = {k: v for k, v in _L0_attn_all.items() if k in ('Wq', 'Wk', 'Wv', 'Wp', 'bp')}
    del _L0_attn_all

    def _L0_xattn_setup():
        import jax, jax.numpy as jnp
        import numpy as np
        from jax import lax
        B, T, F = (32, 128, 256)
        CONV_UNITS = 512
        SHORT_UNITS = 512
        RATE = 4
        key = jax.random.key(seed)
        k1, k2, k3 = jax.random.split(key, 3)
        inputs = jax.random.normal(k1, (B, T, F), dtype=jnp.float32)
        memory = jax.random.normal(k2, (B, CONV_UNITS + SHORT_UNITS, F), dtype=jnp.float32)
        conv_w = jax.random.normal(k3, (RATE, F, F), dtype=jnp.float32) * 0.02
        conv_b = jnp.zeros((F,), dtype=jnp.float32)
        return {'inputs': inputs, 'memory': memory, 'conv_w': conv_w, 'conv_b': conv_b, 'conv_units': CONV_UNITS, 'short_units': SHORT_UNITS, 'rate': RATE}
    _L0_xattn_all = _L0_xattn_setup()
    _L0_xattn_in = {k: v for k, v in _L0_xattn_all.items() if k in ('conv_w', 'conv_b')}
    del _L0_xattn_all

    def _L0_ffn_setup():
        import jax, jax.numpy as jnp
        import numpy as np
        CAPACITY_FACTOR = 1.0

        def _route(token_inputs, Wg, capacity):
            dt = token_inputs.dtype
            logits = jnp.einsum('bnd,de->bne', token_inputs, Wg)
            gates = jax.nn.softmax(logits, axis=-1)
            expert_idx = jnp.argmax(gates, axis=-1)
            mask = jax.nn.one_hot(expert_idx, Wg.shape[1], dtype=dt)
            gate = jnp.sum(gates * mask, axis=-1)
            pos = jnp.cumsum(mask, axis=1) * mask - mask
            keep = mask * (pos < capacity).astype(dt)
            pos_oh = jax.nn.one_hot(pos.astype(jnp.int32), capacity, dtype=dt)
            dispatch = keep[..., None] * pos_oh
            combine = dispatch * gate[:, :, None, None]
            return (dispatch, combine)
        key = jax.random.key(seed)
        k1, k2, k3, k4 = jax.random.split(key, 4)
        B, N, D, E, H = (8, 512, 256, 8, 1024)
        return {'token_inputs': jax.random.normal(k1, (B, N, D), dtype=jnp.float32), 'Wg': jax.random.normal(k2, (D, E), dtype=jnp.float32) * 0.02, 'W1': jax.random.normal(k3, (E, D, H), dtype=jnp.float32) * 0.02, 'W2': jax.random.normal(k4, (E, H, D), dtype=jnp.float32) * 0.02}
    _L0_ffn_all = _L0_ffn_setup()
    _L0_ffn_in = {k: v for k, v in _L0_ffn_all.items() if k in ('Wg', 'W1', 'W2')}
    del _L0_ffn_all
    return {'x': x, 'ctx_1024': ctx_1024, 'L0_attn_Wq': _L0_attn_in['Wq'], 'L0_attn_Wk': _L0_attn_in['Wk'], 'L0_attn_Wv': _L0_attn_in['Wv'], 'L0_attn_Wp': _L0_attn_in['Wp'], 'L0_attn_bp': _L0_attn_in['bp'], 'L0_xattn_conv_w': _L0_xattn_in['conv_w'], 'L0_xattn_conv_b': _L0_xattn_in['conv_b'], 'L0_ffn_Wg': _L0_ffn_in['Wg'], 'L0_ffn_W1': _L0_ffn_in['W1'], 'L0_ffn_W2': _L0_ffn_in['W2']}

def reference(x, ctx_1024, L0_attn_Wq, L0_attn_Wk, L0_attn_Wv, L0_attn_Wp, L0_attn_bp, L0_xattn_conv_w, L0_xattn_conv_b, L0_ffn_Wg, L0_ffn_W1, L0_ffn_W2):
    import jax
    import jax.numpy as jnp

    def _L0_attn_ref(query, Wq, Wk, Wv, Wp, bp):
        import jax, jax.numpy as jnp
        import numpy as np
        HEAD_SIZE = 64
        B, N, D = query.shape
        H, _, E = Wq.shape
        scale = 1.0 / jnp.sqrt(jnp.asarray(E, query.dtype))
        q = jnp.einsum('bnd,hde->bhne', query, Wq) * scale
        k = jnp.einsum('bmd,hde->bhme', query, Wk)
        v = jnp.einsum('bmd,hde->bhme', query, Wv)
        logits = jnp.einsum('bhne,bhme->bhnm', q, k)
        attn = jax.nn.softmax(logits, axis=-1)
        out = jnp.einsum('bhnm,bhme->bnhe', attn, v)
        out = jnp.swapaxes(out, -1, -2).reshape(B, N, E * H)
        return jnp.dot(out, Wp) + bp

    def _L0_xattn_ref(inputs, memory, conv_w, conv_b, conv_units, short_units, rate):
        import jax, jax.numpy as jnp
        import numpy as np
        from jax import lax
        B, T, F = (32, 128, 256)
        CONV_UNITS = 512
        SHORT_UNITS = 512
        RATE = 4
        b, t, f = inputs.shape
        conv_mem = memory[:, :conv_units]
        short_mem = memory[:, -short_units:]
        old_memory = short_mem[:, :t]
        compression = lax.conv_general_dilated(old_memory, conv_w, window_strides=(rate,), padding='VALID', dimension_numbers=('NWC', 'WIO', 'NWC')) + conv_b
        tc = compression.shape[1]
        new_short = jnp.concatenate([short_mem[:, t:], inputs], axis=1)
        new_conv = jnp.concatenate([conv_mem[:, tc:], compression], axis=1)
        return jnp.concatenate([new_conv, new_short], axis=1)

    def _L0_ffn_ref(token_inputs, Wg, W1, W2):
        import jax, jax.numpy as jnp
        import numpy as np
        CAPACITY_FACTOR = 1.0

        def _route(token_inputs, Wg, capacity):
            dt = token_inputs.dtype
            logits = jnp.einsum('bnd,de->bne', token_inputs, Wg)
            gates = jax.nn.softmax(logits, axis=-1)
            expert_idx = jnp.argmax(gates, axis=-1)
            mask = jax.nn.one_hot(expert_idx, Wg.shape[1], dtype=dt)
            gate = jnp.sum(gates * mask, axis=-1)
            pos = jnp.cumsum(mask, axis=1) * mask - mask
            keep = mask * (pos < capacity).astype(dt)
            pos_oh = jax.nn.one_hot(pos.astype(jnp.int32), capacity, dtype=dt)
            dispatch = keep[..., None] * pos_oh
            combine = dispatch * gate[:, :, None, None]
            return (dispatch, combine)
        B, N, D = token_inputs.shape
        E = Wg.shape[1]
        capacity = int(N * CAPACITY_FACTOR // E)
        dispatch, combine = _route(token_inputs, Wg, capacity)
        expert_inputs = jnp.einsum('bnd,bnec->becd', token_inputs, dispatch)
        h = jax.nn.gelu(jnp.einsum('becd,edh->bech', expert_inputs, W1))
        expert_outputs = jnp.einsum('bech,ehd->becd', h, W2)
        output = jnp.einsum('becd,bnec->bnd', expert_outputs, combine)
        return output
    x = _layernorm(x + _L0_attn_ref(x, L0_attn_Wq, L0_attn_Wk, L0_attn_Wv, L0_attn_Wp, L0_attn_bp), axis=-1)
    x = _layernorm(x + _L0_xattn_ref(ctx_1024, x, L0_xattn_conv_w, L0_xattn_conv_b, 512, 512, 4), axis=-1)
    x = _layernorm(x + _L0_ffn_ref(x, L0_ffn_Wg, L0_ffn_W1, L0_ffn_W2), axis=-1)
    return x

_drawn_inputs = setup_inputs


def setup_inputs(seed=0):
    import zlib

    import numpy as np

    out = dict(_drawn_inputs(seed))
    spreads = {'L0_attn_bp': (0.0, 0.1), 'L0_xattn_conv_b': (0.0, 0.464)}
    factors = {'L0_ffn_Wg': 2.925, 'L0_ffn_W1': 2.785, 'L0_ffn_W2': 2.711}
    for name, (base, spread) in spreads.items():
        noise = np.random.default_rng([zlib.crc32(name.encode()), seed]).standard_normal(out[name].shape)
        drawn = base * np.exp(spread * noise) if base else spread * noise
        out[name] = jnp.asarray(drawn.astype(out[name].dtype))
    for name, factor in factors.items():
        out[name] = (out[name] * factor).astype(out[name].dtype)
    return out
```

```python
import concourse.bass as bass
from concourse import mybir
from contextlib import ExitStack

F32 = mybir.dt.float32
F32R = mybir.dt.float32r
ACT = mybir.ActivationFunctionType
ALU = mybir.AluOpType
AX = mybir.AxisListType

P = 128
BANK = 512
HILO = 2

BITES = 6
BITE_SLOTS = (1, 2, 3, 5, 6, 7)
Q0, Q1, K0, K1, V0, V1 = range(BITES)


def wait(eng, sem, value):
    if isinstance(value, int) and value <= 0:
        return
    eng.wait_ge(sem, value)


def wait_then(eng, sem, value, passed):
    wait(eng, sem, value)
    if not isinstance(value, int):
        eng.sem_inc(passed, 1)


def build_constants(nc, ctx):
    ident = ctx.enter_context(nc.sbuf_tensor("ident", [P, P], F32))
    ident_zeroed = ctx.enter_context(nc.semaphore("ident_zeroed"))
    ident_ready = ctx.enter_context(nc.semaphore("ident_ready"))
    passed = ctx.enter_context(nc.semaphore("passed"))
    return ident, ident_zeroed, ident_ready, passed


def build_transpose_x(nc, x, xT_parts, const):
    B, N, D = x.shape
    TILES = N // P
    KC = D // P
    PAIRS = TILES // 2
    GROUPS = B * PAIRS
    ident, ident_zeroed, ident_ready, _ = const
    with ExitStack() as ctx:
        x_tok = ctx.enter_context(nc.sbuf_tensor("x_tok", [P, B, TILES, D], F32))
        xT_sb = ctx.enter_context(nc.sbuf_tensor("xT_sb", [P, B, HILO, KC, N], F32R))
        xT_ps = [ctx.enter_context(nc.psum_tensor(f"xT_ps{i}", [P, KC, 2 * P], F32)) for i in range(2)]
        x_in = [ctx.enter_context(nc.semaphore(f"x_in{b}")) for b in range(B)]
        transposed = ctx.enter_context(nc.semaphore("x_transposed"))
        high_done = ctx.enter_context(nc.semaphore("xT_high_done"))
        low_done = ctx.enter_context(nc.semaphore("xT_low_done"))
        stored = ctx.enter_context(nc.semaphore("xT_stored"))
        block = ctx.enter_context(nc.Block())

        def where(g, part):
            b, i = divmod(g, PAIRS)
            return xT_sb[:, b, part, :, i * 2 * P:(i + 1) * 2 * P]

        @block.gpsimd
        def _(pool):
            pool.memset(ident[:, :], 0.0).then_inc(ident_zeroed, 1)
            pool.wait_ge(ident_zeroed, 1)
            pool.affine_select(out=ident[:, :], in_=ident[:, :], compare_op=ALU.not_equal, fill=1.0,
                               base=0, pattern=[[-1, P]], channel_multiplier=1).then_inc(ident_ready, 1)

        @block.sync
        def _(sp):
            for b in range(B):
                sp.dma_start(x_tok[:, b], x[b].rearrange("(t p) d -> p t d", p=P)).then_inc(x_in[b], 16)
            for b in range(B):
                sp.wait_ge(low_done, PAIRS * (b + 1))
                sp.dma_start(xT_parts[b].rearrange("p a k n -> p (a k n)"),
                             xT_sb[:, b].rearrange("p a k n -> p (a k n)").bitcast(F32)).then_inc(stored, 16)
            sp.wait_ge(stored, 16 * B)

        @block.tensor
        def _(pe):
            pe.wait_ge(ident_ready, 1)
            for g in range(GROUPS):
                b, i = divmod(g, PAIRS)
                if i == 0:
                    pe.wait_ge(x_in[b], 16)
                wait(pe, low_done, g - 1)
                for t in range(2):
                    for k in range(KC):
                        last = pe.transpose(xT_ps[g % 2][:, k, t * P:(t + 1) * P],
                                            x_tok[:, b, 2 * i + t, k * P:(k + 1) * P], ident[:, :])
                last.then_inc(transposed, 1)

        @block.scalar
        def _(act):
            for g in range(GROUPS):
                act.wait_ge(transposed, g + 1)
                act.activation(where(g, 0), xT_ps[g % 2][:, :, :], ACT.Copy).then_inc(high_done, 1)

        @block.vector
        def _(dve):
            for g in range(GROUPS):
                dve.wait_ge(high_done, g + 1)
                dve.tensor_tensor(where(g, 1), xT_ps[g % 2][:, :, :], where(g, 0).bitcast(F32),
                                  ALU.subtract).then_inc(low_done, 1)


def build_attention(nc, xT_parts, Wq, Wk, Wv, o_dram, const):
    B, _, _, KC, N = xT_parts.shape
    H, D, E = Wq.shape
    TILES = N // P
    HP = TILES
    CH = BANK // P
    PAIR_T = 2 * TILES
    IT_T = 2 * PAIR_T
    ITS = B * H // 4
    PER_BATCH = H // 4
    NT = ITS * IT_T
    PAIRS = 2 * ITS
    SCALE = E ** -0.5
    CHUNKS = NT // CH
    ASM = 12
    assert 2 * E == P and HP == 8 and SCALE == 0.125
    ident = const[0]

    with ExitStack() as ctx:
        def sb(name, shape, dt=F32):
            return ctx.enter_context(nc.sbuf_tensor(name, shape, dt))

        def sem(name):
            return ctx.enter_context(nc.semaphore(name))

        xT = sb("xT", [P, HILO, KC, N], F32R)
        w_raw = sb("w_raw", [P, 3, KC, 2 * E])
        w_hi = sb("w_hi", [P, 3, KC, 2 * E], F32R)
        w_lo = sb("w_lo", [P, 3, KC, 2 * E], F32R)
        qk_hi = sb("qk_hi", [P, 2, N], F32R)
        qk_lo = sb("qk_lo", [P, 2, N], F32R)
        q_st = sb("q_st", [P, 2, 2, N], F32R)
        k_hh = sb("k_hh", [P, 2, 2, N], F32R)
        k_ll = sb("k_ll", [P, 2, 2, N], F32R)
        v_st = sb("v_st", [P, 2, HP, 2, HILO, E], F32R)
        probs = sb("probs", [P, 2, N])
        pT_hi = sb("pT_hi", [P, 2, HP, BANK], F32R)
        pT_lo = sb("pT_lo", [P, 2, HP, BANK], F32R)
        oT = sb("oT", [P, 2, BANK])
        o_sum = sb("o_sum", [P, CH, E])
        o_out = sb("o_out", [P, 2, TILES, 2 * E])
        neg_max = sb("neg_max", [P, 4])
        row_sum = sb("row_sum", [P, IT_T])
        inv_sum = sb("inv_sum", [P, CH])

        scores = [ctx.enter_context(nc.psum_tensor(f"scores{i}", [P, N], F32)) for i in range(2)]
        pT_ps = [ctx.enter_context(nc.psum_tensor(f"pT_ps{i}", [P, CH, P], F32)) for i in range(2)]
        av_ps = ctx.enter_context(nc.psum_tensor("av_ps", [P, BANK], F32))
        misc_ps = ctx.enter_context(nc.psum_tensor("misc_ps", [P, BANK], F32))

        w_loaded = sem("w_loaded")
        w_split_hi = sem("w_split_hi")
        w_split = sem("w_split")
        xT_loaded = sem("xT_loaded")
        qk_laid = sem("qk_laid")
        scores_ready = sem("scores_ready")
        max_ready = sem("max_ready")
        probs_ready = sem("probs_ready")
        pT_ready = sem("pT_ready")
        pT_hi_done = sem("pT_hi_done")
        pT_lo_done = sem("pT_lo_done")
        av_ready = sem("av_ready")
        oT_done = sem("oT_done")
        fold_ready = sem("fold_ready")
        fold_read = sem("fold_read")
        inv_done = sem("inv_done")
        o_done = sem("o_done")
        o_stored = sem("o_stored")
        bite_ready = sem("bite_ready")
        bite_hi_done = sem("bite_hi_done")
        bite_lo_done = sem("bite_lo_done")

        block = ctx.enter_context(nc.Block())

        def run(eng, slot):
            for tt in range(IT_T):
                slot(0, tt)
            with eng.Fori(1, ITS - 1) as it:
                for tt in range(IT_T):
                    slot(it, tt)
            for tt in range(IT_T):
                slot(ITS - 1, tt)
            for tt in range(IT_T, IT_T + CH + 2):
                slot(ITS - 1, tt)

        def exists(it, tt, ahead=0):
            return not (isinstance(it, int) and it == ITS - 1 and tt + ahead >= IT_T)

        def bite_of(u):
            return BITE_SLOTS.index(u) if u in BITE_SLOTS else None

        @block.sync
        def _(sp):
            def load_w(g, head):
                wait_then(sp, w_split, g, const[3])
                for i, w in enumerate((Wq, Wk, Wv)):
                    for k in range(KC):
                        sp.dma_start(w_raw[:, i, k, :].rearrange("p (h e) -> p h e", h=2),
                                     w[bass.ds(head, 2), k * P:(k + 1) * P, :].rearrange("h d e -> d h e")
                                     ).then_inc(w_loaded, 16)

            def load_xT(batch):
                sp.dma_start(xT[:, :, :, :].rearrange("p a k n -> p (a k n)").bitcast(F32),
                             xT_parts[bass.ds(batch, 1)].rearrange("b p a k n -> p (b a k n)")
                             ).then_inc(xT_loaded, 16)

            def lay_out(g, par):
                wait_then(sp, bite_lo_done, BITES * g + K1 + 1, const[3])
                wait(sp, scores_ready, PAIR_T * (g - 1))
                for h in range(2):
                    rows = slice(h * E, (h + 1) * E)
                    lo, hi = slice(0, E), slice(E, P)
                    for dst, src in ((q_st[lo, par, h], qk_hi[rows, 0]), (q_st[hi, par, h], qk_lo[rows, 0])):
                        sp.dma_start(dst.bitcast(F32), src.bitcast(F32)).then_inc(qk_laid, 16)
                    for buf, src in ((k_hh, qk_hi[rows, 1]), (k_ll, qk_lo[rows, 1])):
                        for half in (lo, hi):
                            sp.dma_start(buf[half, par, h].bitcast(F32), src.bitcast(F32)).then_inc(qk_laid, 16)

            def store_o(g, par, batch, head):
                wait_then(sp, o_done, 4 * (g + 1), const[3])
                sp.dma_start(o_dram[bass.ds(batch, 1), :, bass.ds(head * E, 2 * E)]
                             .rearrange("b (t p) n -> p (b t) n", p=P), o_out[:, par]).then_inc(o_stored, 16)

            def step(it, s):
                g = 2 * it + s
                final = isinstance(it, int) and it == ITS - 1
                if not final:
                    nxt = it + 1
                    load_w(g + 2, 4 * (nxt % PER_BATCH) + 2 * s)
                if not (isinstance(it, int) and g == 0):
                    if s == 0:
                        prev = it - 1
                        store_o(g - 1, 1, prev // PER_BATCH, 4 * (prev % PER_BATCH) + 2)
                    else:
                        store_o(g - 1, 0, it // PER_BATCH, 4 * (it % PER_BATCH))
                if not (final and s == 1):
                    lay_out(g + 1, (s + 1) % 2)
                if s == 0 and not final:
                    wait_then(sp, bite_ready, BITES * (g + 2), const[3])
                    load_xT(nxt // PER_BATCH)

            load_w(0, 0)
            load_xT(0)
            load_w(1, 2)
            lay_out(0, 0)
            for s in range(2):
                step(0, s)
            with sp.Fori(1, ITS - 1) as it:
                for s in range(2):
                    step(it, s)
            for s in range(2):
                step(ITS - 1, s)
            store_o(PAIRS - 1, 1, B - 1, H - 2)
            sp.wait_ge(o_stored, 16 * PAIRS)

        @block.gpsimd
        def _(pool):
            def split_w(g):
                wait(pool, w_loaded, 6 * 16 * (g + 1))
                wait_then(pool, bite_ready, BITES * g, const[3])
                pool.tensor_copy(w_hi[:, :, :, :], w_raw[:, :, :, :]).then_inc(w_split_hi, 1)
                wait(pool, w_split_hi, g + 1)
                pool.tensor_tensor(w_lo[:, :, :, :], w_raw[:, :, :, :], w_hi[:, :, :, :].bitcast(F32),
                                   ALU.subtract).then_inc(w_split, 1)

            for g in range(4):
                split_w(g)
            with pool.Fori(1, ITS - 1) as it:
                for s in range(2):
                    split_w(2 * it + 2 + s)

        @block.tensor
        def _(pe):
            def misc_free(folds, bites):
                wait(pe, fold_read, folds)
                wait(pe, bite_lo_done, bites)

            def bite(g, k, it_of_xT, folds):
                wait(pe, w_split, g + 1)
                wait(pe, xT_loaded, 16 * (it_of_xT + 1))
                misc_free(folds, BITES * g + k)
                parts = ((w_hi, 0), (w_lo, 0), (w_hi, 1))
                if k in (Q0, Q1, K0, K1):
                    i, c = divmod(k, 2)
                    cols = slice(c * BANK, (c + 1) * BANK)
                    for n, (w, part) in enumerate(parts):
                        for kc in range(KC):
                            last = pe.matmul(misc_ps[:, :], w[:, i, kc, :], xT[:, part, kc, cols],
                                             start=(n == 0 and kc == 0), stop=(n == 2 and kc == KC - 1))
                else:
                    for m in range(CH):
                        rows = slice(((k - V0) * CH + m) * P, ((k - V0) * CH + m + 1) * P)
                        for n, (w, part) in enumerate(parts):
                            for kc in range(KC):
                                last = pe.matmul(misc_ps[:, m * P:(m + 1) * P], xT[:, part, kc, rows],
                                                 w[:, 2, kc, :], start=(n == 0 and kc == 0),
                                                 stop=(n == 2 and kc == KC - 1))
                last.then_inc(bite_ready, 1)

            def score(it, tt):
                T = it * IT_T + tt
                pair, u = divmod(tt, PAIR_T)
                h, j = divmod(u, TILES)
                par = pair % 2
                if u == 0:
                    wait(pe, qk_laid, 16 * ASM * ((T // PAIR_T if isinstance(T, int) else 2 * it + pair) + 1))
                wait(pe, probs_ready, T - 1)
                q = q_st[:, par, h, j * P:(j + 1) * P]
                for c in range(N // BANK):
                    cols = slice(c * BANK, (c + 1) * BANK)
                    pe.matmul(scores[tt % 2][:, cols], q, k_hh[:, par, h, cols], start=True, stop=False)
                    last = pe.matmul(scores[tt % 2][:, cols], q, k_ll[:, par, h, cols], start=False, stop=True)
                last.then_inc(scores_ready, 1)

            def slot(it, tt):
                T = it * IT_T + tt
                pair, u = divmod(tt, PAIR_T)
                first = isinstance(it, int) and it == 0
                if exists(it, tt, 2):
                    score(it, tt + 2)
                if exists(it, tt):
                    wait(pe, probs_ready, T + 1)
                    for half in range(2):
                        wait(pe, pT_lo_done, 2 * T + half - 1)
                        for m in range(CH):
                            mt = half * CH + m
                            last = pe.transpose(pT_ps[half][:, m, :], probs[:, tt % 2, mt * P:(mt + 1) * P],
                                                ident[:, :])
                        last.then_inc(pT_ready, 1)
                if (not first or tt >= CH) and exists(it, tt, -CH):
                    c, part = it * (IT_T // CH) + tt // CH - 1, tt % CH
                    cpar, ch = (tt // CH - 1) % 2, (tt // CH - 1) % 8
                    vpar, h = divmod(ch // 2, 2)
                    if part == 0:
                        wait(pe, pT_lo_done, 2 * CH * (c + 1))
                        wait(pe, oT_done, c)
                        wait(pe, bite_lo_done, BITES * (it * 2 + (tt // CH - 1) // 4 + 1))
                    for mt in (2 * part, 2 * part + 1):
                        v = v_st[:, vpar, mt, h].rearrange("p a e -> p (a e)")
                        pe.matmul(av_ps[:, :], v, pT_hi[:, cpar, mt, :], start=(mt == 0), stop=False)
                        last = pe.matmul(av_ps[:, :], v, pT_lo[:, cpar, mt, :], start=False, stop=(mt == HP - 1))
                    if part == CH - 1:
                        last.then_inc(av_ready, 1)
                folds = it * (IT_T // CH) + tt // CH - 1
                g = 2 * it + pair
                k = bite_of(u)
                if k is not None and exists(it, tt, PAIR_T):
                    bite(g + 1, k, it + pair, folds)
                if tt % CH == 0 and (not first or tt >= 2 * CH) and exists(it, tt, -2 * CH):
                    f = folds - 1
                    wait(pe, oT_done, f + 1)
                    done = 0 if u == 0 else (3 if u == CH else BITES)
                    if not exists(it, tt, PAIR_T):
                        done = 0
                    misc_free(f, BITES * (g + 1) + done if exists(it, tt) else BITES * PAIRS)
                    for m in range(CH):
                        last = pe.transpose(misc_ps[:, m * P:(m + 1) * P],
                                            oT[:, (tt // CH) % 2, m * P:(m + 1) * P], ident[:, :])
                    last.then_inc(fold_ready, 1)

            for k in range(BITES):
                bite(0, k, 0, 0)
            score(0, 0)
            score(0, 1)
            run(pe, slot)

        @block.scalar
        def _(act):
            def bite_hi(g, k, par):
                wait(act, bite_ready, BITES * g + k + 1)
                if k in (Q0, Q1, K0, K1):
                    i, c = divmod(k, 2)
                    wait(act, qk_laid, 16 * ASM * g)
                    act.activation(qk_hi[:, i, c * BANK:(c + 1) * BANK], misc_ps[:, :], ACT.Copy,
                                   scale=SCALE if i == 0 else 1.0).then_inc(bite_hi_done, 1)
                else:
                    wait(act, av_ready, 4 * (g - 1))
                    act.activation(v_st[:, par, (k - V0) * CH:(k - V0 + 1) * CH, :, 0, :],
                                   misc_ps[:, :].rearrange("p (m h e) -> p m h e", m=CH, h=2),
                                   ACT.Copy).then_inc(bite_hi_done, 1)

            def exp(it, tt):
                T = it * IT_T + tt
                wait(act, max_ready, T + 1)
                wait(act, pT_ready, 2 * (T - 1))
                act.activation(probs[:, tt % 2, :], scores[tt % 2][:, :], ACT.Exp,
                               bias=neg_max[:, tt % 4:tt % 4 + 1],
                               accum_out=row_sum[:, tt % IT_T:tt % IT_T + 1]).then_inc(probs_ready, 1)

            def slot(it, tt):
                T = it * IT_T + tt
                pair, u = divmod(tt, PAIR_T)
                first = isinstance(it, int) and it == 0
                if tt % CH == 0 and (not first or tt >= 2 * CH) and exists(it, tt, -2 * CH):
                    c = it * (IT_T // CH) + tt // CH - 2
                    wait(act, av_ready, c + 1)
                    wait(act, fold_ready, c - 1)
                    act.activation(oT[:, (tt // CH) % 2, :], av_ps[:, :], ACT.Copy).then_inc(oT_done, 1)
                if exists(it, tt, 1):
                    exp(it, tt + 1)
                k = bite_of(u - 1)
                if k is not None and exists(it, tt, PAIR_T):
                    bite_hi(2 * it + pair + 1, k, (pair + 1) % 2)
                if exists(it, tt):
                    c = it * (IT_T // CH) + tt // CH
                    if tt % CH == 0:
                        wait(act, av_ready, c - 1)
                    for half in range(2):
                        wait(act, pT_ready, 2 * T + half + 1)
                        act.activation(pT_hi[:, (tt // CH) % 2, half * CH:(half + 1) * CH,
                                             (tt % CH) * P:(tt % CH + 1) * P],
                                       pT_ps[half][:, :, :], ACT.Copy).then_inc(pT_hi_done, 1)

            for k in range(BITES):
                bite_hi(0, k, 0)
            exp(0, 0)
            run(act, slot)

        @block.vector
        def _(dve):
            def bite_lo(g, k, par):
                wait(dve, bite_hi_done, BITES * g + k + 1)
                if k in (Q0, Q1, K0, K1):
                    i, c = divmod(k, 2)
                    cols = slice(c * BANK, (c + 1) * BANK)
                    dve.scalar_tensor_tensor(out=qk_lo[:, i, cols], in0=misc_ps[:, :],
                                             scalar=SCALE if i == 0 else 1.0, in1=qk_hi[:, i, cols].bitcast(F32),
                                             op0=ALU.mult, op1=ALU.subtract).then_inc(bite_lo_done, 1)
                else:
                    mts = slice((k - V0) * CH, (k - V0 + 1) * CH)
                    dve.tensor_tensor(v_st[:, par, mts, :, 1, :],
                                      misc_ps[:, :].rearrange("p (m h e) -> p m h e", m=CH, h=2),
                                      v_st[:, par, mts, :, 0, :].bitcast(F32), ALU.subtract
                                      ).then_inc(bite_lo_done, 1)

            def maximum(it, tt):
                T = it * IT_T + tt
                wait(dve, scores_ready, T + 1)
                dve.tensor_reduce(neg_max[:, tt % 4:tt % 4 + 1], scores[tt % 2][:, :], AX.X, ALU.max,
                                  negate=True).then_inc(max_ready, 1)

            def slot(it, tt):
                T = it * IT_T + tt
                pair, u = divmod(tt, PAIR_T)
                first = isinstance(it, int) and it == 0
                if exists(it, tt, 2):
                    maximum(it, tt + 2)
                if exists(it, tt):
                    for half in range(2):
                        wait(dve, pT_hi_done, 2 * T + half + 1)
                        where = (slice(None), (tt // CH) % 2, slice(half * CH, (half + 1) * CH),
                                 slice((tt % CH) * P, (tt % CH + 1) * P))
                        dve.tensor_tensor(pT_lo[where], pT_ps[half][:, :, :], pT_hi[where].bitcast(F32),
                                          ALU.subtract).then_inc(pT_lo_done, 1)
                k = bite_of(u - 1)
                if k is not None and exists(it, tt, PAIR_T):
                    bite_lo(2 * it + pair + 1, k, (pair + 1) % 2)
                if tt % CH == 1 and (not first or tt >= 2 * CH) and exists(it, tt, -2 * CH - 1):
                    ft = tt // CH - 2
                    f = it * (IT_T // CH) + ft
                    fpair, ch = divmod(ft % (IT_T // CH), 4)
                    h, half = divmod(ch, 2)
                    sums = (ft * CH) % IT_T
                    wait(dve, o_done, f)
                    dve.reciprocal(inv_sum[:, :], row_sum[:, sums:sums + CH]).then_inc(inv_done, 1)
                    wait(dve, fold_ready, f + 1)
                    dve.tensor_reduce(o_sum[:, :, :], misc_ps[:, :].rearrange("p (m a e) -> p m e a", m=CH, a=2),
                                      AX.X, ALU.add).then_inc(fold_read, 1)
                    wait(dve, inv_done, f + 1)
                    wait(dve, fold_read, f + 1)
                    if ch == 0:
                        wait(dve, o_stored, 16 * (2 * it + (ft // 4) - 1))
                    dve.tensor_tensor(o_out[:, fpair, half * CH:(half + 1) * CH, h * E:(h + 1) * E],
                                      o_sum[:, :, :], inv_sum[:, :].rearrange("p (m a) -> p m a", a=1)
                                      .broadcast_to([P, CH, E]), ALU.mult).then_inc(o_done, 1)

            for k in range(BITES):
                bite_lo(0, k, 0)
            maximum(0, 0)
            maximum(0, 1)
            run(dve, slot)


def build_project_norm(nc, o_dram, x, Wp, bp, x1, const):
    B, N, D = x.shape
    HE = o_dram.shape[2]
    H = HE // 64
    CC = HE // P
    TILES = B * N // P
    ident = const[0]
    with ExitStack() as ctx:
        def sb(name, shape, dt=F32):
            return ctx.enter_context(nc.sbuf_tensor(name, shape, dt))

        def sem(name):
            return ctx.enter_context(nc.semaphore(name))

        wp_raw = sb("wp_raw", [P, CC, D])
        wp_hi = sb("wp_hi", [P, CC, D], F32R)
        wp_lo = sb("wp_lo", [P, CC, D], F32R)
        bp_all = sb("bp_all", [P, D])
        eps = sb("eps", [P, 1])
        o_tok = sb("o_tok", [P, 2, HE])
        x_tok = sb("x1_x_tok", [P, 2, D])
        xb = sb("xb", [P, 2, D])
        oT_hi = sb("oT_hi", [P, 2, CC, P], F32R)
        oT_lo = sb("oT_lo", [P, 2, CC, P], F32R)
        z = sb("z1", [P, 2, D])
        stats = sb("stats1", [P, 2, 6])
        moments = sb("moments1", [P, 2, 2])
        root = sb("root1", [P, 2])
        scale = sb("scale1", [P, 2])
        oT_ps = [ctx.enter_context(nc.psum_tensor(f"oT_ps{i}", [P, CC, P], F32)) for i in range(2)]
        y_ps = [ctx.enter_context(nc.psum_tensor(f"y1_ps{i}", [P, D], F32)) for i in range(2)]

        wp_in = sem("wp_in")
        bp_in = sem("bp_in")
        eps_set = sem("eps_set")
        wp_hi_done = sem("wp_hi_done")
        wp_split = sem("wp_split")
        o_in = [sem(f"o_in{i}") for i in range(2)]
        x_in = [sem(f"x1_x_in{i}") for i in range(2)]
        xb_done = sem("xb_done")
        oT_ready = sem("oT_ready")
        oT_hi_done = sem("oT_hi_done")
        oT_lo_done = sem("oT_lo_done")
        y_ready = sem("y1_ready")
        z_done = sem("z1_done")
        stats_done = sem("stats1_done")
        moments_done = sem("moments1_done")
        root_done = sem("root1_done")
        scale_done = sem("scale1_done")
        x1_done = sem("x1_done")
        block = ctx.enter_context(nc.Block())

        o_rows = o_dram.rearrange("b n c -> (b n) c")
        x_rows = x.rearrange("b n c -> (b n) c")

        def run(eng, slot):
            for T in range(4):
                slot(T, T % 2, T // 2)
            with eng.Fori(2, TILES // 2) as it:
                for par in range(2):
                    slot(it * 2 + par, par, it)
            for T in range(TILES, TILES + 2):
                slot(T, T % 2, T // 2)

        def beyond(T, n=0):
            return isinstance(T, int) and T - n >= TILES

        @block.sync
        def _(sp):
            wp_rows = Wp.rearrange("(e c h) n -> c h e n", h=2, c=CC)
            for c in range(CC):
                for h in range(2):
                    sp.dma_start(wp_raw[h * 64:(h + 1) * 64, c, :], wp_rows[c, h]).then_inc(wp_in, 16)
            sp.dma_start(bp_all[:, :], bp.rearrange("(a n) -> a n", a=1).broadcast_to([P, D])).then_inc(bp_in, 16)

            def slot(T, par, it):
                if beyond(T):
                    return
                wait_then(sp, oT_ready, T - 1, const[3])
                sp.dma_start(o_tok[:, par, :], o_rows[bass.ds(T * P, P), :]).then_inc(o_in[par], 16)
                wait_then(sp, xb_done, T - 1, const[3])
                sp.dma_start(x_tok[:, par, :], x_rows[bass.ds(T * P, P), :]).then_inc(x_in[par], 16)

            run(sp, slot)

        @block.gpsimd
        def _(pool):
            pool.memset(eps[:, :], 1e-5).then_inc(eps_set, 1)
            pool.wait_ge(bp_in, 16)

            def slot(T, par, it):
                if beyond(T):
                    return
                wait(pool, x_in[par], 16 * (it + 1))
                wait(pool, z_done, T - 1)
                pool.tensor_tensor(xb[:, par, :], x_tok[:, par, :], bp_all[:, :], ALU.add).then_inc(xb_done, 1)

            run(pool, slot)

        @block.tensor
        def _(pe):
            def slot(T, par, it):
                if not beyond(T):
                    wait(pe, o_in[par], 16 * (it + 1))
                    wait(pe, oT_lo_done, T - 1)
                    for c in range(CC):
                        last = pe.transpose(oT_ps[par][:, c, :], o_tok[:, par, c * P:(c + 1) * P], ident[:, :])
                    last.then_inc(oT_ready, 1)
                if isinstance(T, int) and T == 0 or beyond(T, 1):
                    return
                prev = 1 - par
                if isinstance(T, int) and T == 1:
                    pe.wait_ge(wp_split, 1)
                wait(pe, oT_lo_done, T)
                wait(pe, z_done, T - 2)
                products = ((oT_hi, wp_hi), (oT_hi, wp_lo), (oT_lo, wp_hi))
                for n, (a, w) in enumerate(products):
                    for c in range(CC):
                        last = pe.matmul(y_ps[prev][:, :], a[:, prev, c, :], w[:, c, :],
                                         start=(n == 0 and c == 0), stop=(n == 2 and c == CC - 1))
                last.then_inc(y_ready, 1)

            run(pe, slot)

        @block.scalar
        def _(act):
            act.wait_ge(eps_set, 1)

            def slot(T, par, it):
                if not beyond(T):
                    wait(act, oT_ready, T + 1)
                    wait(act, y_ready, T - 1)
                    act.activation(oT_hi[:, par], oT_ps[par][:, :, :], ACT.Copy).then_inc(oT_hi_done, 1)
                if isinstance(T, int) and T == 0 or beyond(T, 1):
                    return
                prev = 1 - par
                wait(act, moments_done, T)
                act.activation(root[:, prev:prev + 1], moments[:, prev, 1:2], ACT.Sqrt,
                               bias=eps[:, :]).then_inc(root_done, 1)

            run(act, slot)

        @block.vector
        def _(dve):
            dve.wait_ge(wp_in, 16 * 2 * CC)
            dve.tensor_copy(wp_hi[:, :, :], wp_raw[:, :, :]).then_inc(wp_hi_done, 1)
            dve.wait_ge(wp_hi_done, 1)
            dve.tensor_tensor(wp_lo[:, :, :], wp_raw[:, :, :], wp_hi[:, :, :].bitcast(F32),
                              ALU.subtract).then_inc(wp_split, 1)

            def slot(T, par, it):
                prev = 1 - par
                if not beyond(T):
                    wait(dve, oT_hi_done, T + 1)
                    dve.tensor_tensor(oT_lo[:, par], oT_ps[par][:, :, :], oT_hi[:, par].bitcast(F32),
                                      ALU.subtract).then_inc(oT_lo_done, 1)
                if not (isinstance(T, int) and T < 2):
                    wait(dve, root_done, T - 1)
                    dve.reciprocal(scale[:, par:par + 1], root[:, par:par + 1]).then_inc(scale_done, 1)
                    wait(dve, scale_done, T - 1)
                    dve.tensor_scalar(x1[:, bass.ds(T - 2, 1), :], z[:, par:par + 1, :], moments[:, par, 0:1],
                                      scale[:, par:par + 1], ALU.subtract, ALU.mult).then_inc(x1_done, 1)
                if not (isinstance(T, int) and T == 0) and not beyond(T, 1):
                    wait(dve, y_ready, T)
                    wait(dve, xb_done, T)
                    wait(dve, x1_done, T - 2)
                    dve.tensor_tensor(z[:, prev, :], y_ps[prev][:, :], xb[:, prev, :], ALU.add).then_inc(z_done, 1)
                    wait(dve, z_done, T)
                    dve.bn_stats(stats[:, prev, :], z[:, prev, :]).then_inc(stats_done, 1)
                    wait_then(dve, stats_done, T, const[3])
                    dve.bn_aggr(moments[:, prev, :], stats[:, prev, :]).then_inc(moments_done, 1)

            run(dve, slot)


def build_memory_route(nc, ctx_in, conv_w, conv_b, Wg, x1, x2, xe_dram, slot_of, gate_of, const):
    B, S, D = ctx_in.shape
    RATE = conv_w.shape[0]
    TILES = x1.shape[1]
    N = TILES * P // B
    TB = N // P
    HALF = N // 2
    TC = (S - RATE) // RATE + 1
    KC = D // P
    EX = Wg.shape[1]
    CAP = N // EX
    ROWS = EX * B * CAP
    HT = HALF // P
    CT, CP = divmod(HALF - TC, P)
    MT, MP = divmod(N - S, P)
    SC = S - P * (TB - 1 - MT)
    SM = S % P
    assert CT == HT - 1 and MT == TB - 2 and CP + TC == P and SC + MP == P and S == P + SM and MP + SM == P
    ident = const[0]
    with ExitStack() as ctx:
        def sb(name, shape, dt=F32):
            return ctx.enter_context(nc.sbuf_tensor(name, shape, dt))

        def sem(name):
            return ctx.enter_context(nc.semaphore(name))

        zeros = sb("zeros", [P, 2048])
        cw = sb("cw", [P, RATE, KC, D])
        wg = sb("wg", [P, KC, EX])
        old_T = sb("old_T", [P, B, RATE, KC, P])
        x2T = sb("x2T", [P, 2, 2, KC, P])
        eps = sb("eps2", [P, 1])
        stats = sb("stats2", [P, TILES, 6])
        moments = sb("moments2", [P, TILES, 2])
        root = sb("root2", [P, TILES])
        scale = sb("scale2", [P, TILES])
        before = sb("before", [P, P])
        ones = sb("ones", [P, P])
        expert = sb("expert", [P, EX])
        rank = sb("rank", [P, EX])
        base = sb("base", [P, B, TB])
        trash = sb("trash", [P, TILES])
        logits = sb("logits", [P, TILES, EX])
        top = sb("top", [P, TILES])
        probs = sb("gprobs", [P, TILES, EX])
        inv = sb("ginv", [P, TILES])
        first = sb("first", [P, TILES])
        mask = sb("mask", [P, B, TB, EX])
        tiles_before = sb("tiles_before", [P, B, TB, EX])
        work = sb("work", [P, TILES, EX])
        slot = sb("slot", [P, TILES])
        keep = sb("keep", [P, TILES])
        row = sb("row", [P, TILES])
        row_in = sb("row_in", [P, TILES])
        row_out = sb("row_out", [P, TILES])
        send_to = sb("send_to", [P, TILES], mybir.dt.uint32)

        old_ps = [ctx.enter_context(nc.psum_tensor(f"old_ps{i}", [P, KC, 2 * P], F32)) for i in range(2)]
        comp_ps = ctx.enter_context(nc.psum_tensor("comp_ps", [P, B, D], F32))
        x2T_ps = [ctx.enter_context(nc.psum_tensor(f"x2T_ps{i}", [P, 2, KC, P], F32)) for i in range(2)]
        logits_ps = ctx.enter_context(nc.psum_tensor("logits_ps", [P, TILES, EX], F32))
        count_ps = ctx.enter_context(nc.psum_tensor("count_ps", [P, B, TB, EX], F32))

        zeroed = sem("zeroed")
        filled = sem("filled")
        weights_in = sem("weights_in")
        moved = sem("moved")
        patterns = sem("patterns")
        base_seeded = sem("base_seeded")
        old_cleared = sem("old_cleared")
        old_ready = sem("old_ready")
        old_placed = sem("old_placed")
        comp_ready = sem("comp_ready")
        sum_done = sem("sum_done")
        comp_added = sem("comp_added")
        stats_done = sem("stats2_done")
        moments_done = sem("moments2_done")
        root_done = sem("root2_done")
        scale_done = sem("scale2_done")
        x2_done = sem("x2_done")
        x2T_ready = sem("x2T_ready")
        x2T_done = sem("x2T_done")
        logits_ready = sem("logits_ready")
        shifted = sem("shifted")
        exp_done = sem("exp_done")
        mask_done = sem("mask_done")
        count_ready = sem("count_ready")
        dve_step = sem("dve_step")
        rows_ready = sem("rows_ready")
        sent = sem("sent")
        block = ctx.enter_context(nc.Block())

        x1_b = x1[:, :, :].rearrange("p (b t) d -> p b t d", b=B)
        x2_b = x2[:, :, :].rearrange("p (b t) d -> p b t d", b=B)
        MOVES = 7

        @block.sync
        def _(sp):
            sp.dma_start(cw[:, :, :, :], conv_w.rearrange("r (k p) d -> p r k d", p=P)).then_inc(weights_in, 16)
            sp.dma_start(wg[:, :, :], Wg.rearrange("(k p) e -> p k e", p=P)).then_inc(weights_in, 16)
            sp.dma_start(x2_b[0:P - TC, :, 0:HT, :], x1_b[TC:P, :, 0:HT, :]).then_inc(moved, 16)
            sp.dma_start(x2_b[P - TC:P, :, 0:HT - 1, :], x1_b[0:TC, :, 1:HT, :]).then_inc(moved, 16)
            sp.dma_start(x2_b[0:P - SM, :, HT:TB - 1, :], x1_b[SM:P, :, HT + 1:TB, :]).then_inc(moved, 16)
            sp.dma_start(x2_b[P - SM:P, :, HT:TB - 2, :], x1_b[0:SM, :, HT + 2:TB, :]).then_inc(moved, 16)
            sp.dma_start(x2_b[CP:P, :, CT, :], conv_b.rearrange("(a b n) -> a b n", a=1, b=1)
                         .broadcast_to([TC, B, D])).then_inc(moved, 16)
            sp.dma_start(x2_b[MP:P, :, MT, :], ctx_in[:, 0:SC, :].rearrange("b s d -> s b d")).then_inc(moved, 16)
            sp.dma_start(x2_b[:, :, TB - 1, :], ctx_in[:, SC:S, :].rearrange("b s d -> s b d")).then_inc(moved, 16)
            sp.wait_ge(zeroed, 1)
            for i in range(ROWS * D // (P * 2048)):
                sp.dma_start(xe_dram[i * 1024:(i + 1) * 1024, :].rearrange("(p r) d -> p (r d)", p=P),
                             zeros[:, :]).then_inc(filled, 16)

        @block.gpsimd
        def _(pool):
            pool.memset(zeros[:, :], 0.0).then_inc(zeroed, 1)
            pool.memset(eps[:, :], 1e-5).then_inc(patterns, 1)
            pool.memset(ones[:, :], 1.0).then_inc(patterns, 1)
            pool.iota(expert[:, :], pattern=[[1, EX]], base=0, channel_multiplier=0,
                      allow_small_or_imprecise_dtypes=True).then_inc(patterns, 1)
            pool.iota(rank[:, :], pattern=[[-1, EX]], base=EX, channel_multiplier=0,
                      allow_small_or_imprecise_dtypes=True).then_inc(patterns, 1)
            pool.iota(base[:, :, :], pattern=[[CAP, B], [0, TB]], base=0, channel_multiplier=0,
                      allow_small_or_imprecise_dtypes=True).then_inc(patterns, 1)
            pool.iota(trash[:, :], pattern=[[P, TILES]], base=ROWS, channel_multiplier=1,
                      allow_small_or_imprecise_dtypes=True).then_inc(patterns, 1)
            pool.wait_ge(patterns, 2)
            pool.affine_select(out=before[:, :], in_=ones[:, :], compare_op=ALU.is_gt, fill=0.0,
                               base=0, pattern=[[1, P]], channel_multiplier=-1).then_inc(patterns, 1)
            pool.wait_ge(filled, 16 * (ROWS * D // (P * 2048)))
            pool.wait_ge(rows_ready, 1)
            for t in range(TILES):
                pool.indirect_dma_start(out=xe_dram[:, :],
                                        out_offset=bass.IndirectOffsetOnAxis(ap=send_to[:, t:t + 1], axis=0),
                                        in_=x2[:, t, :], in_offset=None).then_inc(sent, 16)
            pool.wait_ge(sent, 16 * TILES)

        @block.tensor
        def _(pe):
            for b in range(B):
                wait(pe, old_placed, b - 1)
                for k in range(KC):
                    for t in range(2):
                        last = pe.transpose(old_ps[b % 2][:, k, t * P:(t + 1) * P],
                                            x1_b[:, b, HT + t, k * P:(k + 1) * P], ident[:, :])
                last.then_inc(old_ready, 1)
            pe.wait_ge(weights_in, 32)
            for b in range(B):
                pe.wait_ge(old_placed, b + 1)
                for r in range(RATE):
                    for k in range(KC):
                        last = pe.matmul(comp_ps[:, b, :], old_T[:, b, r, k, :], cw[:, r, k, :],
                                         start=(r == 0 and k == 0), stop=(r == RATE - 1 and k == KC - 1))
                last.then_inc(comp_ready, 1)
            for i in range(TILES // 2 + 1):
                if i < TILES // 2:
                    pe.wait_ge(x2_done, 2 * i + 2)
                    wait(pe, x2T_done, i - 1)
                    for t in range(2):
                        for k in range(KC):
                            last = pe.transpose(x2T_ps[i % 2][:, t, k, :], x2[:, 2 * i + t, k * P:(k + 1) * P],
                                                ident[:, :])
                    last.then_inc(x2T_ready, 1)
                if i > 0:
                    pe.wait_ge(x2T_done, i)
                    for t in range(2):
                        for k in range(KC):
                            last = pe.matmul(logits_ps[:, 2 * i - 2 + t, :], x2T[:, (i - 1) % 2, t, k, :],
                                             wg[:, k, :], start=(k == 0), stop=(k == KC - 1))
                    last.then_inc(logits_ready, 1)
            pe.wait_ge(patterns, 7)
            pe.wait_ge(mask_done, 1)
            pe.matmul(count_ps[:, :, :, :], before[:, :], mask[:, :, :, :], start=True, stop=False)
            pe.matmul(count_ps[:, :, :, :], ones[:, :], tiles_before[:, :, :, :], start=False,
                      stop=True).then_inc(count_ready, 1)

        @block.scalar
        def _(act):
            act.wait_ge(patterns, 1)
            for b in range(B):
                act.wait_ge(moments_done, TB * (b + 1))
                tiles = slice(b * TB, (b + 1) * TB)
                act.activation(root[:, tiles], moments[:, tiles, 1], ACT.Sqrt, bias=eps[:, :]).then_inc(root_done, 1)
                for i in range(b * TB // 2, (b + 1) * TB // 2):
                    act.wait_ge(x2T_ready, i + 1)
                    wait(act, logits_ready, i - 1)
                    act.activation(x2T[:, i % 2], x2T_ps[i % 2][:, :, :, :], ACT.Copy).then_inc(x2T_done, 1)
            act.wait_ge(shifted, 1)
            act.activation(probs[:, :, :], logits[:, :, :], ACT.Exp).then_inc(exp_done, 1)

        @block.vector
        def _(dve):
            steps = [0]

            def step(ins):
                steps[0] += 1
                ins.then_inc(dve_step, 1)
                dve.wait_ge(dve_step, steps[0])

            step(dve.memset(old_T[:, :, :, :, :], 0.0))
            for b in range(B):
                dve.wait_ge(old_ready, b + 1)
                for k in range(KC):
                    last = dve.tensor_copy(old_T[:, b, :, k, CP:P],
                                           old_ps[b % 2][:, k, 0:TC * RATE].rearrange("p (t r) -> p r t", r=RATE))
                last.then_inc(old_placed, 1)
            dve.wait_ge(moved, 16 * MOVES)
            for b in range(B):
                step(dve.tensor_tensor(x2_b[:, b], x2_b[:, b], x1_b[:, b], ALU.add))
                dve.wait_ge(comp_ready, B)
                step(dve.tensor_tensor(x2_b[:, b, CT, :], comp_ps[:, b, :], x2_b[:, b, CT, :], ALU.add))
                for t in range(b * TB, (b + 1) * TB):
                    dve.bn_stats(stats[:, t, :], x2[:, t, :]).then_inc(stats_done, 1)
                for t in range(b * TB, (b + 1) * TB):
                    dve.wait_ge(stats_done, t + 1)
                    dve.bn_aggr(moments[:, t, :], stats[:, t, :]).then_inc(moments_done, 1)
                dve.wait_ge(root_done, b + 1)
                tiles = slice(b * TB, (b + 1) * TB)
                step(dve.reciprocal(scale[:, tiles], root[:, tiles]))
                for t in range(b * TB, (b + 1) * TB):
                    dve.tensor_scalar(x2[:, t, :], x2[:, t, :], moments[:, t, 0:1], scale[:, t:t + 1],
                                      ALU.subtract, ALU.mult).then_inc(x2_done, 1)

            def spread(a):
                return a[:, :].rearrange("p (t a) -> p t a", a=1).broadcast_to([P, TILES, EX])

            def over_tokens(a):
                return a[:, :].rearrange("p (a e) -> p a e", a=1).broadcast_to([P, TILES, EX])

            dve.wait_ge(logits_ready, TILES // 2)
            step(dve.tensor_reduce(top[:, :], logits_ps[:, :, :], AX.X, ALU.max))
            dve.tensor_tensor(logits[:, :, :], logits_ps[:, :, :], spread(top), ALU.subtract).then_inc(shifted, 1)
            dve.wait_ge(exp_done, 1)
            step(dve.tensor_reduce(top[:, :], probs[:, :, :], AX.X, ALU.add))
            step(dve.reciprocal(inv[:, :], top[:, :]))
            step(dve.tensor_tensor(probs[:, :, :], probs[:, :, :], spread(inv), ALU.mult))
            step(dve.tensor_reduce(gate_of[:, :], probs[:, :, :], AX.X, ALU.max))
            step(dve.tensor_tensor(work[:, :, :], probs[:, :, :], spread(gate_of), ALU.is_ge))
            dve.wait_ge(patterns, 7)
            step(dve.tensor_tensor(work[:, :, :], work[:, :, :], over_tokens(rank), ALU.mult))
            step(dve.tensor_reduce(first[:, :], work[:, :, :], AX.X, ALU.max))
            mask_t = mask[:, :, :, :].rearrange("p b t e -> p (b t) e")
            step(dve.tensor_tensor(mask_t, over_tokens(rank), spread(first), ALU.is_equal))
            step(dve.memset(tiles_before[:, :, 0, :], 0.0))
            for t in range(1, TB):
                ins = dve.tensor_tensor(tiles_before[:, :, t, :], tiles_before[:, :, t - 1, :],
                                        mask[:, :, t - 1, :], ALU.add)
                if t < TB - 1:
                    step(ins)
            ins.then_inc(mask_done, 1)
            dve.wait_ge(count_ready, 1)
            step(dve.tensor_tensor(work[:, :, :], count_ps[:, :, :, :].rearrange("p b t e -> p (b t) e"),
                                   mask_t, ALU.mult))
            step(dve.tensor_reduce(slot[:, :], work[:, :, :], AX.X, ALU.add))
            step(dve.tensor_tensor(work[:, :, :], mask_t, over_tokens(expert), ALU.mult))
            step(dve.tensor_reduce(row[:, :], work[:, :, :], AX.X, ALU.add))
            step(dve.tensor_scalar(keep[:, :], slot[:, :], float(CAP), None, ALU.is_lt))
            step(dve.scalar_tensor_tensor(out=row[:, :], in0=row[:, :], scalar=float(B * CAP),
                                          in1=base[:, :, :].rearrange("p b t -> p (b t)"),
                                          op0=ALU.mult, op1=ALU.add))
            step(dve.tensor_tensor(slot[:, :], slot[:, :], keep[:, :], ALU.mult))
            step(dve.tensor_tensor(row_out[:, :], row[:, :], slot[:, :], ALU.add))
            step(dve.tensor_tensor(row_in[:, :], row_out[:, :], trash[:, :], ALU.subtract))
            step(dve.tensor_tensor(row_in[:, :], row_in[:, :], keep[:, :], ALU.mult))
            step(dve.tensor_tensor(row_in[:, :], row_in[:, :], trash[:, :], ALU.add))
            step(dve.tensor_copy(slot_of[:, :], row_out[:, :]))
            step(dve.tensor_tensor(gate_of[:, :], gate_of[:, :], keep[:, :], ALU.mult))
            dve.tensor_copy(send_to[:, :], row_in[:, :]).then_inc(rows_ready, 1)


def build_experts(nc, W1, W2, xe_dram, ye_dram, const):
    EX, D, HID = W1.shape
    KC = D // P
    HC = HID // P
    R = ye_dram.shape[0] // EX
    RT = R // P
    assert R == BANK
    ident = const[0]
    with ExitStack() as ctx:
        def sb(name, shape, dt=F32):
            return ctx.enter_context(nc.sbuf_tensor(name, shape, dt))

        def sem(name):
            return ctx.enter_context(nc.semaphore(name))

        def split_pair(name, shape):
            return sb(name + "_hi", shape, F32R), sb(name + "_lo", shape, F32R)

        w1_raw = sb("w1_raw", [P, KC, HID])
        w2_raw = sb("w2_raw", [P, HC, D])
        w1 = split_pair("w1", [P, KC, HID])
        w2 = split_pair("w2", [P, HC, D])
        xe = sb("xe", [P, 2, RT, D])
        xeT = split_pair("xeT", [P, KC, R])
        h_act = sb("h_act", [P, 2, R])
        h = split_pair("h", [P, HC, R])
        y = sb("y", [P, 2, RT, D])
        xeT_ps = ctx.enter_context(nc.psum_tensor("xeT_ps", [P, KC, R], F32))
        h_ps = [ctx.enter_context(nc.psum_tensor(f"h_ps{i}", [P, R], F32)) for i in range(2)]
        y_ps = [ctx.enter_context(nc.psum_tensor(f"y_ps{i}", [P, D], F32)) for i in range(4)]

        w_in = sem("w_in")
        w1_hi_done = sem("w1_hi_done")
        w1_split = sem("w1_split")
        w2_hi_done = sem("w2_hi_done")
        w2_split = sem("w2_split")
        xe_in = [sem(f"xe_in{i}") for i in range(2)]
        xeT_ready = sem("xeT_ready")
        xeT_hi_done = sem("xeT_hi_done")
        xeT_done = sem("xeT_done")
        h_ready = sem("h_ready")
        gelu_done = sem("gelu_done")
        h_hi_done = sem("h_hi_done")
        h_done = sem("h_done")
        y_ready = sem("y_ready")
        y_done = sem("y_done")
        y_stored = sem("y_stored")
        block = ctx.enter_context(nc.Block())

        @block.sync
        def _(sp):
            def load(e, s):
                wait(sp, w2_split, e)
                sp.dma_start(w1_raw[:, :, :], W1[e].rearrange("(k p) h -> p k h", p=P)).then_inc(w_in, 16)
                sp.dma_start(w2_raw[:, :, :], W2[e].rearrange("(c p) d -> p c d", p=P)).then_inc(w_in, 16)
                sp.dma_start(xe[:, s], xe_dram[e * R:(e + 1) * R, :].rearrange("(t p) d -> p t d", p=P)
                             ).then_inc(xe_in[s], 16)

            load(0, 0)
            for e in range(EX):
                if e + 1 < EX:
                    load(e + 1, (e + 1) % 2)
                sp.wait_ge(y_done, RT * (e + 1))
                sp.dma_start(ye_dram[e * R:(e + 1) * R, :].rearrange("(t p) d -> p t d", p=P), y[:, e % 2]
                             ).then_inc(y_stored, 16)
            sp.wait_ge(y_stored, 16 * EX)

        @block.tensor
        def _(pe):
            for e in range(EX):
                pe.wait_ge(xe_in[e % 2], 16 * (e // 2 + 1))
                wait(pe, xeT_done, e)
                for k in range(KC):
                    for t in range(RT):
                        last = pe.transpose(xeT_ps[:, k, t * P:(t + 1) * P], xe[:, e % 2, t, k * P:(k + 1) * P],
                                            ident[:, :])
                last.then_inc(xeT_ready, 1)
                pe.wait_ge(xeT_done, e + 1)
                pe.wait_ge(w1_split, e + 1)
                for c in range(HC):
                    n = e * HC + c
                    wait(pe, gelu_done, n - 1)
                    for i, (a, b) in enumerate(((0, 0), (0, 1), (1, 0))):
                        for k in range(KC):
                            last = pe.matmul(h_ps[n % 2][:, :], w1[a][:, k, c * P:(c + 1) * P], xeT[b][:, k, :],
                                             start=(i == 0 and k == 0), stop=(i == 2 and k == KC - 1))
                    last.then_inc(h_ready, 1)
                pe.wait_ge(w2_split, e + 1)
                pe.wait_ge(h_done, HC * (e + 1))
                for t in range(RT):
                    wait(pe, y_done, RT * (e - 1) + t + 1)
                    for i, (a, b) in enumerate(((0, 0), (0, 1), (1, 0))):
                        for c in range(HC):
                            last = pe.matmul(y_ps[t][:, :], h[a][:, c, t * P:(t + 1) * P], w2[b][:, c, :],
                                             start=(i == 0 and c == 0), stop=(i == 2 and c == HC - 1))
                    last.then_inc(y_ready, 1)

        @block.scalar
        def _(act):
            for e in range(EX):
                act.wait_ge(xeT_ready, e + 1)
                wait(act, h_ready, HC * e)
                act.activation(xeT[0][:, :, :], xeT_ps[:, :, :], ACT.Copy).then_inc(xeT_hi_done, 1)
                for c in range(HC):
                    n = e * HC + c
                    act.wait_ge(h_ready, n + 1)
                    wait(act, h_done, n - 1)
                    act.activation(h_act[:, n % 2, :], h_ps[n % 2][:, :], ACT.Gelu_apprx_tanh).then_inc(gelu_done, 1)
                for t in range(RT):
                    act.wait_ge(y_ready, e * RT + t + 1)
                    wait(act, y_stored, 16 * (e - 1))
                    act.activation(y[:, e % 2, t, :], y_ps[t][:, :], ACT.Copy).then_inc(y_done, 1)

        @block.vector
        def _(dve):
            for e in range(EX):
                dve.wait_ge(w_in, 32 * (e + 1))
                wait(dve, h_ready, HC * e)
                dve.tensor_copy(w1[0][:, :, :], w1_raw[:, :, :]).then_inc(w1_hi_done, 1)
                dve.wait_ge(w1_hi_done, e + 1)
                dve.tensor_tensor(w1[1][:, :, :], w1_raw[:, :, :], w1[0][:, :, :].bitcast(F32),
                                  ALU.subtract).then_inc(w1_split, 1)
                dve.wait_ge(xeT_hi_done, e + 1)
                dve.tensor_tensor(xeT[1][:, :, :], xeT_ps[:, :, :], xeT[0][:, :, :].bitcast(F32),
                                  ALU.subtract).then_inc(xeT_done, 1)
                wait(dve, y_ready, RT * e)
                dve.tensor_copy(w2[0][:, :, :], w2_raw[:, :, :]).then_inc(w2_hi_done, 1)
                dve.wait_ge(w2_hi_done, e + 1)
                dve.tensor_tensor(w2[1][:, :, :], w2_raw[:, :, :], w2[0][:, :, :].bitcast(F32),
                                  ALU.subtract).then_inc(w2_split, 1)
                for c in range(HC):
                    n = e * HC + c
                    dve.wait_ge(gelu_done, n + 1)
                    dve.tensor_copy(h[0][:, c, :], h_act[:, n % 2, :]).then_inc(h_hi_done, 1)
                    dve.wait_ge(h_hi_done, n + 1)
                    dve.tensor_tensor(h[1][:, c, :], h_act[:, n % 2, :], h[0][:, c, :].bitcast(F32),
                                      ALU.subtract).then_inc(h_done, 1)


def build_combine_norm(nc, ye_dram, x2, slot_of, gate_of, out):
    B, N, D = out.shape
    TILES = B * N // P
    G = 8
    with ExitStack() as ctx:
        def sb(name, shape, dt=F32):
            return ctx.enter_context(nc.sbuf_tensor(name, shape, dt))

        def sem(name):
            return ctx.enter_context(nc.semaphore(name))

        y = sb("y_tok", [P, TILES, D])
        eps = sb("eps3", [P, 1])
        stats = sb("stats3", [P, TILES, 6])
        moments = sb("moments3", [P, TILES, 2])
        root = sb("root3", [P, TILES])
        scale = sb("scale3", [P, TILES])
        gathered = [sem(f"gathered{g}") for g in range(TILES // G)]
        eps_set = sem("eps3_set")
        z_done = sem("z3_done")
        stats_done = sem("stats3_done")
        moments_done = sem("moments3_done")
        root_done = sem("root3_done")
        scale_done = sem("scale3_done")
        out_done = sem("out_done")
        stored = sem("out_stored")
        block = ctx.enter_context(nc.Block())

        @block.gpsimd
        def _(pool):
            for t in range(TILES):
                pool.indirect_dma_start(out=y[:, t, :], out_offset=None, in_=ye_dram[:, :],
                                        in_offset=bass.IndirectOffsetOnAxis(ap=slot_of[:, t:t + 1], axis=0)
                                        ).then_inc(gathered[t // G], 16)

        @block.sync
        def _(sp):
            for b in range(B):
                sp.wait_ge(out_done, G * (b + 1))
                sp.dma_start(out[b].rearrange("(t p) d -> p t d", p=P), y[:, b * G:(b + 1) * G, :]
                             ).then_inc(stored, 16)
            sp.wait_ge(stored, 16 * B)

        @block.scalar
        def _(act):
            act.wait_ge(eps_set, 1)
            for b in range(B):
                tiles = slice(b * G, (b + 1) * G)
                act.wait_ge(moments_done, G * (b + 1))
                act.activation(root[:, tiles], moments[:, tiles, 1], ACT.Sqrt, bias=eps[:, :]).then_inc(root_done, 1)

        @block.vector
        def _(dve):
            dve.memset(eps[:, :], 1e-5).then_inc(eps_set, 1)
            for b in range(B):
                dve.wait_ge(gathered[b], 16 * G)
                for t in range(b * G, (b + 1) * G):
                    dve.scalar_tensor_tensor(out=y[:, t, :], in0=y[:, t, :], scalar=gate_of[:, t:t + 1],
                                             in1=x2[:, t, :], op0=ALU.mult, op1=ALU.add).then_inc(z_done, 1)
                for t in range(b * G, (b + 1) * G):
                    dve.wait_ge(z_done, t + 1)
                    dve.bn_stats(stats[:, t, :], y[:, t, :]).then_inc(stats_done, 1)
                for t in range(b * G, (b + 1) * G):
                    dve.wait_ge(stats_done, t + 1)
                    dve.bn_aggr(moments[:, t, :], stats[:, t, :]).then_inc(moments_done, 1)
                dve.wait_ge(root_done, b + 1)
                tiles = slice(b * G, (b + 1) * G)
                dve.reciprocal(scale[:, tiles], root[:, tiles]).then_inc(scale_done, 1)
                dve.wait_ge(scale_done, b + 1)
                for t in range(b * G, (b + 1) * G):
                    dve.tensor_scalar(y[:, t, :], y[:, t, :], moments[:, t, 0:1], scale[:, t:t + 1],
                                      ALU.subtract, ALU.mult).then_inc(out_done, 1)


def build(nc, x, ctx_in, Wq, Wk, Wv, Wp, bp, conv_w, conv_b, Wg, W1, W2, out):
    B, N, D = x.shape
    H, _, E = Wq.shape
    EX = Wg.shape[1]
    TILES = B * N // P
    xT_parts = nc.dram_tensor("xT_parts", [B, P, HILO, D // P, N], F32, kind="Internal").ap()
    o_dram = nc.dram_tensor("o_tokens", [B, N, H * E], F32, kind="Internal").ap()
    xe_dram = nc.dram_tensor("expert_rows", [2 * B * N, D], F32, kind="Internal").ap()
    ye_dram = nc.dram_tensor("expert_outputs", [B * N, D], F32, kind="Internal").ap()
    with ExitStack() as ctx:
        const = build_constants(nc, ctx)
        build_transpose_x(nc, x, xT_parts, const)
        build_attention(nc, xT_parts, Wq, Wk, Wv, o_dram, const)
        x2 = ctx.enter_context(nc.sbuf_tensor("x2", [P, TILES, D], F32))
        slot_of = ctx.enter_context(nc.sbuf_tensor("slot_of", [P, TILES], mybir.dt.uint32))
        gate_of = ctx.enter_context(nc.sbuf_tensor("gate_of", [P, TILES], F32))
        with nc.sbuf_tensor("x1", [P, TILES, D], F32) as x1:
            build_project_norm(nc, o_dram, x, Wp, bp, x1, const)
            build_memory_route(nc, ctx_in, conv_w, conv_b, Wg, x1, x2, xe_dram, slot_of, gate_of, const)
        build_experts(nc, W1, W2, xe_dram, ye_dram, const)
        build_combine_norm(nc, ye_dram, x2, slot_of, gate_of, out)


_INS = ['x', 'ctx_1024', 'L0_attn_Wq', 'L0_attn_Wk', 'L0_attn_Wv', 'L0_attn_Wp', 'L0_attn_bp',
        'L0_xattn_conv_w', 'L0_xattn_conv_b', 'L0_ffn_Wg', 'L0_ffn_W1', 'L0_ffn_W2']


def kernel(**inputs):
    import numpy as _np
    import concourse.bacc as _bacc
    from concourse import mybir as _mybir
    from concourse.bass_utils import run_bass_kernel_spmd as _run

    nc = _bacc.Bacc("TRN2", target_bir_lowering=False, num_devices=1)
    arrays, args = {}, []
    for name in _INS:
        a = _np.ascontiguousarray(inputs[name])
        arrays[f"in_{name}_dram"] = a
        args.append(nc.dram_tensor(f"in_{name}_dram", a.shape, _mybir.dt.from_np(a.dtype), kind="ExternalInput").ap())
    shape = inputs['x'].shape
    args.append(nc.dram_tensor("out_dram", shape, _mybir.dt.float32, kind="ExternalOutput").ap())
    build(nc, *args)
    r = _run(nc, [arrays], core_ids=[0])
    return r.results[0]["out_dram"]
```

```python
import concourse.bass as bass
from concourse import mybir
from contextlib import ExitStack

F32 = mybir.dt.float32
F32R = mybir.dt.float32r
ACT = mybir.ActivationFunctionType
ALU = mybir.AluOpType
AX = mybir.AxisListType

P = 128
BANK = 512
HILO = 2

QK_BITES = 4
V_BITES = 4
IT_BITES = 2 * QK_BITES + V_BITES
Q0, Q1, K0, K1 = range(QK_BITES)
BITE_SLOTS = ((1, 2, 3, 5), (1, 2, 3, 5, 6, 7, 9, 10))


def bites_to(pair, of_it):
    return IT_BITES * of_it + (QK_BITES if pair == 0 else IT_BITES)


def v_bites_to(of_it):
    return IT_BITES * of_it + QK_BITES + V_BITES


def wait(eng, sem, value):
    if isinstance(value, int) and value <= 0:
        return
    eng.wait_ge(sem, value)


def wait_then(eng, sem, value, passed):
    wait(eng, sem, value)
    if not isinstance(value, int):
        eng.sem_inc(passed, 1)


def build_constants(nc, ctx):
    ident = ctx.enter_context(nc.sbuf_tensor("ident", [P, P], F32))
    ident_zeroed = ctx.enter_context(nc.semaphore("ident_zeroed"))
    ident_ready = ctx.enter_context(nc.semaphore("ident_ready"))
    passed = ctx.enter_context(nc.semaphore("passed"))
    return ident, ident_zeroed, ident_ready, passed


def build_transpose_x(nc, x, xT_parts, const):
    B, N, D = x.shape
    TILES = N // P
    KC = D // P
    PAIRS = TILES // 2
    GROUPS = B * PAIRS
    ident, ident_zeroed, ident_ready, _ = const
    with ExitStack() as ctx:
        x_tok = ctx.enter_context(nc.sbuf_tensor("x_tok", [P, B, TILES, D], F32))
        xT_sb = ctx.enter_context(nc.sbuf_tensor("xT_sb", [P, B, HILO, KC, N], F32R))
        xT_ps = [ctx.enter_context(nc.psum_tensor(f"xT_ps{i}", [P, KC, 2 * P], F32)) for i in range(2)]
        x_in = [ctx.enter_context(nc.semaphore(f"x_in{b}")) for b in range(B)]
        transposed = ctx.enter_context(nc.semaphore("x_transposed"))
        high_done = ctx.enter_context(nc.semaphore("xT_high_done"))
        low_done = ctx.enter_context(nc.semaphore("xT_low_done"))
        stored = ctx.enter_context(nc.semaphore("xT_stored"))
        block = ctx.enter_context(nc.Block())

        def where(g, part):
            b, i = divmod(g, PAIRS)
            return xT_sb[:, b, part, :, i * 2 * P:(i + 1) * 2 * P]

        @block.gpsimd
        def _(pool):
            pool.memset(ident[:, :], 0.0).then_inc(ident_zeroed, 1)
            pool.wait_ge(ident_zeroed, 1)
            pool.affine_select(out=ident[:, :], in_=ident[:, :], compare_op=ALU.not_equal, fill=1.0,
                               base=0, pattern=[[-1, P]], channel_multiplier=1).then_inc(ident_ready, 1)

        @block.sync
        def _(sp):
            for b in range(B):
                sp.dma_start(x_tok[:, b], x[b].rearrange("(t p) d -> p t d", p=P)).then_inc(x_in[b], 16)
            for b in range(B):
                sp.wait_ge(low_done, PAIRS * (b + 1))
                sp.dma_start(xT_parts[b].rearrange("p a k n -> p (a k n)"),
                             xT_sb[:, b].rearrange("p a k n -> p (a k n)").bitcast(F32)).then_inc(stored, 16)
            sp.wait_ge(stored, 16 * B)

        @block.tensor
        def _(pe):
            pe.wait_ge(ident_ready, 1)
            for g in range(GROUPS):
                b, i = divmod(g, PAIRS)
                if i == 0:
                    pe.wait_ge(x_in[b], 16)
                wait(pe, low_done, g - 1)
                for t in range(2):
                    for k in range(KC):
                        last = pe.transpose(xT_ps[g % 2][:, k, t * P:(t + 1) * P],
                                            x_tok[:, b, 2 * i + t, k * P:(k + 1) * P], ident[:, :])
                last.then_inc(transposed, 1)

        @block.scalar
        def _(act):
            for g in range(GROUPS):
                act.wait_ge(transposed, g + 1)
                act.activation(where(g, 0), xT_ps[g % 2][:, :, :], ACT.Copy).then_inc(high_done, 1)

        @block.vector
        def _(dve):
            for g in range(GROUPS):
                dve.wait_ge(high_done, g + 1)
                dve.tensor_tensor(where(g, 1), xT_ps[g % 2][:, :, :], where(g, 0).bitcast(F32),
                                  ALU.subtract).then_inc(low_done, 1)


def build_attention(nc, xT_parts, Wq, Wk, Wv, o_dram, xe_dram, y_dram, const):
    B, _, _, KC, N = xT_parts.shape
    H, D, E = Wq.shape
    TILES = N // P
    HP = TILES
    CH = BANK // P
    PAIR_T = 2 * TILES
    IT_T = 2 * PAIR_T
    ITS = B * H // 4
    PER_BATCH = H // 4
    NT = ITS * IT_T
    PAIRS = 2 * ITS
    SCALE = E ** -0.5
    CHUNKS = NT // CH
    FILL_ROWS = 2
    FILLS = B * N // (P * FILL_ROWS)
    ASM = 12
    assert 2 * E == P and HP == 8 and SCALE == 0.125
    ident = const[0]

    with ExitStack() as ctx:
        def sb(name, shape, dt=F32):
            return ctx.enter_context(nc.sbuf_tensor(name, shape, dt))

        def sem(name):
            return ctx.enter_context(nc.semaphore(name))

        xT = sb("xT", [P, HILO, KC, N], F32R)
        w_raw = sb("w_raw", [P, 2, KC, 2 * E])
        w_hi = sb("w_hi", [P, 2, KC, 2 * E], F32R)
        w_lo = sb("w_lo", [P, 2, KC, 2 * E], F32R)
        wv_raw = sb("wv_raw", [P, KC, 4 * E])
        wv_hi = sb("wv_hi", [P, KC, 4 * E], F32R)
        wv_lo = sb("wv_lo", [P, KC, 4 * E], F32R)
        qk_hi = sb("qk_hi", [P, 2, N], F32R)
        qk_lo = sb("qk_lo", [P, 2, N], F32R)
        q_st = sb("q_st", [P, 2, 2, N], F32R)
        k_hh = sb("k_hh", [P, 2, 2, N], F32R)
        k_ll = sb("k_ll", [P, 2, 2, N], F32R)
        v_st = sb("v_st", [P, 3, HP, 2, HILO, E], F32R)
        probs = sb("probs", [P, 2, N])
        pT_hi = sb("pT_hi", [P, 2, HP, BANK], F32R)
        pT_lo = sb("pT_lo", [P, 2, HP, BANK], F32R)
        oT = sb("oT", [P, 2, BANK])
        o_sum = sb("o_sum", [P, CH, E])
        o_out = sb("o_out", [P, 2, TILES, 2 * E])
        neg_max = sb("neg_max", [P, 4])
        zeros = sb("zeros", [P, FILL_ROWS * D])
        row_tail = sb("row_tail", [P, FILLS * FILL_ROWS, 4])
        row_sum = sb("row_sum", [P, IT_T])
        inv_sum = sb("inv_sum", [P, CH])

        scores = [ctx.enter_context(nc.psum_tensor(f"scores{i}", [P, N], F32)) for i in range(2)]
        pT_ps = [ctx.enter_context(nc.psum_tensor(f"pT_ps{i}", [P, CH, P], F32)) for i in range(2)]
        av_ps = ctx.enter_context(nc.psum_tensor("av_ps", [P, BANK], F32))
        misc_ps = ctx.enter_context(nc.psum_tensor("misc_ps", [P, BANK], F32))

        zeroed = sem("zeroed")
        filled = sem("filled")
        w_loaded = sem("w_loaded")
        w_split_hi = sem("w_split_hi")
        w_split = sem("w_split")
        wv_loaded = sem("wv_loaded")
        wv_split_hi = sem("wv_split_hi")
        wv_split = sem("wv_split")
        v_moved = sem("v_moved")
        xT_loaded = sem("xT_loaded")
        qk_laid = sem("qk_laid")
        scores_ready = sem("scores_ready")
        max_ready = sem("max_ready")
        probs_ready = sem("probs_ready")
        pT_ready = sem("pT_ready")
        pT_hi_done = sem("pT_hi_done")
        pT_lo_done = sem("pT_lo_done")
        av_ready = sem("av_ready")
        oT_done = sem("oT_done")
        fold_ready = sem("fold_ready")
        fold_read = sem("fold_read")
        inv_done = sem("inv_done")
        o_done = sem("o_done")
        o_stored = sem("o_stored")
        bite_ready = sem("bite_ready")
        bite_hi_done = sem("bite_hi_done")
        bite_lo_done = sem("bite_lo_done")

        block = ctx.enter_context(nc.Block())

        def run(eng, slot):
            for tt in range(IT_T):
                slot(0, tt)
            with eng.Fori(1, ITS - 1) as it:
                for tt in range(IT_T):
                    slot(it, tt)
            for tt in range(IT_T):
                slot(ITS - 1, tt)
            for tt in range(IT_T, IT_T + CH + 2):
                slot(ITS - 1, tt)

        def exists(it, tt, ahead=0):
            return not (isinstance(it, int) and it == ITS - 1 and tt + ahead >= IT_T)

        def bite_of(pair, u):
            return BITE_SLOTS[pair].index(u) if u in BITE_SLOTS[pair] else None

        def bites_before(it, pair, u):
            return bites_to(pair, it) + (V_BITES if pair == 0 else 0) + sum(x < u for x in BITE_SLOTS[pair])

        v_bank = misc_ps[:, :].rearrange("p (m a h e) -> p a m h e", m=2, a=2, h=2)

        def v_part(k, part):
            mts = slice(2 * (k - QK_BITES), 2 * (k - QK_BITES) + 2)
            return v_st[:, 0:2, mts, :, part, :]

        @block.sync
        def _(sp):
            def load_w(g, head):
                wait_then(sp, w_split, g, const[3])
                for i, w in enumerate((Wq, Wk)):
                    for k in range(KC):
                        sp.dma_start(w_raw[:, i, k, :].rearrange("p (h e) -> p h e", h=2),
                                     w[bass.ds(head, 2), k * P:(k + 1) * P, :].rearrange("h d e -> d h e")
                                     ).then_inc(w_loaded, 16)

            def load_wv(it, head):
                wait_then(sp, wv_split, it, const[3])
                for k in range(KC):
                    sp.dma_start(wv_raw[:, k, :].rearrange("p (h e) -> p h e", h=4),
                                 Wv[bass.ds(head, 4), k * P:(k + 1) * P, :].rearrange("h d e -> d h e")
                                 ).then_inc(wv_loaded, 16)

            def move_v(it):
                wait_then(sp, bite_lo_done, v_bites_to(it), const[3])
                wait(sp, av_ready, 8 * it)
                sp.dma_start(v_st[:, 2].rearrange("p m h a e -> p (m h a e)").bitcast(F32),
                             v_st[:, 1].rearrange("p m h a e -> p (m h a e)").bitcast(F32)).then_inc(v_moved, 16)

            def load_xT(batch):
                sp.dma_start(xT[:, :, :, :].rearrange("p a k n -> p (a k n)").bitcast(F32),
                             xT_parts[bass.ds(batch, 1)].rearrange("b p a k n -> p (b a k n)")
                             ).then_inc(xT_loaded, 16)

            def lay_out(g, par, bites):
                wait_then(sp, bite_lo_done, bites, const[3])
                wait(sp, scores_ready, PAIR_T * (g - 1))
                for h in range(2):
                    rows = slice(h * E, (h + 1) * E)
                    lo, hi = slice(0, E), slice(E, P)
                    for dst, src in ((q_st[lo, par, h], qk_hi[rows, 0]), (q_st[hi, par, h], qk_lo[rows, 0])):
                        sp.dma_start(dst.bitcast(F32), src.bitcast(F32)).then_inc(qk_laid, 16)
                    for buf, src in ((k_hh, qk_hi[rows, 1]), (k_ll, qk_lo[rows, 1])):
                        for half in (lo, hi):
                            sp.dma_start(buf[half, par, h].bitcast(F32), src.bitcast(F32)).then_inc(qk_laid, 16)

            def store_o(g, par, batch, head):
                wait_then(sp, o_done, 4 * (g + 1), const[3])
                sp.dma_start(o_dram[bass.ds(batch, 1), :, bass.ds(head * E, 2 * E)]
                             .rearrange("b (t p) n -> p (b t) n", p=P), o_out[:, par]).then_inc(o_stored, 16)

            def step(it, s):
                g = 2 * it + s
                final = isinstance(it, int) and it == ITS - 1
                if not final:
                    nxt = it + 1
                    load_w(g + 2, 4 * (nxt % PER_BATCH) + 2 * s)
                    if s == 0:
                        load_wv(nxt, 4 * (nxt % PER_BATCH))
                if not (isinstance(it, int) and g == 0):
                    if s == 0:
                        prev = it - 1
                        store_o(g - 1, 1, prev // PER_BATCH, 4 * (prev % PER_BATCH) + 2)
                    else:
                        store_o(g - 1, 0, it // PER_BATCH, 4 * (it % PER_BATCH))
                if s == 0:
                    move_v(it)
                if not (final and s == 1):
                    lay_out(g + 1, (s + 1) % 2, bites_to(1, it) if s == 0 else bites_to(0, it + 1))
                if s == 0 and not final:
                    wait_then(sp, bite_ready, bites_to(1, it), const[3])
                    load_xT(nxt // PER_BATCH)

            load_w(0, 0)
            load_xT(0)
            load_wv(0, 0)
            load_w(1, 2)
            lay_out(0, 0, bites_to(0, 0))
            for s in range(2):
                step(0, s)
            with sp.Fori(1, ITS - 1) as it:
                for s in range(2):
                    step(it, s)
            for s in range(2):
                step(ITS - 1, s)
            store_o(PAIRS - 1, 1, B - 1, H - 2)
            sp.wait_ge(o_stored, 16 * PAIRS)

        @block.gpsimd
        def _(pool):
            def split_w(g, read):
                wait(pool, w_loaded, 4 * 16 * (g + 1))
                wait_then(pool, bite_ready, read, const[3])
                pool.tensor_copy(w_hi[:, :, :, :], w_raw[:, :, :, :]).then_inc(w_split_hi, 1)
                wait(pool, w_split_hi, g + 1)
                pool.tensor_tensor(w_lo[:, :, :, :], w_raw[:, :, :, :], w_hi[:, :, :, :].bitcast(F32),
                                   ALU.subtract).then_inc(w_split, 1)

            def split_wv(it):
                wait(pool, wv_loaded, 2 * 16 * (it + 1))
                wait_then(pool, bite_ready, v_bites_to(it - 1), const[3])
                pool.tensor_copy(wv_hi[:, :, :], wv_raw[:, :, :]).then_inc(wv_split_hi, 1)
                wait(pool, wv_split_hi, it + 1)
                pool.tensor_tensor(wv_lo[:, :, :], wv_raw[:, :, :], wv_hi[:, :, :].bitcast(F32),
                                   ALU.subtract).then_inc(wv_split, 1)

            def step(it):
                split_w(2 * it + 2, bites_to(1, it))
                split_wv(it + 1)
                split_w(2 * it + 3, bites_to(0, it + 1))

            split_w(0, 0)
            split_wv(0)
            split_w(1, bites_to(0, 0))
            pool.memset(zeros[:, :], 0.0).then_inc(zeroed, 1)
            pool.memset(row_tail[:, :, :], 0.0).then_inc(zeroed, 1)
            pool.wait_ge(zeroed, 2)
            pool.iota(row_tail[:, :, 0:1].bitcast(mybir.dt.uint32),
                      pattern=[[P * FILL_ROWS, FILLS], [1, FILL_ROWS]], base=B * N,
                      channel_multiplier=FILL_ROWS).then_inc(zeroed, 1)
            pool.wait_ge(zeroed, 3)
            for i in range(FILLS):
                rows = slice(i * P * FILL_ROWS, (i + 1) * P * FILL_ROWS)
                pool.dma_start(xe_dram[rows, 0:D].rearrange("(p r) d -> p r d", p=P),
                               zeros[:, :].rearrange("p (r d) -> p r d", d=D)).then_inc(filled, 16)
                pool.dma_start(xe_dram[rows, D:].rearrange("(p r) d -> p r d", p=P),
                               row_tail[:, i * FILL_ROWS:(i + 1) * FILL_ROWS, :]).then_inc(filled, 16)
                pool.dma_start(y_dram[rows, :].rearrange("(p r) d -> p (r d)", p=P), zeros[:, :]
                               ).then_inc(filled, 16)
            step(0)
            with pool.Fori(1, ITS - 1) as it:
                step(it)
            pool.wait_ge(filled, 16 * 3 * FILLS)

        @block.tensor
        def _(pe):
            def misc_free(folds, bites):
                wait(pe, fold_read, folds)
                wait(pe, bite_lo_done, bites)

            def bite(g, k, of_it, before, folds):
                wait(pe, xT_loaded, 16 * (of_it + 1))
                misc_free(folds, before)
                if k < QK_BITES:
                    wait(pe, w_split, g + 1)
                    i, c = divmod(k, 2)
                    cols = slice(c * BANK, (c + 1) * BANK)
                    for n, (w, part) in enumerate(((w_hi, 0), (w_lo, 0), (w_hi, 1))):
                        for kc in range(KC):
                            last = pe.matmul(misc_ps[:, :], w[:, i, kc, :], xT[:, part, kc, cols],
                                             start=(n == 0 and kc == 0), stop=(n == 2 and kc == KC - 1))
                else:
                    wait(pe, wv_split, of_it + 1)
                    for m in range(2):
                        mt = 2 * (k - QK_BITES) + m
                        for n, (w, part) in enumerate(((wv_hi, 0), (wv_lo, 0), (wv_hi, 1))):
                            for kc in range(KC):
                                last = pe.matmul(misc_ps[:, m * 4 * E:(m + 1) * 4 * E],
                                                 xT[:, part, kc, mt * P:(mt + 1) * P], w[:, kc, :],
                                                 start=(n == 0 and kc == 0), stop=(n == 2 and kc == KC - 1))
                last.then_inc(bite_ready, 1)

            def score(it, tt):
                T = it * IT_T + tt
                pair, u = divmod(tt, PAIR_T)
                h, j = divmod(u, TILES)
                par = pair % 2
                if u == 0:
                    wait(pe, qk_laid, 16 * ASM * ((T // PAIR_T if isinstance(T, int) else 2 * it + pair) + 1))
                wait(pe, probs_ready, T - 1)
                q = q_st[:, par, h, j * P:(j + 1) * P]
                for c in range(N // BANK):
                    cols = slice(c * BANK, (c + 1) * BANK)
                    pe.matmul(scores[tt % 2][:, cols], q, k_hh[:, par, h, cols], start=True, stop=False)
                    last = pe.matmul(scores[tt % 2][:, cols], q, k_ll[:, par, h, cols], start=False, stop=True)
                last.then_inc(scores_ready, 1)

            def slot(it, tt):
                T = it * IT_T + tt
                pair, u = divmod(tt, PAIR_T)
                first = isinstance(it, int) and it == 0
                if exists(it, tt, 2):
                    score(it, tt + 2)
                if exists(it, tt):
                    wait(pe, probs_ready, T + 1)
                    for half in range(2):
                        wait(pe, pT_lo_done, 2 * T + half - 1)
                        for m in range(CH):
                            mt = half * CH + m
                            last = pe.transpose(pT_ps[half][:, m, :], probs[:, tt % 2, mt * P:(mt + 1) * P],
                                                ident[:, :])
                        last.then_inc(pT_ready, 1)
                if (not first or tt >= CH) and exists(it, tt, -CH):
                    c, part = it * (IT_T // CH) + tt // CH - 1, tt % CH
                    cpar, ch = (tt // CH - 1) % 2, (tt // CH - 1) % 8
                    vpar, h = divmod(ch // 2, 2)
                    if part == 0:
                        wait(pe, pT_lo_done, 2 * CH * (c + 1))
                        wait(pe, oT_done, c)
                        of_it, of_pair = divmod((tt // CH - 1) // 4, 2)
                        if of_pair == 0:
                            wait(pe, bite_lo_done, v_bites_to(it + of_it))
                        else:
                            wait(pe, v_moved, 16 * (it + of_it + 1))
                    for mt in (2 * part, 2 * part + 1):
                        v = v_st[:, 2 * vpar, mt, h].rearrange("p a e -> p (a e)")
                        pe.matmul(av_ps[:, :], v, pT_hi[:, cpar, mt, :], start=(mt == 0), stop=False)
                        last = pe.matmul(av_ps[:, :], v, pT_lo[:, cpar, mt, :], start=False, stop=(mt == HP - 1))
                    if part == CH - 1:
                        last.then_inc(av_ready, 1)
                folds = it * (IT_T // CH) + tt // CH - 1
                k = bite_of(pair, u) if pair < 2 else None
                if k is not None and exists(it, tt, PAIR_T):
                    bite(2 * it + pair + 1, k, it + pair, bites_before(it, pair, u), folds)
                if tt % CH == 0 and (not first or tt >= 2 * CH) and exists(it, tt, -2 * CH):
                    f = folds - 1
                    wait(pe, oT_done, f + 1)
                    if exists(it, tt, PAIR_T):
                        done = bites_before(it, pair, u)
                    else:
                        done = bites_to(1, it)
                    misc_free(f, done)
                    for m in range(CH):
                        last = pe.transpose(misc_ps[:, m * P:(m + 1) * P],
                                            oT[:, (tt // CH) % 2, m * P:(m + 1) * P], ident[:, :])
                    last.then_inc(fold_ready, 1)

            for k in range(QK_BITES + V_BITES):
                bite(0, k, 0, k, 0)
            score(0, 0)
            score(0, 1)
            run(pe, slot)

        @block.scalar
        def _(act):
            def bite_hi(g, k, of_it, before):
                wait(act, bite_ready, before + 1)
                if k < QK_BITES:
                    i, c = divmod(k, 2)
                    wait(act, qk_laid, 16 * ASM * g)
                    act.activation(qk_hi[:, i, c * BANK:(c + 1) * BANK], misc_ps[:, :], ACT.Copy,
                                   scale=SCALE if i == 0 else 1.0).then_inc(bite_hi_done, 1)
                else:
                    wait(act, av_ready, 8 * of_it - 4)
                    wait(act, v_moved, 16 * of_it)
                    act.activation(v_part(k, 0), v_bank, ACT.Copy).then_inc(bite_hi_done, 1)

            def exp(it, tt):
                T = it * IT_T + tt
                wait(act, max_ready, T + 1)
                wait(act, pT_ready, 2 * (T - 1))
                act.activation(probs[:, tt % 2, :], scores[tt % 2][:, :], ACT.Exp,
                               bias=neg_max[:, tt % 4:tt % 4 + 1],
                               accum_out=row_sum[:, tt % IT_T:tt % IT_T + 1]).then_inc(probs_ready, 1)

            def slot(it, tt):
                T = it * IT_T + tt
                pair, u = divmod(tt, PAIR_T)
                first = isinstance(it, int) and it == 0
                k = bite_of(pair, u - 1) if pair < 2 else None
                if k is not None and exists(it, tt, PAIR_T):
                    bite_hi(2 * it + pair + 1, k, it + pair, bites_before(it, pair, u - 1))
                if tt % CH == 0 and (not first or tt >= 2 * CH) and exists(it, tt, -2 * CH):
                    c = it * (IT_T // CH) + tt // CH - 2
                    wait(act, av_ready, c + 1)
                    wait(act, fold_ready, c - 1)
                    act.activation(oT[:, (tt // CH) % 2, :], av_ps[:, :], ACT.Copy).then_inc(oT_done, 1)
                if exists(it, tt, 1):
                    exp(it, tt + 1)
                if exists(it, tt):
                    c = it * (IT_T // CH) + tt // CH
                    if tt % CH == 0:
                        wait(act, av_ready, c - 1)
                    for half in range(2):
                        wait(act, pT_ready, 2 * T + half + 1)
                        act.activation(pT_hi[:, (tt // CH) % 2, half * CH:(half + 1) * CH,
                                             (tt % CH) * P:(tt % CH + 1) * P],
                                       pT_ps[half][:, :, :], ACT.Copy).then_inc(pT_hi_done, 1)

            for k in range(QK_BITES + V_BITES):
                bite_hi(0, k, 0, k)
            exp(0, 0)
            run(act, slot)

        @block.vector
        def _(dve):
            def bite_lo(k, before):
                wait(dve, bite_hi_done, before + 1)
                if k < QK_BITES:
                    i, c = divmod(k, 2)
                    cols = slice(c * BANK, (c + 1) * BANK)
                    dve.scalar_tensor_tensor(out=qk_lo[:, i, cols], in0=misc_ps[:, :],
                                             scalar=SCALE if i == 0 else 1.0, in1=qk_hi[:, i, cols].bitcast(F32),
                                             op0=ALU.mult, op1=ALU.subtract).then_inc(bite_lo_done, 1)
                else:
                    dve.tensor_tensor(v_part(k, 1), v_bank, v_part(k, 0).bitcast(F32), ALU.subtract
                                      ).then_inc(bite_lo_done, 1)

            def maximum(it, tt):
                T = it * IT_T + tt
                wait(dve, scores_ready, T + 1)
                dve.tensor_reduce(neg_max[:, tt % 4:tt % 4 + 1], scores[tt % 2][:, :], AX.X, ALU.max,
                                  negate=True).then_inc(max_ready, 1)

            def slot(it, tt):
                T = it * IT_T + tt
                pair, u = divmod(tt, PAIR_T)
                first = isinstance(it, int) and it == 0
                k = bite_of(pair, u - 1) if pair < 2 else None
                if k is not None and exists(it, tt, PAIR_T):
                    bite_lo(k, bites_before(it, pair, u - 1))
                if tt % CH == 1 and (not first or tt >= 2 * CH) and exists(it, tt, -2 * CH - 1):
                    ft = tt // CH - 2
                    f = it * (IT_T // CH) + ft
                    fpair, ch = divmod(ft % (IT_T // CH), 4)
                    h, half = divmod(ch, 2)
                    sums = (ft * CH) % IT_T
                    wait(dve, o_done, f)
                    dve.reciprocal(inv_sum[:, :], row_sum[:, sums:sums + CH]).then_inc(inv_done, 1)
                    wait(dve, fold_ready, f + 1)
                    dve.tensor_reduce(o_sum[:, :, :], misc_ps[:, :].rearrange("p (m a e) -> p m e a", m=CH, a=2),
                                      AX.X, ALU.add).then_inc(fold_read, 1)
                    wait(dve, inv_done, f + 1)
                    wait(dve, fold_read, f + 1)
                    if ch == 0:
                        wait(dve, o_stored, 16 * (2 * it + (ft // 4) - 1))
                    dve.tensor_tensor(o_out[:, fpair, half * CH:(half + 1) * CH, h * E:(h + 1) * E],
                                      o_sum[:, :, :], inv_sum[:, :].rearrange("p (m a) -> p m a", a=1)
                                      .broadcast_to([P, CH, E]), ALU.mult).then_inc(o_done, 1)
                if exists(it, tt, 2):
                    maximum(it, tt + 2)
                if exists(it, tt):
                    for half in range(2):
                        wait(dve, pT_hi_done, 2 * T + half + 1)
                        where = (slice(None), (tt // CH) % 2, slice(half * CH, (half + 1) * CH),
                                 slice((tt % CH) * P, (tt % CH + 1) * P))
                        dve.tensor_tensor(pT_lo[where], pT_ps[half][:, :, :], pT_hi[where].bitcast(F32),
                                          ALU.subtract).then_inc(pT_lo_done, 1)

            for k in range(QK_BITES + V_BITES):
                bite_lo(k, k)
            maximum(0, 0)
            maximum(0, 1)
            run(dve, slot)


def build_project_route(nc, o_dram, x, Wp, bp, ctx_in, conv_w, conv_b, Wg, x2, xe_dram, weights, const):
    B, N, D = x.shape
    HE = o_dram.shape[2]
    CC = HE // P
    S = ctx_in.shape[1]
    RATE = conv_w.shape[0]
    TILES = B * N // P
    TB = N // P
    HALF = N // 2
    TC = (S - RATE) // RATE + 1
    KC = D // P
    EX = Wg.shape[1]
    CAP = N // EX
    ROWS = EX * B * CAP
    HT = HALF // P
    CT, CP = divmod(HALF - TC, P)
    MT, MP = divmod(N - S, P)
    SC = S - P * (TB - 1 - MT)
    SM = S % P
    RING = 3
    STAGES = 12
    SLOTS = TILES + STAGES
    OLD, COMP, NORM, X2T, GATES, PLACES = 1, 2, 3, 5, 9, 10
    assert CT == HT - 1 and MT == TB - 2 and CP + TC == P and SC + MP == P and S == P + SM and MP + SM == P
    ident, _, _, _ = const
    w1_raw, w2_raw, expert_w_in, W1, W2 = weights
    ID, GATE = D, D + 1
    with ExitStack() as ctx:
        def sb(name, shape, dt=F32):
            return ctx.enter_context(nc.sbuf_tensor(name, shape, dt))

        def psum(name, shape):
            return ctx.enter_context(nc.psum_tensor(name, shape, F32))

        def sem(name):
            return ctx.enter_context(nc.semaphore(name))

        wp_raw = sb("wp_raw", [P, CC, D])
        wp_hi = sb("wp_hi", [P, CC, D], F32R)
        wp_lo = sb("wp_lo", [P, CC, D], F32R)
        bp_all = sb("bp_all", [P, D])
        eps = sb("eps", [P, 1])
        o_tok = sb("o_tok", [P, RING, HE])
        oT_hi = sb("oT_hi", [P, 2, CC, P], F32R)
        oT_lo = sb("oT_lo", [P, 2, CC, P], F32R)
        x1 = sb("x1", [P, TILES, D])
        stats = sb("stats1", [P, 2, 6])
        moments = sb("moments1", [P, 2, 2])
        root = sb("root1", [P, 2])
        scale = sb("scale1", [P, 2])

        cw = sb("cw", [P, RATE, KC, D])
        wg = sb("wg", [P, KC, EX])
        old_T = sb("old_T", [P, RATE, KC, P])
        x2T = sb("x2T", [P, 2, KC, P])
        stats2 = sb("stats2", [P, TB, 6])
        moments2 = sb("moments2", [P, TB, 2])
        root2 = sb("root2", [P, TB])
        scale2 = sb("scale2", [P, TB])
        before = sb("before", [P, P])
        ones = sb("ones", [P, P])
        expert = sb("expert", [P, EX])
        rank = sb("rank", [P, EX])
        trash = sb("trash", [P, TILES])
        logits = sb("logits", [P, TB, EX])
        top = sb("top", [P, TB])
        gates = sb("gates", [P, TB, EX])
        inv = sb("inv", [P, TB])
        gate = sb("gate", [P, TB])
        first = sb("first", [P, TB])
        mask = sb("mask", [P, TB, EX])
        tiles_before = sb("tiles_before", [P, TB, EX])
        work = sb("work", [P, TB, EX])
        place = sb("place", [P, TB])
        keep = sb("keep", [P, TB])
        row = sb("row", [P, TB])
        send_to = sb("send_to", [P, TILES], mybir.dt.uint32)

        oT_ps = [psum(f"oT_ps{i}", [P, CC, P]) for i in range(2)]
        y_ps = [psum(f"y1_ps{i}", [P, D]) for i in range(2)]
        wide_ps = psum("wide_ps", [P, 2, KC, P])
        thin_ps = psum("thin_ps", [P, BANK])
        old_ps = wide_ps[:, :, :, :].rearrange("p a k n -> p (a k n)").rearrange("p (k n) -> p k n", k=KC)
        logits_ps = thin_ps[:, 0:TB * EX].rearrange("p (t e) -> p t e", t=TB)

        wp_in = sem("wp_in")
        bp_in = sem("bp_in")
        consts_set = sem("consts_set")
        wp_hi_done = sem("wp_hi_done")
        wp_split = sem("wp_split")
        o_in = [sem(f"o_in{i}") for i in range(RING)]
        x_in = [sem(f"x1_x_in{b}") for b in range(B)]
        xb_done = sem("xb_done")
        oT_ready = sem("oT_ready")
        oT_hi_done = sem("oT_hi_done")
        oT_lo_done = sem("oT_lo_done")
        y_ready = sem("y1_ready")
        z_done = sem("z1_done")
        stats_done = sem("stats1_done")
        moments_done = sem("moments1_done")
        root_done = sem("root1_done")
        scale_done = sem("scale1_done")
        x1_done = sem("x1_done")

        weights_in = sem("weights_in")
        moved = [sem(f"moved{b}") for b in range(B)]
        new_in = [sem(f"new_in{b}") for b in range(B)]
        old_cleared = sem("old_cleared")
        old_ready = sem("old_ready")
        old_placed = sem("old_placed")
        comp_ready = sem("comp_ready")
        sum_done = sem("sum_done")
        comp_added = sem("comp_added")
        stats2_done = sem("stats2_done")
        moments2_done = sem("moments2_done")
        root2_done = sem("root2_done")
        x2_done = sem("x2_done")
        x2T_ready = sem("x2T_ready")
        x2T_done = sem("x2T_done")
        logits_ready = sem("logits_ready")
        shifted = sem("shifted")
        exp_done = sem("exp_done")
        mask_done = sem("mask_done")
        count_ready = sem("count_ready")
        count_read = sem("count_read")
        dve_step = sem("dve_step")
        rows_ready = sem("rows_ready")
        sent = sem("sent")
        block = ctx.enter_context(nc.Block())

        x1_b = x1[:, :, :].rearrange("p (b t) d -> p b t d", b=B)
        x2_b = x2[:, :, 0:D].rearrange("p (b t) d -> p b t d", b=B)
        MOVES = 4
        NEW = 3
        CONSTS = 8

        def stages(s):
            return [(b, s - TB * (b + 1)) for b in range(B) if 0 <= s - TB * (b + 1) < STAGES]

        @block.sync
        def _(sp):
            o_rows = o_dram.rearrange("b n c -> (b n) c")

            def load_o(s):
                wait(sp, oT_ready, s - RING + 1)
                sp.dma_start(o_tok[:, s % RING, :], o_rows[s * P:(s + 1) * P, :]).then_inc(o_in[s % RING], 16)

            load_o(0)
            load_o(1)
            wp_rows = Wp.rearrange("(e c h) n -> h e c n", h=2, c=CC)
            for h in range(2):
                sp.dma_start(wp_raw[h * (P // 2):(h + 1) * (P // 2), :, :], wp_rows[h]).then_inc(wp_in, 16)
            for b in range(B):
                sp.dma_start(x1_b[:, b], x[b].rearrange("(t p) d -> p t d", p=P)).then_inc(x_in[b], 16)
                if b == 0:
                    sp.dma_start(bp_all[:, :], bp.rearrange("(a n) -> a n", a=1).broadcast_to([P, D])
                                 ).then_inc(bp_in, 16)
                    load_o(2)
            sp.dma_start(cw[:, :, :, :], conv_w.rearrange("r (k p) d -> p r k d", p=P)).then_inc(weights_in, 16)
            sp.dma_start(wg[:, :, :], Wg.rearrange("(k p) e -> p k e", p=P)).then_inc(weights_in, 16)
            for b in range(B):
                sp.dma_start(x2_b[CP:P, b, CT, :], conv_b.rearrange("(a n) -> a n", a=1).broadcast_to([TC, D])
                             ).then_inc(new_in[b], 16)
                sp.dma_start(x2_b[MP:P, b, MT, :], ctx_in[b, 0:SC, :]).then_inc(new_in[b], 16)
                sp.dma_start(x2_b[:, b, TB - 1, :], ctx_in[b, SC:S, :]).then_inc(new_in[b], 16)
            for s in range(SLOTS):
                if s + RING < TILES:
                    load_o(s + RING)
                for b, k in stages(s):
                    if k == COMP:
                        sp.wait_ge(x1_done, TB * (b + 1))
                        for dst, src in (((slice(0, P - TC), 0, HT), (slice(TC, P), 0)),
                                         ((slice(P - TC, P), 0, HT - 1), (slice(0, TC), 1)),
                                         ((slice(0, P - SM), HT, TB - 1), (slice(SM, P), HT + 1)),
                                         ((slice(P - SM, P), HT, TB - 2), (slice(0, SM), HT + 2))):
                            n = dst[2] - dst[1]
                            sp.dma_start(x2_b[dst[0], b, dst[1]:dst[2], :], x1_b[src[0], b, src[1]:src[1] + n, :]
                                         ).then_inc(moved[b], 16)
            sp.dma_start(w1_raw[:, :, :], W1[0].rearrange("(k p) h -> p k h", p=P)).then_inc(expert_w_in[0], 16)
            sp.dma_start(w2_raw[:, :, :], W2[0].rearrange("(c p) d -> p c d", p=P)).then_inc(expert_w_in[1], 16)

        @block.gpsimd
        def _(pool):
            pool.memset(eps[:, :], 1e-5).then_inc(consts_set, 1)
            pool.memset(ones[:, :], 1.0).then_inc(consts_set, 1)
            pool.wait_ge(wp_hi_done, 1)
            pool.tensor_tensor(wp_lo[:, :, :], wp_raw[:, :, :], wp_hi[:, :, :].bitcast(F32),
                               ALU.subtract).then_inc(wp_split, 1)
            pool.wait_ge(bp_in, 16)
            bias = bp_all[:, :].rearrange("p (a d) -> p a d", a=1).broadcast_to([P, TB, D])
            for b in range(B):
                pool.wait_ge(x_in[b], 16)
                pool.tensor_tensor(x1_b[:, b], x1_b[:, b], bias, ALU.add).then_inc(xb_done, 1)
                if b == 0:
                    pool.memset(old_T[:, :, :, :], 0.0).then_inc(old_cleared, 1)
                    pool.iota(expert[:, :], pattern=[[1, EX]], base=0, channel_multiplier=0,
                              allow_small_or_imprecise_dtypes=True).then_inc(consts_set, 1)
                    pool.iota(rank[:, :], pattern=[[-1, EX]], base=EX, channel_multiplier=0,
                              allow_small_or_imprecise_dtypes=True).then_inc(consts_set, 1)
                    pool.iota(trash[:, :], pattern=[[P, TILES]], base=ROWS, channel_multiplier=1,
                              allow_small_or_imprecise_dtypes=True).then_inc(consts_set, 1)
                    pool.iota(x2[:, :, ID:ID + 1].bitcast(mybir.dt.uint32), pattern=[[P, TILES]], base=0,
                              channel_multiplier=1).then_inc(consts_set, 1)
                    pool.memset(x2[:, :, GATE + 1:], 0.0).then_inc(consts_set, 1)
                    pool.wait_ge(consts_set, 2)
                    pool.affine_select(out=before[:, :], in_=ones[:, :], compare_op=ALU.is_gt, fill=0.0,
                                       base=0, pattern=[[1, P]], channel_multiplier=-1).then_inc(consts_set, 1)
            for b in range(B):
                pool.wait_ge(new_in[b], 16 * NEW)
                pool.wait_ge(moved[b], 16 * MOVES)
                pool.tensor_tensor(x2_b[:, b], x2_b[:, b], x1_b[:, b], ALU.add).then_inc(sum_done, 1)
                for c in ([b - 1] if b > 0 else []) + ([b] if b == B - 1 else []):
                    pool.wait_ge(rows_ready, c + 1)
                    for t in range(c * TB, (c + 1) * TB):
                        pool.indirect_dma_start(
                            out=xe_dram[:, :], out_offset=bass.IndirectOffsetOnAxis(ap=send_to[:, t:t + 1], axis=0),
                            in_=x2[:, t, :], in_offset=None).then_inc(sent, 16)
            pool.wait_ge(sent, 16 * TILES)

        @block.tensor
        def _(pe):
            def transposes(b, k):
                if k == OLD:
                    pe.wait_ge(x1_done, TB * b + HT + 2)
                    wait(pe, x2T_done, TB // 2 * b)
                    for kc in range(KC):
                        for t in range(2):
                            last = pe.transpose(old_ps[:, kc, t * P:(t + 1) * P],
                                                x1_b[:, b, HT + t, kc * P:(kc + 1) * P], ident[:, :])
                    last.then_inc(old_ready, 1)
                if k == COMP:
                    pe.wait_ge(weights_in, 32)
                    pe.wait_ge(old_placed, b + 1)
                    wait(pe, count_read, b)
                    for r in range(RATE):
                        for kc in range(KC):
                            last = pe.matmul(thin_ps[:, 0:D], old_T[:, r, kc, :], cw[:, r, kc, :],
                                             start=(r == 0 and kc == 0), stop=(r == RATE - 1 and kc == KC - 1))
                    last.then_inc(comp_ready, 1)
                i = k - X2T
                if 0 <= i < TB // 2:
                    pe.wait_ge(x2_done, TB * b + 2 * i + 2)
                    wait(pe, x2T_done, TB // 2 * b + i)
                    for t in range(2):
                        for kc in range(KC):
                            last = pe.transpose(wide_ps[:, t, kc, :],
                                                x2_b[:, b, 2 * i + t, kc * P:(kc + 1) * P], ident[:, :])
                    last.then_inc(x2T_ready, 1)

            def products(b, k):
                i = k - X2T
                if 0 <= i < TB // 2:
                    pe.wait_ge(x2T_done, TB // 2 * b + i + 1)
                    pe.wait_ge(comp_added, b + 1)
                    for t in range(2):
                        for kc in range(KC):
                            last = pe.matmul(logits_ps[:, 2 * i + t, :], x2T[:, t, kc, :], wg[:, kc, :],
                                             start=(kc == 0), stop=(kc == KC - 1))
                    last.then_inc(logits_ready, 1)
                if k == GATES:
                    pe.wait_ge(consts_set, CONSTS)
                    pe.wait_ge(mask_done, b + 1)
                    pe.matmul(logits_ps, before[:, :], mask[:, :, :], start=True, stop=False)
                    pe.matmul(logits_ps, ones[:, :], tiles_before[:, :, :], start=False,
                              stop=True).then_inc(count_ready, 1)

            for s in range(SLOTS):
                if s < TILES:
                    pe.wait_ge(o_in[s % RING], 16 * (s // RING + 1))
                    wait(pe, oT_lo_done, s - 1)
                    for c in range(CC):
                        last = pe.transpose(oT_ps[s % 2][:, c, :], o_tok[:, s % RING, c * P:(c + 1) * P],
                                            ident[:, :])
                    last.then_inc(oT_ready, 1)
                for b, k in stages(s):
                    transposes(b, k)
                if 1 <= s <= TILES:
                    if s == 1:
                        pe.wait_ge(wp_split, 1)
                    par = (s - 1) % 2
                    pe.wait_ge(oT_lo_done, s)
                    wait(pe, z_done, s - 2)
                    for n, (a, w) in enumerate(((oT_hi, wp_hi), (oT_hi, wp_lo), (oT_lo, wp_hi))):
                        for c in range(CC):
                            last = pe.matmul(y_ps[par][:, :], a[:, par, c, :], w[:, c, :],
                                             start=(n == 0 and c == 0), stop=(n == 2 and c == CC - 1))
                    last.then_inc(y_ready, 1)
                for b, k in stages(s):
                    products(b, k)

        @block.scalar
        def _(act):
            act.wait_ge(wp_in, 32)
            act.activation(wp_hi[:, :, :], wp_raw[:, :, :], ACT.Copy).then_inc(wp_hi_done, 1)
            act.wait_ge(consts_set, 1)

            def stage(b, k):
                if k == NORM:
                    act.wait_ge(moments2_done, TB * (b + 1))
                    act.activation(root2[:, :], moments2[:, :, 1], ACT.Sqrt, bias=eps[:, :]).then_inc(root2_done, 1)
                i = k - X2T
                if 0 <= i < TB // 2:
                    n = TB // 2 * b + i
                    act.wait_ge(x2T_ready, n + 1)
                    wait(act, logits_ready, n)
                    act.activation(x2T[:, :, :, :], wide_ps[:, :, :, :], ACT.Copy).then_inc(x2T_done, 1)
                if k == GATES:
                    act.wait_ge(shifted, b + 1)
                    act.activation(gates[:, :, :], logits[:, :, :], ACT.Exp).then_inc(exp_done, 1)

            for s in range(SLOTS):
                if s < TILES:
                    act.wait_ge(oT_ready, s + 1)
                    wait(act, y_ready, s - 1)
                    act.activation(oT_hi[:, s % 2], oT_ps[s % 2][:, :, :], ACT.Copy).then_inc(oT_hi_done, 1)
                for b, k in stages(s):
                    stage(b, k)
                if 1 <= s <= TILES:
                    par = (s - 1) % 2
                    act.wait_ge(moments_done, s)
                    act.activation(root[:, par:par + 1], moments[:, par, 1:2], ACT.Sqrt,
                                   bias=eps[:, :]).then_inc(root_done, 1)

        @block.vector
        def _(dve):
            steps = [0]

            def step(ins):
                steps[0] += 1
                ins.then_inc(dve_step, 1)
                dve.wait_ge(dve_step, steps[0])

            def spread(a):
                return a[:, :].rearrange("p (t a) -> p t a", a=1).broadcast_to([P, TB, EX])

            def over_tokens(a):
                return a[:, :].rearrange("p (a e) -> p a e", a=1).broadcast_to([P, TB, EX])

            def place_old(b):
                dve.wait_ge(old_ready, b + 1)
                dve.wait_ge(old_cleared, 1)
                wait(dve, comp_ready, b)
                for kc in range(KC):
                    last = dve.tensor_copy(old_T[:, :, kc, CP:P],
                                           old_ps[:, kc, 0:TC * RATE].rearrange("p (t r) -> p r t", r=RATE))
                last.then_inc(old_placed, 1)

            def norm_stats(b):
                dve.wait_ge(sum_done, b + 1)
                dve.wait_ge(comp_ready, b + 1)
                dve.tensor_tensor(x2_b[:, b, CT, :], thin_ps[:, 0:D], x2_b[:, b, CT, :], ALU.add
                                  ).then_inc(comp_added, 1)
                wait(dve, x2_done, TB * b)
                for t in [t for t in range(TB) if t != CT] + [CT]:
                    if t == CT:
                        dve.wait_ge(comp_added, b + 1)
                    dve.bn_stats(stats2[:, t, :], x2_b[:, b, t, :]).then_inc(stats2_done, 1)
                dve.wait_ge(stats2_done, TB * (b + 1))
                for t in range(TB):
                    dve.bn_aggr(moments2[:, t, :], stats2[:, t, :]).then_inc(moments2_done, 1)

            def norm(b):
                dve.wait_ge(root2_done, b + 1)
                step(dve.reciprocal(scale2[:, :], root2[:, :]))
                for t in range(TB):
                    dve.tensor_scalar(x2_b[:, b, t, :], x2_b[:, b, t, :], moments2[:, t, 0:1],
                                      scale2[:, t:t + 1], ALU.subtract, ALU.mult).then_inc(x2_done, 1)

            def choose(b):
                dve.wait_ge(logits_ready, TB // 2 * (b + 1))
                step(dve.tensor_reduce(top[:, :], logits_ps, AX.X, ALU.max))
                dve.tensor_tensor(logits[:, :, :], logits_ps, spread(top), ALU.subtract).then_inc(shifted, 1)
                dve.wait_ge(exp_done, b + 1)
                step(dve.tensor_reduce(top[:, :], gates[:, :, :], AX.X, ALU.add))
                step(dve.reciprocal(inv[:, :], top[:, :]))
                step(dve.tensor_tensor(gates[:, :, :], gates[:, :, :], spread(inv), ALU.mult))
                step(dve.tensor_reduce(gate[:, :], gates[:, :, :], AX.X, ALU.max))
                step(dve.tensor_tensor(work[:, :, :], gates[:, :, :], spread(gate), ALU.is_ge))
                dve.wait_ge(consts_set, CONSTS)
                step(dve.tensor_tensor(work[:, :, :], work[:, :, :], over_tokens(rank), ALU.mult))
                step(dve.tensor_reduce(first[:, :], work[:, :, :], AX.X, ALU.max))
                step(dve.tensor_tensor(mask[:, :, :], over_tokens(rank), spread(first), ALU.is_equal))
                step(dve.memset(tiles_before[:, 0, :], 0.0))
                for t in range(1, TB):
                    ins = dve.tensor_tensor(tiles_before[:, t, :], tiles_before[:, t - 1, :], mask[:, t - 1, :],
                                            ALU.add)
                    if t < TB - 1:
                        step(ins)
                ins.then_inc(mask_done, 1)

            def find_rows(b):
                tiles = slice(b * TB, (b + 1) * TB)
                dve.wait_ge(count_ready, b + 1)
                dve.tensor_tensor(work[:, :, :], logits_ps, mask[:, :, :], ALU.mult).then_inc(count_read, 1)
                dve.wait_ge(count_read, b + 1)
                step(dve.tensor_reduce(place[:, :], work[:, :, :], AX.X, ALU.add))
                step(dve.tensor_tensor(work[:, :, :], mask[:, :, :], over_tokens(expert), ALU.mult))
                step(dve.tensor_reduce(row[:, :], work[:, :, :], AX.X, ALU.add))
                step(dve.tensor_scalar(keep[:, :], place[:, :], float(CAP), None, ALU.is_lt))
                step(dve.tensor_scalar(row[:, :], row[:, :], float(B * CAP), float(b * CAP), ALU.mult, ALU.add))
                step(dve.tensor_tensor(row[:, :], row[:, :], place[:, :], ALU.add))
                step(dve.tensor_tensor(row[:, :], row[:, :], trash[:, tiles], ALU.subtract))
                step(dve.tensor_tensor(row[:, :], row[:, :], keep[:, :], ALU.mult))
                step(dve.tensor_tensor(row[:, :], row[:, :], trash[:, tiles], ALU.add))
                step(dve.tensor_copy(send_to[:, tiles], row[:, :]))
                dve.tensor_copy(x2[:, tiles, GATE:GATE + 1], gate[:, :].rearrange("p (t a) -> p t a", a=1)
                                ).then_inc(rows_ready, 1)

            for s in range(SLOTS):
                for b, k in stages(s):
                    if k == PLACES:
                        find_rows(b)
                if s < TILES:
                    dve.wait_ge(oT_hi_done, s + 1)
                    dve.tensor_tensor(oT_lo[:, s % 2], oT_ps[s % 2][:, :, :], oT_hi[:, s % 2].bitcast(F32),
                                      ALU.subtract).then_inc(oT_lo_done, 1)
                if 2 <= s < TILES + 2:
                    par = s % 2
                    dve.wait_ge(root_done, s - 1)
                    dve.reciprocal(scale[:, par:par + 1], root[:, par:par + 1]).then_inc(scale_done, 1)
                    dve.wait_ge(scale_done, s - 1)
                    dve.tensor_scalar(x1[:, s - 2, :], x1[:, s - 2, :], moments[:, par, 0:1],
                                      scale[:, par:par + 1], ALU.subtract, ALU.mult).then_inc(x1_done, 1)
                for b, k in stages(s):
                    if k == OLD:
                        place_old(b)
                    elif k == NORM:
                        norm_stats(b)
                    elif k == NORM + 1:
                        norm(b)
                    elif k == GATES:
                        choose(b)
                if 1 <= s <= TILES:
                    prev = s - 1
                    par = prev % 2
                    dve.wait_ge(y_ready, s)
                    dve.wait_ge(xb_done, prev // TB + 1)
                    dve.tensor_tensor(x1[:, prev, :], y_ps[par][:, :], x1[:, prev, :], ALU.add).then_inc(z_done, 1)
                    dve.wait_ge(z_done, s)
                    dve.bn_stats(stats[:, par, :], x1[:, prev, :]).then_inc(stats_done, 1)
                    dve.wait_ge(stats_done, s)
                    wait(dve, x1_done, s - 2)
                    dve.bn_aggr(moments[:, par, :], stats[:, par, :]).then_inc(moments_done, 1)


def build_experts(nc, W1, W2, w1_raw, w2_raw, w_in, xe_dram, y_dram, x2, out, const):
    EX, D, HID = W1.shape
    B, N, _ = out.shape
    TB = N // P
    TILES = B * TB
    KC = D // P
    HC = HID // P
    ROWL = xe_dram.shape[1]
    ID, GATE = D, D + 1
    R = B * N // EX
    RT = R // P
    assert R == BANK
    ident = const[0]
    with ExitStack() as ctx:
        def sb(name, shape, dt=F32):
            return ctx.enter_context(nc.sbuf_tensor(name, shape, dt))

        def sem(name):
            return ctx.enter_context(nc.semaphore(name))

        def split_pair(name, shape):
            return sb(name + "_hi", shape, F32R), sb(name + "_lo", shape, F32R)

        w1 = split_pair("w1", [P, KC, HID])
        w2 = split_pair("w2", [P, HC, D])
        xe = sb("xe", [P, 2, RT, ROWL])
        xeT = split_pair("xeT", [P, KC, R])
        h_act = sb("h_act", [P, 2, R])
        h = split_pair("h", [P, HC, R])
        y = sb("y", [P, 2, RT, D])
        y_tok = sb("y_tok", [P, B, TB, D])
        eps = sb("eps3", [P, 1])
        stats = sb("stats3", [P, TILES, 6])
        moments = sb("moments3", [P, TILES, 2])
        root = sb("root3", [P, TILES])
        scale = sb("scale3", [P, TILES])
        shift = sb("shift3", [P, TILES])
        xeT_ps = ctx.enter_context(nc.psum_tensor("xeT_ps", [P, KC, R], F32))
        h_ps = [ctx.enter_context(nc.psum_tensor(f"h_ps{i}", [P, R], F32)) for i in range(2)]
        y_ps = [ctx.enter_context(nc.psum_tensor(f"y_ps{i}", [P, D], F32)) for i in range(RT)]

        w1_hi_done = sem("w1_hi_done")
        w1_split = sem("w1_split")
        w2_hi_done = sem("w2_hi_done")
        w2_split = sem("w2_split")
        xe_in = [sem(f"xe_in{i}") for i in range(2)]
        xeT_ready = sem("xeT_ready")
        xeT_hi_done = sem("xeT_hi_done")
        xeT_done = sem("xeT_done")
        h_ready = sem("h_ready")
        gelu_done = sem("gelu_done")
        h_hi_done = sem("h_hi_done")
        h_done = sem("h_done")
        y_ready = sem("y_ready")
        y_done = sem("y_done")
        y_sent = sem("y_sent")
        y_tok_in = [sem(f"y_tok_in{b}") for b in range(B)]
        eps_set = sem("eps3_set")
        z_done = [sem(f"z3_done{b}") for b in range(B)]
        stats_done = sem("stats3_done")
        moments_done = sem("moments3_done")
        root_done = sem("root3_done")
        scale_done = sem("scale3_done")
        shift_done = sem("shift3_done")
        out_done = sem("out_done")
        out_stored = sem("out_stored")
        block = ctx.enter_context(nc.Block())

        x2_b = x2[:, :, 0:D].rearrange("p (b t) d -> p b t d", b=B)
        LAST = HC - 1
        products = ((0, 0), (0, 1), (1, 0))

        @block.sync
        def _(sp):
            def load_xe(e):
                wait(sp, y_done, RT * (e - 1))
                wait(sp, y_sent, 16 * RT * (e - 1))
                sp.dma_start(xe[:, e % 2], xe_dram[e * R:(e + 1) * R, :].rearrange("(t p) d -> p t d", p=P)
                             ).then_inc(xe_in[e % 2], 16)

            load_xe(0)
            load_xe(1)
            for e in range(1, EX):
                sp.wait_ge(w1_split, e)
                sp.dma_start(w1_raw[:, :, :], W1[e].rearrange("(k p) h -> p k h", p=P)).then_inc(w_in[0], 16)
                sp.wait_ge(w2_split, e)
                sp.dma_start(w2_raw[:, :, :], W2[e].rearrange("(c p) d -> p c d", p=P)).then_inc(w_in[1], 16)
                if e + 1 < EX:
                    load_xe(e + 1)
            sp.wait_ge(y_sent, 16 * RT * EX)
            for b in range(B):
                sp.dma_start(y_tok[:, b], y_dram[b * N:(b + 1) * N, :].rearrange("(t p) d -> p t d", p=P)
                             ).then_inc(y_tok_in[b], 16)
            for b in range(B):
                sp.wait_ge(out_done, TB * (b + 1))
                sp.dma_start(out[b].rearrange("(t p) d -> p t d", p=P), y_tok[:, b]).then_inc(out_stored, 16)
            sp.wait_ge(out_stored, 16 * B)

        @block.gpsimd
        def _(pool):
            def split_w1(e):
                pool.wait_ge(w1_hi_done, e + 1)
                wait(pool, h_ready, HC * e)
                pool.tensor_tensor(w1[1][:, :, :], w1_raw[:, :, :], w1[0][:, :, :].bitcast(F32),
                                   ALU.subtract).then_inc(w1_split, 1)

            def split_w2(e):
                pool.wait_ge(w2_hi_done, e + 1)
                wait(pool, y_ready, RT * e)
                pool.tensor_tensor(w2[1][:, :, :], w2_raw[:, :, :], w2[0][:, :, :].bitcast(F32),
                                   ALU.subtract).then_inc(w2_split, 1)

            def send(e):
                for t in range(RT):
                    pool.wait_ge(y_done, RT * e + t + 1)
                    token = xe[:, e % 2, t, ID:ID + 1].bitcast(mybir.dt.uint32)
                    pool.indirect_dma_start(out=y_dram[:, :],
                                            out_offset=bass.IndirectOffsetOnAxis(ap=token, axis=0),
                                            in_=y[:, e % 2, t, :], in_offset=None).then_inc(y_sent, 16)

            for e in range(EX):
                if e == 0:
                    split_w1(0)
                split_w2(e)
                if e + 1 < EX:
                    split_w1(e + 1)
                send(e)
            for b in range(1, B, 2):
                pool.wait_ge(y_tok_in[b], 16)
                pool.tensor_tensor(y_tok[:, b], y_tok[:, b], x2_b[:, b], ALU.add).then_inc(z_done[b], 1)

        @block.tensor
        def _(pe):
            def transpose_rows(e):
                pe.wait_ge(xe_in[e % 2], 16 * (e // 2 + 1))
                wait(pe, xeT_done, e)
                for k in range(KC):
                    for t in range(RT):
                        last = pe.transpose(xeT_ps[:, k, t * P:(t + 1) * P], xe[:, e % 2, t, k * P:(k + 1) * P],
                                            ident[:, :])
                last.then_inc(xeT_ready, 1)

            transpose_rows(0)
            for e in range(EX):
                pe.wait_ge(xeT_done, e + 1)
                pe.wait_ge(w1_split, e + 1)
                for c in range(HC):
                    n = e * HC + c
                    wait(pe, gelu_done, n - 1)
                    for i, (a, b) in enumerate(products):
                        for k in range(KC):
                            last = pe.matmul(h_ps[n % 2][:, :], w1[a][:, k, c * P:(c + 1) * P], xeT[b][:, k, :],
                                             start=(i == 0 and k == 0), stop=(i == 2 and k == KC - 1))
                    last.then_inc(h_ready, 1)
                if e + 1 < EX:
                    transpose_rows(e + 1)
                pe.wait_ge(w2_split, e + 1)
                wait(pe, y_done, RT * e)
                for chunks in (range(LAST), range(LAST, HC)):
                    pe.wait_ge(h_done, HC * e + chunks[-1] + 1)
                    for t in range(RT):
                        for c in chunks:
                            for i, (a, b) in enumerate(products):
                                last = pe.matmul(y_ps[t][:, :], h[a][:, c, t * P:(t + 1) * P], w2[b][:, c, :],
                                                 start=(c == 0 and i == 0), stop=(c == LAST and i == 2))
                        if chunks[-1] == LAST:
                            last.then_inc(y_ready, 1)

        @block.scalar
        def _(act):
            def split_w1(e):
                act.wait_ge(w_in[0], 16 * (e + 1))
                wait(act, h_ready, HC * e)
                act.activation(w1[0][:, :, :], w1_raw[:, :, :], ACT.Copy).then_inc(w1_hi_done, 1)

            def split_w2(e):
                act.wait_ge(w_in[1], 16 * (e + 1))
                wait(act, y_ready, RT * e)
                act.activation(w2[0][:, :, :], w2_raw[:, :, :], ACT.Copy).then_inc(w2_hi_done, 1)

            def rows_high(e):
                act.wait_ge(xeT_ready, e + 1)
                wait(act, h_ready, HC * e)
                act.activation(xeT[0][:, :, :], xeT_ps[:, :, :], ACT.Copy).then_inc(xeT_hi_done, 1)

            split_w1(0)
            rows_high(0)
            split_w2(0)
            for e in range(EX):
                for c in range(HC):
                    n = e * HC + c
                    act.wait_ge(h_ready, n + 1)
                    wait(act, h_done, n - 1)
                    act.activation(h_act[:, n % 2, :], h_ps[n % 2][:, :], ACT.Gelu_apprx_tanh).then_inc(gelu_done, 1)
                if e + 1 < EX:
                    rows_high(e + 1)
                    split_w1(e + 1)
                for t in range(RT):
                    act.wait_ge(y_ready, e * RT + t + 1)
                    wait(act, y_sent, 16 * RT * (e - 1))
                    act.activation(y[:, e % 2, t, :], y_ps[t][:, :], ACT.Copy,
                                   scale=xe[:, e % 2, t, GATE:GATE + 1]).then_inc(y_done, 1)
                if e + 1 < EX:
                    split_w2(e + 1)
            act.wait_ge(eps_set, 1)
            for b in range(B):
                tiles = slice(b * TB, (b + 1) * TB)
                act.wait_ge(moments_done, TB * (b + 1))
                act.activation(root[:, tiles], moments[:, tiles, 1], ACT.Sqrt, bias=eps[:, :]).then_inc(root_done, 1)
                act.wait_ge(shift_done, b + 1)
                for t in range(b * TB, (b + 1) * TB):
                    act.activation(y_tok[:, b, t % TB, :], y_tok[:, b, t % TB, :], ACT.Identity,
                                   scale=scale[:, t:t + 1], bias=shift[:, t:t + 1]).then_inc(out_done, 1)

        @block.vector
        def _(dve):
            dve.memset(eps[:, :], 1e-5).then_inc(eps_set, 1)

            def rows_low(e):
                dve.wait_ge(xeT_hi_done, e + 1)
                dve.tensor_tensor(xeT[1][:, :, :], xeT_ps[:, :, :], xeT[0][:, :, :].bitcast(F32),
                                  ALU.subtract).then_inc(xeT_done, 1)

            rows_low(0)
            for e in range(EX):
                wait(dve, y_ready, RT * e)
                for c in range(HC):
                    n = e * HC + c
                    dve.wait_ge(gelu_done, n + 1)
                    dve.tensor_copy(h[0][:, c, :], h_act[:, n % 2, :]).then_inc(h_hi_done, 1)
                    dve.wait_ge(h_hi_done, n + 1)
                    dve.tensor_tensor(h[1][:, c, :], h_act[:, n % 2, :], h[0][:, c, :].bitcast(F32),
                                      ALU.subtract).then_inc(h_done, 1)
                if e + 1 < EX:
                    rows_low(e + 1)
            for b in range(B):
                if b % 2 == 0:
                    dve.wait_ge(y_tok_in[b], 16)
                    dve.tensor_tensor(y_tok[:, b], y_tok[:, b], x2_b[:, b], ALU.add).then_inc(z_done[b], 1)
                dve.wait_ge(z_done[b], 1)
                tiles = slice(b * TB, (b + 1) * TB)
                for t in range(b * TB, (b + 1) * TB):
                    dve.bn_stats(stats[:, t, :], y_tok[:, b, t % TB, :]).then_inc(stats_done, 1)
                dve.wait_ge(stats_done, TB * (b + 1))
                for t in range(b * TB, (b + 1) * TB):
                    dve.bn_aggr(moments[:, t, :], stats[:, t, :]).then_inc(moments_done, 1)
                dve.wait_ge(root_done, b + 1)
                dve.reciprocal(scale[:, tiles], root[:, tiles]).then_inc(scale_done, 1)
                dve.wait_ge(scale_done, b + 1)
                dve.scalar_tensor_tensor(out=shift[:, tiles], in0=moments[:, tiles, 0], scalar=-1.0,
                                         in1=scale[:, tiles], op0=ALU.mult, op1=ALU.mult).then_inc(shift_done, 1)


def build(nc, x, ctx_in, Wq, Wk, Wv, Wp, bp, conv_w, conv_b, Wg, W1, W2, out):
    B, N, D = x.shape
    H, _, E = Wq.shape
    HID = W1.shape[2]
    TILES = B * N // P
    ROWL = D + 4
    xT_parts = nc.dram_tensor("xT_parts", [B, P, HILO, D // P, N], F32, kind="Internal").ap()
    o_dram = nc.dram_tensor("o_tokens", [B, N, H * E], F32, kind="Internal").ap()
    xe_dram = nc.dram_tensor("expert_rows", [2 * B * N, ROWL], F32, kind="Internal").ap()
    y_dram = nc.dram_tensor("expert_outputs", [2 * B * N, D], F32, kind="Internal").ap()
    with ExitStack() as ctx:
        const = build_constants(nc, ctx)
        build_transpose_x(nc, x, xT_parts, const)
        build_attention(nc, xT_parts, Wq, Wk, Wv, o_dram, xe_dram, y_dram, const)
        x2 = ctx.enter_context(nc.sbuf_tensor("x2", [P, TILES, ROWL], F32))
        w1_raw = ctx.enter_context(nc.sbuf_tensor("w1_raw", [P, D // P, HID], F32))
        w2_raw = ctx.enter_context(nc.sbuf_tensor("w2_raw", [P, HID // P, D], F32))
        w_in = [ctx.enter_context(nc.semaphore(f"expert_w{i}_in")) for i in (1, 2)]
        build_project_route(nc, o_dram, x, Wp, bp, ctx_in, conv_w, conv_b, Wg, x2, xe_dram,
                            (w1_raw, w2_raw, w_in, W1, W2), const)
        build_experts(nc, W1, W2, w1_raw, w2_raw, w_in, xe_dram, y_dram, x2, out, const)


_INS = ['x', 'ctx_1024', 'L0_attn_Wq', 'L0_attn_Wk', 'L0_attn_Wv', 'L0_attn_Wp', 'L0_attn_bp',
        'L0_xattn_conv_w', 'L0_xattn_conv_b', 'L0_ffn_Wg', 'L0_ffn_W1', 'L0_ffn_W2']


def kernel(**inputs):
    import numpy as _np
    import concourse.bacc as _bacc
    from concourse import mybir as _mybir
    from concourse.bass_utils import run_bass_kernel_spmd as _run

    nc = _bacc.Bacc("TRN2", target_bir_lowering=False, num_devices=1)
    arrays, args = {}, []
    for name in _INS:
        a = _np.ascontiguousarray(inputs[name])
        arrays[f"in_{name}_dram"] = a
        args.append(nc.dram_tensor(f"in_{name}_dram", a.shape, _mybir.dt.from_np(a.dtype), kind="ExternalInput").ap())
    shape = inputs['x'].shape
    args.append(nc.dram_tensor("out_dram", shape, _mybir.dt.float32, kind="ExternalOutput").ap())
    build(nc, *args)
    r = _run(nc, [arrays], core_ids=[0])
    return r.results[0]["out_dram"]
```

```python
import concourse.bass as bass
from concourse import mybir
from contextlib import ExitStack

F32 = mybir.dt.float32
F32R = mybir.dt.float32r
ACT = mybir.ActivationFunctionType
ALU = mybir.AluOpType
AX = mybir.AxisListType

P = 128
BANK = 512
EARLY_BATCHES = 2
HILO = 2

QK_BITES = 4
V_BITES = 4
IT_BITES = 2 * QK_BITES + V_BITES
Q0, Q1, K0, K1 = range(QK_BITES)
BITE_SLOTS = ((1, 2, 3, 5), (1, 2, 3, 5, 6, 7, 9, 10))


def bites_to(pair, of_it):
    return IT_BITES * of_it + (QK_BITES if pair == 0 else IT_BITES)


def v_bites_to(of_it):
    return IT_BITES * of_it + QK_BITES + V_BITES


def wait(eng, sem, value):
    if isinstance(value, int) and value <= 0:
        return
    eng.wait_ge(sem, value)


def wait_then(eng, sem, value, passed):
    wait(eng, sem, value)
    if not isinstance(value, int):
        eng.sem_inc(passed, 1)


def build_constants(nc, ctx):
    ident = ctx.enter_context(nc.sbuf_tensor("ident", [P, P], F32))
    ident_zeroed = ctx.enter_context(nc.semaphore("ident_zeroed"))
    ident_ready = ctx.enter_context(nc.semaphore("ident_ready"))
    passed = ctx.enter_context(nc.semaphore("passed"))
    return ident, ident_zeroed, ident_ready, passed


def build_attention(nc, x, xT_parts, Wq, Wk, Wv, o_dram, const, xT, qk_hi, qk_lo, early):
    B, _, _, KC, N = xT_parts.shape
    H, D, E = Wq.shape
    TILES = N // P
    HP = TILES
    CH = BANK // P
    PAIR_T = 2 * TILES
    IT_T = 2 * PAIR_T
    ITS = B * H // 4
    PER_BATCH = H // 4
    PAIRS = 2 * ITS
    SCALE = E ** -0.5
    T_PAIRS = TILES // 2
    GROUPS = B * T_PAIRS
    ASM = 12
    assert 2 * E == P and HP == 8 and SCALE == 0.125 and B == 4
    ident, ident_zeroed, ident_ready, _ = const
    FIRST_WORK = [("x^T", g) for g in range(T_PAIRS)] + [("bite", k) for k in range(QK_BITES)]
    rest = iter(range(T_PAIRS, GROUPS))
    FIRST_WORK += [("x^T", next(rest)) for _ in range(T_PAIRS)]
    for k in range(V_BITES):
        FIRST_WORK.append(("bite", QK_BITES + k))
        FIRST_WORK += [("x^T", next(rest)) for _ in range((GROUPS - 2 * T_PAIRS) // V_BITES)]

    with ExitStack() as ctx:
        def sb(name, shape, dt=F32):
            return ctx.enter_context(nc.sbuf_tensor(name, shape, dt))

        def sem(name):
            return ctx.enter_context(nc.semaphore(name))

        w_raw = sb("w_raw", [P, 2, KC, 2 * E])
        w_hi = sb("w_hi", [P, 2, KC, 2 * E], F32R)
        w_lo = sb("w_lo", [P, 2, KC, 2 * E], F32R)
        wv_raw = sb("wv_raw", [P, KC, 4 * E])
        wv_hi = sb("wv_hi", [P, KC, 4 * E], F32R)
        wv_lo = sb("wv_lo", [P, KC, 4 * E], F32R)
        q_st = sb("q_st", [P, 2, 2, N], F32R)
        k_hh = sb("k_hh", [P, 2, 2, N], F32R)
        k_ll = sb("k_ll", [P, 2, 2, N], F32R)
        v_st = sb("v_st", [P, 3, HP, 2, HILO, E], F32R)
        probs = sb("probs", [P, 2, N])
        pT_hi = sb("pT_hi", [P, 2, HP, BANK], F32R)
        pT_lo = sb("pT_lo", [P, 2, HP, BANK], F32R)
        oT = sb("oT", [P, 2, BANK])
        o_sum = sb("o_sum", [P, CH, E])
        o_out = sb("o_out", [P, 2, TILES, 2 * E])
        neg_max = sb("neg_max", [P, 4])
        row_sum = sb("row_sum", [P, IT_T])
        inv_sum = sb("inv_sum", [P, CH])

        scores = [ctx.enter_context(nc.psum_tensor(f"scores{i}", [P, N], F32)) for i in range(2)]
        pT_ps = [ctx.enter_context(nc.psum_tensor(f"pT_ps{i}", [P, CH, P], F32)) for i in range(2)]
        av_ps = ctx.enter_context(nc.psum_tensor("av_ps", [P, BANK], F32))
        misc_ps = ctx.enter_context(nc.psum_tensor("misc_ps", [P, BANK], F32))

        x_tok = [buf.rearrange("p (t d) -> p t d", d=D)
                 for buf in (probs[:, :, :].rearrange("p a n -> p (a n)"),
                             o_out[:, :, :, :].rearrange("p a t e -> p (a t e)"))]

        def xT_place(b):
            if b == 0:
                return xT[:, 0], xT[:, 1]
            if b == B - 1:
                return q_st[:, 1], k_hh[:, 1]
            both = (pT_lo[:, b - 1].rearrange("p m n -> p (m n)")
                    .rearrange("p (a k n) -> p a k n", a=HILO, k=KC))
            return both[:, 0], both[:, 1]

        FIRST_BANKS = (misc_ps, av_ps)
        xT_ps = [bank[:, 0:BANK].rearrange("p (k n) -> p k n", k=KC) for bank in scores]

        x_in = [sem(f"x_in{b}") for b in range(B)]
        x_half_in = sem("x_half_in")
        x_transposed = sem("x_transposed")
        xT_high_done = sem("xT_high_done")
        xT_low_done = sem("xT_low_done")
        xT_stored = [sem(f"xT_stored{b}") for b in range(B)]
        w_loaded = sem("w_loaded")
        w_split_hi = sem("w_split_hi")
        w_split = sem("w_split")
        wv_loaded = sem("wv_loaded")
        wv_split_hi = sem("wv_split_hi")
        wv_split = sem("wv_split")
        v_moved = sem("v_moved")
        xT_loaded = sem("xT_loaded")
        qk_laid = sem("qk_laid")
        scores_ready = sem("scores_ready")
        max_ready = sem("max_ready")
        probs_ready = sem("probs_ready")
        pT_ready = sem("pT_ready")
        pT_hi_done = sem("pT_hi_done")
        pT_lo_done = sem("pT_lo_done")
        av_ready = sem("av_ready")
        oT_done = sem("oT_done")
        fold_ready = sem("fold_ready")
        fold_read = sem("fold_read")
        inv_done = sem("inv_done")
        o_done = sem("o_done")
        o_stored = sem("o_stored")
        bite_ready = sem("bite_ready")
        bite_hi_done = sem("bite_hi_done")
        bite_lo_done = sem("bite_lo_done")

        block = ctx.enter_context(nc.Block())

        def run(eng, slot):
            for tt in range(IT_T):
                slot(0, tt)
            with eng.Fori(1, ITS - 1) as it:
                for tt in range(IT_T):
                    slot(it, tt)
            for tt in range(IT_T):
                slot(ITS - 1, tt)
            for tt in range(IT_T, IT_T + CH + 2):
                slot(ITS - 1, tt)

        def exists(it, tt, ahead=0):
            return not (isinstance(it, int) and it == ITS - 1 and tt + ahead >= IT_T)

        def bite_of(pair, u):
            return BITE_SLOTS[pair].index(u) if u in BITE_SLOTS[pair] else None

        def bites_before(it, pair, u):
            return bites_to(pair, it) + (V_BITES if pair == 0 else 0) + sum(x < u for x in BITE_SLOTS[pair])

        def v_view(bank):
            return bank[:, :].rearrange("p (m a h e) -> p a m h e", m=2, a=2, h=2)

        def v_part(k, part):
            mts = slice(2 * (k - QK_BITES), 2 * (k - QK_BITES) + 2)
            return v_st[:, 0:2, mts, :, part, :]

        @block.sync
        def _(sp):
            def load_w(g, head):
                wait_then(sp, w_split, g, const[3])
                for i, w in enumerate((Wq, Wk)):
                    for k in range(KC):
                        sp.dma_start(w_raw[:, i, k, :].rearrange("p (h e) -> p h e", h=2),
                                     w[bass.ds(head, 2), k * P:(k + 1) * P, :].rearrange("h d e -> d h e")
                                     ).then_inc(w_loaded, 16)

            def load_wv(it, head):
                wait_then(sp, wv_split, it, const[3])
                for k in range(KC):
                    sp.dma_start(wv_raw[:, k, :].rearrange("p (h e) -> p h e", h=4),
                                 Wv[bass.ds(head, 4), k * P:(k + 1) * P, :].rearrange("h d e -> d h e")
                                 ).then_inc(wv_loaded, 16)

            def move_v(it):
                wait_then(sp, bite_lo_done, v_bites_to(it), const[3])
                wait(sp, av_ready, 8 * it)
                sp.dma_start(v_st[:, 2].rearrange("p m h a e -> p (m h a e)").bitcast(F32),
                             v_st[:, 1].rearrange("p m h a e -> p (m h a e)").bitcast(F32)).then_inc(v_moved, 16)

            def load_xT(batch):
                sp.dma_start(xT[:, :, :, :].rearrange("p a k n -> p (a k n)").bitcast(F32),
                             xT_parts[bass.ds(batch, 1)].rearrange("b p a k n -> p (b a k n)")
                             ).then_inc(xT_loaded, 16)

            def lay_out(g, par, bites):
                wait_then(sp, bite_lo_done, bites, const[3])
                wait(sp, scores_ready, PAIR_T * (g - 1))
                lay_out_q(par)
                lay_out_k(par)

            lo, hi = slice(0, E), slice(E, P)

            def lay_out_q(par):
                for h in range(2):
                    rows = slice(h * E, (h + 1) * E)
                    for dst, src in ((q_st[lo, par, h], qk_hi[rows, 0]), (q_st[hi, par, h], qk_lo[rows, 0])):
                        sp.dma_start(dst.bitcast(F32), src.bitcast(F32)).then_inc(qk_laid, 16)

            def lay_out_k(par):
                for h in range(2):
                    rows = slice(h * E, (h + 1) * E)
                    for buf, src in ((k_hh, qk_hi[rows, 1]), (k_ll, qk_lo[rows, 1])):
                        for half in (lo, hi):
                            sp.dma_start(buf[half, par, h].bitcast(F32), src.bitcast(F32)).then_inc(qk_laid, 16)

            def store_o(g, par, batch, head):
                wait_then(sp, o_done, 4 * (g + 1), const[3])
                sp.dma_start(o_dram[bass.ds(batch, 1), :, bass.ds(head * E, 2 * E)]
                             .rearrange("b (t p) n -> p (b t) n", p=P), o_out[:, par]).then_inc(o_stored, 16)

            def step(it, s):
                g = 2 * it + s
                final = isinstance(it, int) and it == ITS - 1
                if not final:
                    nxt = it + 1
                    load_w(g + 2, 4 * (nxt % PER_BATCH) + 2 * s)
                    if s == 0:
                        load_wv(nxt, 4 * (nxt % PER_BATCH))
                if not (isinstance(it, int) and g == 0):
                    if s == 0:
                        prev = it - 1
                        store_o(g - 1, 1, prev // PER_BATCH, 4 * (prev % PER_BATCH) + 2)
                    else:
                        store_o(g - 1, 0, it // PER_BATCH, 4 * (it % PER_BATCH))
                if s == 0:
                    move_v(it)
                if not (final and s == 1):
                    lay_out(g + 1, (s + 1) % 2, bites_to(1, it) if s == 0 else bites_to(0, it + 1))
                if s == 0 and not final:
                    wait_then(sp, bite_ready, bites_to(1, it), const[3])
                    load_xT(nxt // PER_BATCH)

            def store_xT(b):
                sp.wait_ge(xT_low_done, T_PAIRS * (b + 1))
                for part in range(HILO):
                    sp.dma_start(xT_parts[b, :, part], xT_place(b)[part].bitcast(F32)).then_inc(xT_stored[b], 16)

            def load_x(b):
                wait(sp, x_transposed, T_PAIRS * (b - 1))
                sp.dma_start(x_tok[b % 2], x[b].rearrange("(t p) d -> p t d", p=P)).then_inc(x_in[b], 16)

            half = TILES // 2
            x_rows = x[0].rearrange("(t p) d -> p t d", p=P)
            sp.dma_start(x_tok[0][:, 0:half], x_rows[:, 0:half]).then_inc(x_half_in, 16)
            load_w(0, 0)
            sp.dma_start(x_tok[0][:, half:], x_rows[:, half:]).then_inc(x_in[0], 16)
            load_wv(0, 0)
            load_x(1)
            load_w(1, 2)
            load_x(2)
            sp.wait_ge(bite_lo_done, K0)
            lay_out_q(0)
            sp.wait_ge(bite_lo_done, QK_BITES)
            lay_out_k(0)
            load_x(3)
            for b in (1, 2, 3, 0):
                store_xT(b)
            for b in range(B):
                sp.wait_ge(xT_stored[b], 16 * HILO)
            for s in range(2):
                step(0, s)
            with sp.Fori(1, ITS - 1) as it:
                for s in range(2):
                    step(it, s)
            for s in range(2):
                step(ITS - 1, s)
            sp.wait_ge(qk_laid, 16 * ASM * PAIRS)
            early.load_wp(sp)
            sp.wait_ge(o_stored, 16 * (PAIRS - 1))
            early.load_o(sp, 0)
            early.load_o(sp, 1)
            store_o(PAIRS - 1, 1, B - 1, H - 2)
            sp.wait_ge(o_stored, 16 * PAIRS)

        @block.gpsimd
        def _(pool):
            def split_w(g, read):
                wait(pool, w_loaded, 4 * 16 * (g + 1))
                wait_then(pool, bite_ready, read, const[3])
                pool.tensor_copy(w_hi[:, :, :, :], w_raw[:, :, :, :]).then_inc(w_split_hi, 1)
                wait(pool, w_split_hi, g + 1)
                pool.tensor_tensor(w_lo[:, :, :, :], w_raw[:, :, :, :], w_hi[:, :, :, :].bitcast(F32),
                                   ALU.subtract).then_inc(w_split, 1)

            def split_wv(it):
                wait(pool, wv_loaded, 2 * 16 * (it + 1))
                wait_then(pool, bite_ready, v_bites_to(it - 1), const[3])
                pool.tensor_copy(wv_hi[:, :, :], wv_raw[:, :, :]).then_inc(wv_split_hi, 1)
                wait(pool, wv_split_hi, it + 1)
                pool.tensor_tensor(wv_lo[:, :, :], wv_raw[:, :, :], wv_hi[:, :, :].bitcast(F32),
                                   ALU.subtract).then_inc(wv_split, 1)

            def step(it):
                split_w(2 * it + 2, bites_to(1, it))
                split_wv(it + 1)
                split_w(2 * it + 3, bites_to(0, it + 1))

            pool.memset(ident[:, :], 0.0).then_inc(ident_zeroed, 1)
            pool.wait_ge(ident_zeroed, 1)
            pool.affine_select(out=ident[:, :], in_=ident[:, :], compare_op=ALU.not_equal, fill=1.0,
                               base=0, pattern=[[-1, P]], channel_multiplier=1).then_inc(ident_ready, 1)
            split_w(0, 0)
            split_wv(0)
            split_w(1, bites_to(0, 0))
            step(0)
            with pool.Fori(1, ITS - 1) as it:
                step(it)
            early.split_wp_low(pool)

        @block.tensor
        def _(pe):
            def misc_free(folds, bites):
                wait(pe, fold_read, folds)
                wait(pe, bite_lo_done, bites)

            def bite(g, k, of_it, bank):
                if k < QK_BITES:
                    wait(pe, w_split, g + 1)
                    i, c = divmod(k, 2)
                    cols = slice(c * BANK, (c + 1) * BANK)
                    for n, (w, part) in enumerate(((w_hi, 0), (w_lo, 0), (w_hi, 1))):
                        for kc in range(KC):
                            last = pe.matmul(bank[:, :], w[:, i, kc, :], xT[:, part, kc, cols],
                                             start=(n == 0 and kc == 0), stop=(n == 2 and kc == KC - 1))
                else:
                    wait(pe, wv_split, of_it + 1)
                    for m in range(2):
                        mt = 2 * (k - QK_BITES) + m
                        for n, (w, part) in enumerate(((wv_hi, 0), (wv_lo, 0), (wv_hi, 1))):
                            for kc in range(KC):
                                last = pe.matmul(bank[:, m * 4 * E:(m + 1) * 4 * E],
                                                 xT[:, part, kc, mt * P:(mt + 1) * P], w[:, kc, :],
                                                 start=(n == 0 and kc == 0), stop=(n == 2 and kc == KC - 1))
                last.then_inc(bite_ready, 1)

            def score(it, tt):
                T = it * IT_T + tt
                pair, u = divmod(tt, PAIR_T)
                h, j = divmod(u, TILES)
                par = pair % 2
                if u == 0:
                    wait(pe, qk_laid, 16 * ASM * ((T // PAIR_T if isinstance(T, int) else 2 * it + pair) + 1))
                wait(pe, probs_ready, T - 1)
                q = q_st[:, par, h, j * P:(j + 1) * P]
                for c in range(N // BANK):
                    cols = slice(c * BANK, (c + 1) * BANK)
                    pe.matmul(scores[tt % 2][:, cols], q, k_hh[:, par, h, cols], start=True, stop=False)
                    last = pe.matmul(scores[tt % 2][:, cols], q, k_ll[:, par, h, cols], start=False, stop=True)
                last.then_inc(scores_ready, 1)

            def slot(it, tt):
                T = it * IT_T + tt
                pair, u = divmod(tt, PAIR_T)
                first = isinstance(it, int) and it == 0
                if exists(it, tt, 2):
                    score(it, tt + 2)
                if exists(it, tt):
                    wait(pe, probs_ready, T + 1)
                    for half in range(2):
                        wait(pe, pT_lo_done, 2 * T + half - 1)
                        for m in range(CH):
                            mt = half * CH + m
                            last = pe.transpose(pT_ps[half][:, m, :], probs[:, tt % 2, mt * P:(mt + 1) * P],
                                                ident[:, :])
                        last.then_inc(pT_ready, 1)
                if (not first or tt >= CH) and exists(it, tt, -CH):
                    c, part = it * (IT_T // CH) + tt // CH - 1, tt % CH
                    cpar, ch = (tt // CH - 1) % 2, (tt // CH - 1) % 8
                    vpar, h = divmod(ch // 2, 2)
                    if part == 0:
                        wait(pe, pT_lo_done, 2 * CH * (c + 1))
                        wait(pe, oT_done, c)
                        of_it, of_pair = divmod((tt // CH - 1) // 4, 2)
                        if of_pair == 0:
                            wait(pe, bite_lo_done, v_bites_to(it + of_it))
                        else:
                            wait(pe, v_moved, 16 * (it + of_it + 1))
                    for mt in (2 * part, 2 * part + 1):
                        v = v_st[:, 2 * vpar, mt, h].rearrange("p a e -> p (a e)")
                        pe.matmul(av_ps[:, :], v, pT_hi[:, cpar, mt, :], start=(mt == 0), stop=False)
                        last = pe.matmul(av_ps[:, :], v, pT_lo[:, cpar, mt, :], start=False, stop=(mt == HP - 1))
                    if part == CH - 1:
                        last.then_inc(av_ready, 1)
                folds = it * (IT_T // CH) + tt // CH - 1
                k = bite_of(pair, u) if pair < 2 else None
                if k is not None and exists(it, tt, PAIR_T):
                    wait(pe, xT_loaded, 16 * (it + pair))
                    misc_free(folds, bites_before(it, pair, u))
                    bite(2 * it + pair + 1, k, it + pair, misc_ps)
                if tt % CH == 0 and (not first or tt >= 2 * CH) and exists(it, tt, -2 * CH):
                    f = folds - 1
                    wait(pe, oT_done, f + 1)
                    if exists(it, tt, PAIR_T):
                        done = bites_before(it, pair, u)
                    else:
                        done = bites_to(1, it)
                    misc_free(f, done)
                    for m in range(CH):
                        last = pe.transpose(misc_ps[:, m * P:(m + 1) * P],
                                            oT[:, (tt // CH) % 2, m * P:(m + 1) * P], ident[:, :])
                    last.then_inc(fold_ready, 1)

            pe.wait_ge(ident_ready, 1)
            for kind, n in FIRST_WORK:
                if kind == "bite":
                    pe.wait_ge(xT_low_done, T_PAIRS)
                    wait(pe, bite_lo_done, n - 1)
                    bite(0, n, 0, FIRST_BANKS[n % 2])
                else:
                    b, i = divmod(n, T_PAIRS)
                    if n < T_PAIRS // 2:
                        pe.wait_ge(x_half_in, 16)
                    else:
                        pe.wait_ge(x_in[b], 16)
                    wait(pe, xT_low_done, n - 1)
                    for t in range(2):
                        for k in range(KC):
                            last = pe.transpose(xT_ps[n % 2][:, k, t * P:(t + 1) * P],
                                                x_tok[b % 2][:, 2 * i + t, k * P:(k + 1) * P], ident[:, :])
                    last.then_inc(x_transposed, 1)
            pe.wait_ge(xT_low_done, GROUPS)
            score(0, 0)
            score(0, 1)
            run(pe, slot)

        @block.scalar
        def _(act):
            def bite_hi(g, k, of_it, before, bank):
                wait(act, bite_ready, before + 1)
                if k < QK_BITES:
                    i, c = divmod(k, 2)
                    wait(act, qk_laid, 16 * ASM * g)
                    act.activation(qk_hi[:, i, c * BANK:(c + 1) * BANK], bank[:, :], ACT.Copy,
                                   scale=SCALE if i == 0 else 1.0).then_inc(bite_hi_done, 1)
                else:
                    wait(act, av_ready, 8 * of_it - 4)
                    wait(act, v_moved, 16 * of_it)
                    act.activation(v_part(k, 0), v_view(bank), ACT.Copy).then_inc(bite_hi_done, 1)

            def exp(it, tt):
                T = it * IT_T + tt
                wait(act, max_ready, T + 1)
                wait(act, pT_ready, 2 * (T - 1))
                act.activation(probs[:, tt % 2, :], scores[tt % 2][:, :], ACT.Exp,
                               bias=neg_max[:, tt % 4:tt % 4 + 1],
                               accum_out=row_sum[:, tt % IT_T:tt % IT_T + 1]).then_inc(probs_ready, 1)

            def slot(it, tt):
                T = it * IT_T + tt
                pair, u = divmod(tt, PAIR_T)
                first = isinstance(it, int) and it == 0
                k = bite_of(pair, u - 1) if pair < 2 else None
                if k is not None and exists(it, tt, PAIR_T):
                    bite_hi(2 * it + pair + 1, k, it + pair, bites_before(it, pair, u - 1), misc_ps)
                if tt % CH == 0 and (not first or tt >= 2 * CH) and exists(it, tt, -2 * CH):
                    c = it * (IT_T // CH) + tt // CH - 2
                    wait(act, av_ready, c + 1)
                    wait(act, fold_ready, c - 1)
                    act.activation(oT[:, (tt // CH) % 2, :], av_ps[:, :], ACT.Copy).then_inc(oT_done, 1)
                if isinstance(it, int) and it == ITS - 1 and tt == IT_T - CH:
                    act.wait_ge(bite_ready, bites_to(1, it))
                    early.split_wp_high(act)
                if exists(it, tt, 1):
                    exp(it, tt + 1)
                if exists(it, tt):
                    c = it * (IT_T // CH) + tt // CH
                    if tt % CH == 0:
                        wait(act, av_ready, c - 1)
                    for half in range(2):
                        wait(act, pT_ready, 2 * T + half + 1)
                        act.activation(pT_hi[:, (tt // CH) % 2, half * CH:(half + 1) * CH,
                                             (tt % CH) * P:(tt % CH + 1) * P],
                                       pT_ps[half][:, :, :], ACT.Copy).then_inc(pT_hi_done, 1)

            for kind, n in FIRST_WORK:
                if kind == "bite":
                    bite_hi(0, n, 0, n, FIRST_BANKS[n % 2])
                else:
                    b, i = divmod(n, T_PAIRS)
                    act.wait_ge(x_transposed, n + 1)
                    act.activation(xT_place(b)[0][:, :, i * 2 * P:(i + 1) * 2 * P], xT_ps[n % 2], ACT.Copy
                                   ).then_inc(xT_high_done, 1)
            exp(0, 0)
            run(act, slot)

        @block.vector
        def _(dve):
            def bite_lo(k, before, bank):
                wait(dve, bite_hi_done, before + 1)
                if k < QK_BITES:
                    i, c = divmod(k, 2)
                    cols = slice(c * BANK, (c + 1) * BANK)
                    dve.scalar_tensor_tensor(out=qk_lo[:, i, cols], in0=bank[:, :],
                                             scalar=SCALE if i == 0 else 1.0, in1=qk_hi[:, i, cols].bitcast(F32),
                                             op0=ALU.mult, op1=ALU.subtract).then_inc(bite_lo_done, 1)
                else:
                    dve.tensor_tensor(v_part(k, 1), v_view(bank), v_part(k, 0).bitcast(F32), ALU.subtract
                                      ).then_inc(bite_lo_done, 1)

            def maximum(it, tt):
                T = it * IT_T + tt
                wait(dve, scores_ready, T + 1)
                dve.tensor_reduce(neg_max[:, tt % 4:tt % 4 + 1], scores[tt % 2][:, :], AX.X, ALU.max,
                                  negate=True).then_inc(max_ready, 1)

            def slot(it, tt):
                T = it * IT_T + tt
                pair, u = divmod(tt, PAIR_T)
                first = isinstance(it, int) and it == 0
                k = bite_of(pair, u - 1) if pair < 2 else None
                if k is not None and exists(it, tt, PAIR_T):
                    bite_lo(k, bites_before(it, pair, u - 1), misc_ps)
                if tt % CH == 1 and (not first or tt >= 2 * CH) and exists(it, tt, -2 * CH - 1):
                    ft = tt // CH - 2
                    f = it * (IT_T // CH) + ft
                    fpair, ch = divmod(ft % (IT_T // CH), 4)
                    h, half = divmod(ch, 2)
                    sums = (ft * CH) % IT_T
                    wait(dve, o_done, f)
                    dve.reciprocal(inv_sum[:, :], row_sum[:, sums:sums + CH]).then_inc(inv_done, 1)
                    wait(dve, fold_ready, f + 1)
                    dve.tensor_reduce(o_sum[:, :, :], misc_ps[:, :].rearrange("p (m a e) -> p m e a", m=CH, a=2),
                                      AX.X, ALU.add).then_inc(fold_read, 1)
                    wait(dve, inv_done, f + 1)
                    wait(dve, fold_read, f + 1)
                    if ch == 0:
                        wait(dve, o_stored, 16 * (2 * it + (ft // 4) - 1))
                    dve.tensor_tensor(o_out[:, fpair, half * CH:(half + 1) * CH, h * E:(h + 1) * E],
                                      o_sum[:, :, :], inv_sum[:, :].rearrange("p (m a) -> p m a", a=1)
                                      .broadcast_to([P, CH, E]), ALU.mult).then_inc(o_done, 1)
                if exists(it, tt, 2):
                    maximum(it, tt + 2)
                if exists(it, tt):
                    if first and tt in (0, CH):
                        dve.wait_ge(xT_stored[1 + tt // CH], 16 * HILO)
                    for half in range(2):
                        wait(dve, pT_hi_done, 2 * T + half + 1)
                        where = (slice(None), (tt // CH) % 2, slice(half * CH, (half + 1) * CH),
                                 slice((tt % CH) * P, (tt % CH + 1) * P))
                        dve.tensor_tensor(pT_lo[where], pT_ps[half][:, :, :], pT_hi[where].bitcast(F32),
                                          ALU.subtract).then_inc(pT_lo_done, 1)

            for kind, n in FIRST_WORK:
                if kind == "bite":
                    bite_lo(n, n, FIRST_BANKS[n % 2])
                else:
                    b, i = divmod(n, T_PAIRS)
                    cols = slice(i * 2 * P, (i + 1) * 2 * P)
                    dve.wait_ge(xT_high_done, n + 1)
                    dve.tensor_tensor(xT_place(b)[1][:, :, cols], xT_ps[n % 2],
                                      xT_place(b)[0][:, :, cols].bitcast(F32), ALU.subtract).then_inc(xT_low_done, 1)
            maximum(0, 0)
            maximum(0, 1)
            run(dve, slot)


class ForProjection:
    RING = 3
    TILES = 2

    def __init__(self, nc, ctx, xT, qk_hi, qk_lo, o_dram, Wp):
        HE, D = Wp.shape
        CC = HE // P
        self.o_rows = o_dram.rearrange("b n c -> (b n) c")
        self.wp_rows = Wp.rearrange("(e c h) n -> h e c n", h=2, c=CC)
        flat = [xT[:, part].rearrange("p k n -> p (k n)") for part in range(HILO)]
        self.wp_hi, self.wp_lo = [f.rearrange("p (c d) -> p c d", c=CC) for f in flat]
        self.wp_raw = (qk_hi[:, :, :].rearrange("p a n -> p (a n)").bitcast(F32)
                       .rearrange("p (c d) -> p c d", c=CC))
        self.o_tok = [qk_lo[:, i].bitcast(F32) for i in range(self.TILES)]
        self.wp_in = ctx.enter_context(nc.semaphore("wp_in"))
        self.wp_hi_done = ctx.enter_context(nc.semaphore("wp_hi_done"))
        self.wp_split = ctx.enter_context(nc.semaphore("wp_split"))
        self.o_in = [ctx.enter_context(nc.semaphore(f"o_in{i}")) for i in range(self.RING)]

    def load_wp(self, sp):
        for h in range(2):
            rows = slice(h * (P // 2), (h + 1) * (P // 2))
            sp.dma_start(self.wp_raw[rows, :, :], self.wp_rows[h]).then_inc(self.wp_in, 16)

    def load_o(self, sp, s):
        ring = s % self.RING
        sp.dma_start(self.o_tok[ring], self.o_rows[s * P:(s + 1) * P, :]).then_inc(self.o_in[ring], 16)

    def split_wp_high(self, act):
        act.wait_ge(self.wp_in, 32)
        act.activation(self.wp_hi, self.wp_raw, ACT.Copy).then_inc(self.wp_hi_done, 1)

    def split_wp_low(self, pool):
        pool.wait_ge(self.wp_hi_done, 1)
        pool.tensor_tensor(self.wp_lo, self.wp_raw, self.wp_hi.bitcast(F32), ALU.subtract).then_inc(self.wp_split, 1)


class ExpertWeights:
    PIECES = 4

    def __init__(self, nc, ctx, W1, W2):
        _, D, HID = W1.shape
        self.W1, self.W2 = W1, W2
        shapes = ([P, D // P, HID], [P, HID // P, D])
        self.raw = [ctx.enter_context(nc.sbuf_tensor(f"w{i + 1}_raw", s, F32)) for i, s in enumerate(shapes)]
        self.high = [ctx.enter_context(nc.sbuf_tensor(f"w{i + 1}_hi", s, F32R)) for i, s in enumerate(shapes)]
        self.low = [ctx.enter_context(nc.sbuf_tensor(f"w{i + 1}_lo", s, F32R)) for i, s in enumerate(shapes)]
        self.loaded = [ctx.enter_context(nc.semaphore(f"w{i + 1}_in")) for i in range(2)]
        self.high_done = [ctx.enter_context(nc.semaphore(f"w{i + 1}_hi_done")) for i in range(2)]
        self.split = [ctx.enter_context(nc.semaphore(f"w{i + 1}_split")) for i in range(2)]

    def load(self, sp, i, e):
        W = (self.W1, self.W2)[i]
        sp.dma_start(self.raw[i][:, :, :], W[e].rearrange("(k p) n -> p k n", p=P)).then_inc(self.loaded[i], 16)

    def piece(self, w, j):
        flat = w[:, :, :].rearrange("p a b -> p (a b)")
        size = flat.shape[1] // self.PIECES
        return flat[:, j * size:(j + 1) * size]

    def split_high(self, act, i, e, j):
        act.wait_ge(self.loaded[i], 16 * (e + 1))
        act.activation(self.piece(self.high[i], j), self.piece(self.raw[i], j), ACT.Copy
                       ).then_inc(self.high_done[i], 1)

    def split_low(self, pool, i, e):
        for j in range(self.PIECES):
            pool.wait_ge(self.high_done[i], self.PIECES * e + j + 1)
            pool.tensor_tensor(self.piece(self.low[i], j), self.piece(self.raw[i], j),
                               self.piece(self.high[i], j).bitcast(F32), ALU.subtract).then_inc(self.split[i], 1)

    def wait_split(self, eng, i, e):
        eng.wait_ge(self.split[i], self.PIECES * (e + 1))


def build_project_route(nc, o_dram, x, bp, ctx_in, conv_w, conv_b, Wg, x2, send_to, xe_dram, late_sent, early,
                        weights, const):
    B, N, D = x.shape
    HE = o_dram.shape[2]
    CC = HE // P
    S = ctx_in.shape[1]
    RATE = conv_w.shape[0]
    TILES = B * N // P
    TB = N // P
    HALF = N // 2
    TC = (S - RATE) // RATE + 1
    KC = D // P
    EX = Wg.shape[1]
    CAP = N // EX
    HT = HALF // P
    CT, CP = divmod(HALF - TC, P)
    MT, MP = divmod(N - S, P)
    SC = S - P * (TB - 1 - MT)
    SM = S % P
    RING = early.RING
    LAG = 2
    STEADY = dict(move=3, old=3, comp=5, stats=5, norm=6,
                  x2T=7, logits=8, gates=11, counts=12, places=13)
    NEXT_TO_LAST = dict(move=3, old=3, comp=5, stats=5, norm=6,
                        x2T=7, logits=8, gates=12, counts=12, places=15)
    LAST = dict(old=2, comp=3, move=3, stats=5, norm=6,
                x2T=6, logits=6, gates=7, counts=7, places=8)
    SLOTS = TILES + LAST["places"] + 1
    SCHEDULE = [STEADY] * (B - 2) + [NEXT_TO_LAST, LAST]
    GROUP = {b: 2 for b in range(B - 1)}
    GROUP[B - 1] = 4
    assert CT == HT - 1 and MT == TB - 2 and CP + TC == P and SC + MP == P and S == P + SM and MP + SM == P
    ident, _, _, _ = const
    ID, GATE = D, D + 1
    with ExitStack() as ctx:
        def sb(name, shape, dt=F32):
            return ctx.enter_context(nc.sbuf_tensor(name, shape, dt))

        def psum(name, shape):
            return ctx.enter_context(nc.psum_tensor(name, shape, F32))

        def sem(name):
            return ctx.enter_context(nc.semaphore(name))

        wp_hi, wp_lo, wp_split, o_in = early.wp_hi, early.wp_lo, early.wp_split, early.o_in
        bp_all = sb("bp_all", [P, D])
        eps = sb("eps", [P, 1])
        o_tok = early.o_tok + [sb("o_tok", [P, HE])[:, :]]
        oT_hi = sb("oT_hi", [P, LAG + 1, CC, P], F32R)
        oT_lo = sb("oT_lo", [P, LAG + 1, CC, P], F32R)
        x1 = sb("x1", [P, TILES, D])
        stats = sb("stats1", [P, 2, 6])
        moments = sb("moments1", [P, 2, 2])
        root = sb("root1", [P, 2])
        scale = sb("scale1", [P, 2])
        shift = sb("shift1", [P, 2])

        cw = sb("cw", [P, RATE, KC, D])
        wg = sb("wg", [P, KC, EX])
        old_T = sb("old_T", [P, RATE, KC, P])
        x2T = sb("x2T", [P, TB, KC, P])
        stats2 = sb("stats2", [P, TB, 6])
        moments2 = sb("moments2", [P, TB, 2])
        root2 = sb("root2", [P, TB])
        scale2 = sb("scale2", [P, TB])
        shift2 = sb("shift2", [P, TB])
        before = sb("before", [P, P])
        ones = sb("ones", [P, P])
        rank = sb("rank", [P, EX])
        lower = sb("lower", [P, EX, EX])
        base = sb("base", [P, B, EX])
        logits = sb("logits", [P, TB, EX])
        top = sb("top", [P, TB])
        gates = sb("gates", [P, TB, EX])
        inv = sb("inv", [P, TB])
        gate = sb("gate", [P, TB])
        first = sb("first", [P, TB])
        mask = sb("mask", [P, TB, EX])
        tiles_before = sb("tiles_before", [P, TB + 1, EX])
        work = sb("work", [P, TB, EX])
        place = sb("place", [P, TB])
        keep = sb("keep", [P, TB])
        taken = sb("taken", [P, EX])
        spare = sb("spare", [P, EX])
        spare_before = sb("spare_before", [P, EX])
        spare_row = sb("spare_row", [P, EX])
        triangle = sb("triangle", [P, EX, EX])
        dropped = sb("dropped", [P, TB, EX])
        dropped_before = sb("dropped_before", [P, TB])
        number = sb("number", [P, TB, EX])
        inside = sb("inside", [P, TB, EX])
        kept = sb("kept", [P, TB, EX])
        row = sb("row", [P, TB])

        oT_ps = [psum(f"oT_ps{i}", [P, CC, P]) for i in range(2)]
        y_ps = [psum(f"y1_ps{i}", [P, D]) for i in range(2)]
        wide_ps = psum("wide_ps", [P, 2, KC, P])
        thin_ps = psum("thin_ps", [P, BANK])
        def old_ps(b):
            bank = oT_ps[0][:, 0:4] if b == B - 1 else wide_ps[:, :, :, :].rearrange("p a k n -> p (a k) n")
            return bank.rearrange("p a n -> p (a n)").rearrange("p (k n) -> p k n", k=KC)

        def comp_ps(b):
            bank = oT_ps[0][:, 4:6] if b == B - 1 else wide_ps[:, 0]
            return bank.rearrange("p k n -> p (k n)")

        def x2T_ps(b, i):
            if b == B - 1:
                return oT_ps[1 - i][:, :, :].rearrange("p (a k) n -> p a k n", k=KC)
            return wide_ps[:, :, :, :]

        def x2T_sb(b, i):
            first = GROUP[b] * i if b == B - 1 else 0
            return x2T[:, first:first + GROUP[b], :, :]

        def logits_ps(b):
            bank = y_ps[0] if b == B - 1 else thin_ps
            return bank[:, 0:TB * EX].rearrange("p (t e) -> p t e", t=TB)

        def total_ps(b):
            bank = y_ps[0] if b == B - 1 else thin_ps
            return bank[:, TB * EX:(TB + 1) * EX]


        bp_in = sem("bp_in")
        consts_set = sem("consts_set")
        x_in = [sem(f"x1_x_in{b}") for b in range(B)]
        xb_done = sem("xb_done")
        oT_ready = sem("oT_ready")
        oT_hi_done = sem("oT_hi_done")
        oT_lo_done = sem("oT_lo_done")
        y_ready = sem("y1_ready")
        z_done = sem("z1_done")
        stats_done = sem("stats1_done")
        moments_done = sem("moments1_done")
        root_done = sem("root1_done")
        scale_done = sem("scale1_done")
        shift_done = sem("shift1_done")
        x1_done = sem("x1_done")

        weights_in = sem("weights_in")
        moved = [sem(f"moved{b}") for b in range(B)]
        new_in = [sem(f"new_in{b}") for b in range(B)]
        old_cleared = sem("old_cleared")
        old_ready = sem("old_ready")
        old_placed = sem("old_placed")
        comp_ready = sem("comp_ready")
        sum_done = sem("sum_done")
        half_sum_done = sem("half_sum_done")
        comp_added = sem("comp_added")
        stats2_done = sem("stats2_done")
        moments2_done = sem("moments2_done")
        root2_done = sem("root2_done")
        shift2_done = sem("shift2_done")
        x2_done = sem("x2_done")
        x2T_ready = sem("x2T_ready")
        x2T_done = sem("x2T_done")
        logits_ready = sem("logits_ready")
        shifted = sem("shifted")
        exp_done = sem("exp_done")
        mask_done = sem("mask_done")
        count_ready = sem("count_ready")
        count_read = sem("count_read")
        dve_step = sem("dve_step")
        rows_ready = sem("rows_ready")
        sent = sem("sent")
        block = ctx.enter_context(nc.Block())

        x1_b = x1[:, :, :].rearrange("p (b t) d -> p b t d", b=B)
        x2_b = x2[:, :, 0:D].rearrange("p (b t) d -> p b t d", b=B)
        MOVES = 4
        NEW = 3
        CONSTS = 8

        def stages(s):
            found = []
            for b in range(B):
                for name, k in SCHEDULE[b].items():
                    groups = TB // GROUP[b] if name in ("x2T", "logits", "norm") else 1
                    i = s - TB * (b + 1) - k
                    if b == B - 1:
                        found += [(b, name, i) for i in range(groups) if s == TB * (b + 1) + k]
                    elif 0 <= i < groups:
                        found.append((b, name, i))
            return found

        def groups_before(b, i):
            return sum(TB // GROUP[c] for c in range(b)) + i

        @block.sync
        def _(sp):
            def load_o(s):
                wait(sp, oT_ready, s - RING + 1)
                sp.dma_start(o_tok[s % RING], early.o_rows[s * P:(s + 1) * P, :]).then_inc(o_in[s % RING], 16)

            def load_x(b):
                sp.dma_start(x1_b[:, b], x[b].rearrange("(t p) d -> p t d", p=P)).then_inc(x_in[b], 16)

            def load_new(b):
                sp.dma_start(x2_b[CP:P, b, CT, :], conv_b.rearrange("(a n) -> a n", a=1).broadcast_to([TC, D])
                             ).then_inc(new_in[b], 16)
                sp.dma_start(x2_b[MP:P, b, MT, :], ctx_in[b, 0:SC, :]).then_inc(new_in[b], 16)
                sp.dma_start(x2_b[:, b, TB - 1, :], ctx_in[b, SC:S, :]).then_inc(new_in[b], 16)

            load_o(2)
            load_x(0)
            sp.dma_start(bp_all[:, :], bp.rearrange("(a n) -> a n", a=1).broadcast_to([P, D])).then_inc(bp_in, 16)
            for s in range(SLOTS):
                if s + RING < TILES:
                    load_o(s + RING)
                if s == 1:
                    sp.dma_start(cw[:, :, :, :], conv_w.rearrange("r (k p) d -> p r k d", p=P)
                                 ).then_inc(weights_in, 16)
                    sp.dma_start(wg[:, :, :], Wg.rearrange("(k p) e -> p k e", p=P)).then_inc(weights_in, 16)
                if s % TB == 3 and s // TB + 1 < B:
                    load_x(s // TB + 1)
                if s % TB == 5 and s // TB < B:
                    load_new(s // TB)
                if s in (TB, TB + 2):
                    weights.load(sp, (s - TB) // 2, 0)
                for b, name, _ in stages(s):
                    if name == "move":
                        sp.wait_ge(x1_done, TB * (b + 1))
                        for dst, src in (((slice(0, P - TC), 0, HT), (slice(TC, P), 0)),
                                         ((slice(P - TC, P), 0, HT - 1), (slice(0, TC), 1)),
                                         ((slice(0, P - SM), HT, TB - 1), (slice(SM, P), HT + 1)),
                                         ((slice(P - SM, P), HT, TB - 2), (slice(0, SM), HT + 2))):
                            n = dst[2] - dst[1]
                            sp.dma_start(x2_b[dst[0], b, dst[1]:dst[2], :], x1_b[src[0], b, src[1]:src[1] + n, :]
                                         ).then_inc(moved[b], 16)

        @block.gpsimd
        def _(pool):
            pool.memset(eps[:, :], 1e-5).then_inc(consts_set, 1)
            pool.memset(ones[:, :], 1.0).then_inc(consts_set, 1)
            pool.wait_ge(bp_in, 16)
            bias = bp_all[:, :].rearrange("p (a d) -> p a d", a=1).broadcast_to([P, TB, D])
            def add_bias(b):
                pool.wait_ge(x_in[b], 16)
                pool.tensor_tensor(x1_b[:, b], x1_b[:, b], bias, ALU.add).then_inc(xb_done, 1)

            for b in range(2):
                add_bias(b)
                if b == 0:
                    pool.memset(old_T[:, :, :, :], 0.0).then_inc(old_cleared, 1)
                    pool.iota(rank[:, :], pattern=[[-1, EX]], base=EX, channel_multiplier=0,
                              allow_small_or_imprecise_dtypes=True).then_inc(consts_set, 1)
                    pool.iota(base[:, :, :], pattern=[[CAP, B], [B * CAP, EX]], base=0, channel_multiplier=0,
                              allow_small_or_imprecise_dtypes=True).then_inc(consts_set, 1)
                    pool.iota(x2[:, :, ID:ID + 1].bitcast(mybir.dt.uint32), pattern=[[P, TILES]], base=0,
                              channel_multiplier=1).then_inc(consts_set, 1)
                    pool.memset(x2[:, :, GATE + 1:], 0.0).then_inc(consts_set, 1)
                    pool.wait_ge(consts_set, 2)
                    pool.affine_select(out=before[:, :], in_=ones[:, :], compare_op=ALU.is_gt, fill=0.0,
                                       base=0, pattern=[[1, P]], channel_multiplier=-1).then_inc(consts_set, 1)
                    pool.affine_select(out=lower[:, :, :],
                                       in_=ones[:, 0:EX * EX].rearrange("p (e f) -> p e f", e=EX),
                                       compare_op=ALU.is_gt, fill=0.0, base=0, pattern=[[1, EX], [-1, EX]],
                                       channel_multiplier=0).then_inc(consts_set, 1)
            for b in range(B):
                pool.wait_ge(new_in[b], 16 * NEW)
                pool.wait_ge(moved[b], 16 * MOVES)
                for t in range(0, HT if b == B - 1 else TB, 2):
                    pool.tensor_tensor(x2_b[:, b, t:t + 2], x2_b[:, b, t:t + 2], x1_b[:, b, t:t + 2], ALU.add
                                       ).then_inc(sum_done, 1)
                if b + 2 < B:
                    add_bias(b + 2)
                for c in [b - 1] if b > 0 else []:
                    pool.wait_ge(rows_ready, c + 1)
                    for t in range(c * TB, (c + 1) * TB):
                        pool.indirect_dma_start(
                            out=xe_dram[:, :], out_offset=bass.IndirectOffsetOnAxis(ap=send_to[:, t:t + 1], axis=0),
                            in_=x2[:, t, :], in_offset=None
                        ).then_inc(sent if c < EARLY_BATCHES else late_sent, 16)
                if b == B - 2:
                    for i in range(2):
                        weights.split_low(pool, i, 0)
            pool.wait_ge(sent, 16 * TB * EARLY_BATCHES)

        @block.tensor
        def _(pe):
            def transposes(b, name, i):
                if name == "old":
                    pe.wait_ge(x1_done, TB * b + HT + 2)
                    if b == B - 1:
                        pe.wait_ge(oT_lo_done, TILES)
                    else:
                        wait(pe, x2T_done, groups_before(b, 0))
                    for kc in range(KC):
                        for t in range(2):
                            last = pe.transpose(old_ps(b)[:, kc, t * P:(t + 1) * P],
                                                x1_b[:, b, HT + t, kc * P:(kc + 1) * P], ident[:, :])
                    last.then_inc(old_ready, 1)
                if name == "comp":
                    pe.wait_ge(weights_in, 32)
                    pe.wait_ge(old_placed, b + 1)
                    for r in range(RATE):
                        for kc in range(KC):
                            last = pe.matmul(comp_ps(b), old_T[:, r, kc, :], cw[:, r, kc, :],
                                             start=(r == 0 and kc == 0), stop=(r == RATE - 1 and kc == KC - 1))
                    last.then_inc(comp_ready, 1)
                if name == "x2T":
                    pe.wait_ge(comp_added, b + 1)
                    if b < B - 1:
                        wait(pe, x2T_done, groups_before(b, i))
                    for t in range(GROUP[b]):
                        pe.wait_ge(x2_done, TB * b + GROUP[b] * i + t + 1)
                        for kc in range(KC):
                            last = pe.transpose(x2T_ps(b, i)[:, t, kc, :],
                                                x2_b[:, b, GROUP[b] * i + t, kc * P:(kc + 1) * P], ident[:, :])
                    last.then_inc(x2T_ready, 1)

            def products(b, name, i):
                if name == "logits":
                    pe.wait_ge(x2T_done, groups_before(b, i) + 1)
                    if b == B - 1:
                        pe.wait_ge(z_done, TILES)
                    else:
                        wait(pe, count_read, b)
                    for t in range(GROUP[b]):
                        for kc in range(KC):
                            last = pe.matmul(logits_ps(b)[:, GROUP[b] * i + t, :], x2T_sb(b, i)[:, t, kc, :],
                                             wg[:, kc, :],
                                             start=(kc == 0), stop=(kc == KC - 1))
                    last.then_inc(logits_ready, 1)
                if name == "counts":
                    pe.wait_ge(consts_set, CONSTS)
                    pe.wait_ge(mask_done, b + 1)
                    pe.matmul(logits_ps(b), before[:, :], mask[:, :, :], start=True, stop=False)
                    pe.matmul(logits_ps(b), ones[:, :], tiles_before[:, 0:TB, :], start=False, stop=True)
                    pe.matmul(total_ps(b), ones[:, :], tiles_before[:, TB, :], start=True,
                              stop=True).then_inc(count_ready, 1)

            for s in range(SLOTS):
                if s < TILES:
                    pe.wait_ge(o_in[s % RING], 16 * (s // RING + 1))
                    wait(pe, oT_lo_done, s - 1)
                    for c in range(CC):
                        last = pe.transpose(oT_ps[s % 2][:, c, :], o_tok[s % RING][:, c * P:(c + 1) * P],
                                            ident[:, :])
                    last.then_inc(oT_ready, 1)
                after = [(b, name, i) for b, name, i in stages(s) if name == "x2T" and b < B - 1]
                for stage in stages(s):
                    if stage not in after:
                        transposes(*stage)
                tile = s - LAG
                if 0 <= tile < TILES:
                    if tile == 0:
                        pe.wait_ge(wp_split, 1)
                    ring = tile % (LAG + 1)
                    pe.wait_ge(oT_lo_done, tile + 1)
                    wait(pe, z_done, tile - 1)
                    for n, (a, w) in enumerate(((oT_hi, wp_hi), (oT_hi, wp_lo), (oT_lo, wp_hi))):
                        for c in range(CC):
                            last = pe.matmul(y_ps[tile % 2][:, :], a[:, ring, c, :], w[:, c, :],
                                             start=(n == 0 and c == 0), stop=(n == 2 and c == CC - 1))
                    last.then_inc(y_ready, 1)
                for stage in reversed(stages(s)):
                    products(*stage)
                for stage in after:
                    transposes(*stage)

        @block.scalar
        def _(act):
            act.wait_ge(consts_set, 1)

            def stage(b, name, i):
                if name == "stats":
                    act.wait_ge(moments2_done, TB * (b + 1))
                    act.activation(root2[:, :], moments2[:, :, 1], ACT.Sqrt, bias=eps[:, :]).then_inc(root2_done, 1)
                if name == "norm" and b < B - 1:
                    act.wait_ge(shift2_done, b + 1)
                    for t in range(GROUP[b] * i, GROUP[b] * (i + 1)):
                        act.activation(x2_b[:, b, t, :], x2_b[:, b, t, :], ACT.Identity,
                                       scale=scale2[:, t:t + 1], bias=shift2[:, t:t + 1]).then_inc(x2_done, 1)
                if name == "x2T":
                    n = groups_before(b, i)
                    act.wait_ge(x2T_ready, n + 1)
                    wait(act, logits_ready, groups_before(b, 0) if b == B - 1 else n)
                    act.activation(x2T_sb(b, i), x2T_ps(b, i), ACT.Copy).then_inc(x2T_done, 1)
                if name == "gates":
                    act.wait_ge(shifted, b + 1)
                    act.activation(gates[:, :, :], logits[:, :, :], ACT.Exp).then_inc(exp_done, 1)

            for s in range(SLOTS):
                if s < TILES:
                    act.wait_ge(oT_ready, s + 1)
                    wait(act, y_ready, s - LAG)
                    act.activation(oT_hi[:, s % (LAG + 1)], oT_ps[s % 2][:, :, :], ACT.Copy).then_inc(oT_hi_done, 1)
                for b_name_i in stages(s):
                    stage(*b_name_i)
                if s in (2 * TB + 1, 2 * TB + 2):
                    for j in range(weights.PIECES):
                        weights.split_high(act, s - 2 * TB - 1, 0, j)
                tile = s - LAG - 1
                if 0 <= tile < TILES:
                    par = tile % 2
                    act.wait_ge(moments_done, tile + 1)
                    act.activation(root[:, par:par + 1], moments[:, par, 1:2], ACT.Sqrt,
                                   bias=eps[:, :]).then_inc(root_done, 1)
                tile = s - LAG - 2
                if 0 <= tile < TILES:
                    par = tile % 2
                    act.wait_ge(shift_done, tile + 1)
                    act.activation(x1[:, tile, :], x1[:, tile, :], ACT.Identity, scale=scale[:, par:par + 1],
                                   bias=shift[:, par:par + 1]).then_inc(x1_done, 1)

        @block.vector
        def _(dve):
            steps = [0]

            def step(ins):
                steps[0] += 1
                ins.then_inc(dve_step, 1)
                dve.wait_ge(dve_step, steps[0])

            def spread(a):
                return a[:, :].rearrange("p (t a) -> p t a", a=1).broadcast_to([P, TB, EX])

            def over_tokens(a):
                return a[:, :].rearrange("p (a e) -> p a e", a=1).broadcast_to([P, TB, EX])

            def place_old(b):
                dve.wait_ge(old_ready, b + 1)
                dve.wait_ge(old_cleared, 1)
                wait(dve, comp_ready, b)
                for kc in range(KC):
                    last = dve.tensor_copy(old_T[:, :, kc, CP:P],
                                           old_ps(b)[:, kc, 0:TC * RATE].rearrange("p (t r) -> p r t", r=RATE))
                last.then_inc(old_placed, 1)

            def norm_stats(b):
                wait(dve, x2_done, TB * b)
                if b == B - 1:
                    dve.wait_ge(new_in[b], 16 * NEW)
                    dve.wait_ge(moved[b], 16 * MOVES)
                    dve.tensor_tensor(x2_b[:, b, HT:], x2_b[:, b, HT:], x1_b[:, b, HT:], ALU.add
                                      ).then_inc(half_sum_done, 1)
                    dve.wait_ge(half_sum_done, 1)
                    for t in range(HT, TB):
                        dve.bn_stats(stats2[:, t, :], x2_b[:, b, t, :]).then_inc(stats2_done, 1)
                dve.wait_ge(sum_done, TB // 2 * b + CT // 2 + 1)
                dve.wait_ge(comp_ready, b + 1)
                dve.tensor_tensor(x2_b[:, b, CT, :], comp_ps(b), x2_b[:, b, CT, :], ALU.add
                                  ).then_inc(comp_added, 1)
                for t in [t for t in range(HT if b == B - 1 else TB) if t != CT] + [CT]:
                    if t == CT:
                        dve.wait_ge(comp_added, b + 1)
                    else:
                        dve.wait_ge(sum_done, TB // 2 * b + t // 2 + 1)
                    dve.bn_stats(stats2[:, t, :], x2_b[:, b, t, :]).then_inc(stats2_done, 1)
                dve.wait_ge(stats2_done, TB * (b + 1))
                for t in range(TB):
                    dve.bn_aggr(moments2[:, t, :], stats2[:, t, :]).then_inc(moments2_done, 1)

            def norm(b):
                dve.wait_ge(root2_done, b + 1)
                step(dve.reciprocal(scale2[:, :], root2[:, :]))
                if b < B - 1:
                    dve.scalar_tensor_tensor(out=shift2[:, :], in0=moments2[:, :, 0], scalar=-1.0,
                                             in1=scale2[:, :], op0=ALU.mult, op1=ALU.mult).then_inc(shift2_done, 1)
                    return
                for t in range(TB):
                    dve.tensor_scalar(x2_b[:, b, t, :], x2_b[:, b, t, :], moments2[:, t, 0:1],
                                      scale2[:, t:t + 1], ALU.subtract, ALU.mult).then_inc(x2_done, 1)

            def choose(b):
                dve.wait_ge(logits_ready, groups_before(b + 1, 0))
                step(dve.tensor_reduce(top[:, :], logits_ps(b), AX.X, ALU.max))
                dve.tensor_tensor(logits[:, :, :], logits_ps(b), spread(top), ALU.subtract).then_inc(shifted, 1)
                dve.wait_ge(exp_done, b + 1)
                step(dve.tensor_reduce(top[:, :], gates[:, :, :], AX.X, ALU.add))
                step(dve.reciprocal(inv[:, :], top[:, :]))
                step(dve.tensor_tensor(gates[:, :, :], gates[:, :, :], spread(inv), ALU.mult))
                step(dve.tensor_reduce(gate[:, :], gates[:, :, :], AX.X, ALU.max))
                step(dve.tensor_tensor(work[:, :, :], gates[:, :, :], spread(gate), ALU.is_ge))
                dve.wait_ge(consts_set, CONSTS)
                step(dve.tensor_tensor(work[:, :, :], work[:, :, :], over_tokens(rank), ALU.mult))
                step(dve.tensor_reduce(first[:, :], work[:, :, :], AX.X, ALU.max))
                step(dve.tensor_tensor(mask[:, :, :], over_tokens(rank), spread(first), ALU.is_equal))
                step(dve.memset(tiles_before[:, 0, :], 0.0))
                for t in range(1, TB + 1):
                    ins = dve.tensor_tensor(tiles_before[:, t, :], tiles_before[:, t - 1, :], mask[:, t - 1, :],
                                            ALU.add)
                    if t < TB:
                        step(ins)
                ins.then_inc(mask_done, 1)

            def find_rows(b):
                tiles = slice(b * TB, (b + 1) * TB)
                base_b = base[:, b, :].rearrange("p (a e) -> p a e", a=1).broadcast_to([P, TB, EX])
                dve.wait_ge(count_ready, b + 1)
                dve.tensor_scalar(taken[:, :], total_ps(b), float(CAP), None, ALU.min)
                dve.tensor_scalar(dropped[:, :, :], logits_ps(b), -float(CAP), 0.0, ALU.add, ALU.max)
                dve.tensor_tensor(number[:, :, :], logits_ps(b), base_b, ALU.add)
                step(dve.scalar_tensor_tensor(out=kept[:, :, :], in0=logits_ps(b), scalar=float(CAP),
                                              in1=mask[:, :, :], op0=ALU.is_lt, op1=ALU.mult))
                dve.sem_inc(count_read, 1)
                dve.tensor_scalar(spare[:, :], taken[:, :], -1.0, float(CAP), ALU.mult, ALU.add)
                dve.tensor_tensor(spare_row[:, :], taken[:, :], base[:, b, :], ALU.add)
                dve.tensor_reduce(dropped_before[:, :], dropped[:, :, :], AX.X, ALU.add)
                dve.tensor_reduce(keep[:, :], kept[:, :, :], AX.X, ALU.add)
                step(dve.tensor_tensor(work[:, :, :], number[:, :, :], kept[:, :, :], ALU.mult))
                dve.tensor_reduce(row[:, :], work[:, :, :], AX.X, ALU.add)
                dve.tensor_tensor(x2[:, tiles, GATE:GATE + 1], gate[:, :].rearrange("p (t a) -> p t a", a=1),
                                  keep[:, :].rearrange("p (t a) -> p t a", a=1), ALU.mult)
                step(dve.tensor_tensor(triangle[:, :, :], lower[:, :, :],
                                       spare[:, :].rearrange("p (a f) -> p a f", a=1).broadcast_to([P, EX, EX]),
                                       ALU.mult))
                step(dve.tensor_reduce(spare_before[:, :], triangle[:, :, :], AX.X, ALU.add))
                step(dve.tensor_tensor(number[:, :, :], spread(dropped_before), over_tokens(spare_before),
                                       ALU.subtract))
                dve.tensor_tensor(inside[:, :, :], number[:, :, :], over_tokens(spare), ALU.is_lt)
                step(dve.tensor_tensor(work[:, :, :], number[:, :, :], over_tokens(spare_row), ALU.add))
                step(dve.scalar_tensor_tensor(out=inside[:, :, :], in0=number[:, :, :], scalar=0.0,
                                              in1=inside[:, :, :], op0=ALU.is_ge, op1=ALU.mult))
                step(dve.tensor_tensor(work[:, :, :], work[:, :, :], inside[:, :, :], ALU.mult))
                step(dve.tensor_reduce(place[:, :], work[:, :, :], AX.X, ALU.add))
                step(dve.tensor_scalar(keep[:, :], keep[:, :], -1.0, 1.0, ALU.mult, ALU.add))
                step(dve.tensor_tensor(place[:, :], place[:, :], keep[:, :], ALU.mult))
                step(dve.tensor_tensor(row[:, :], row[:, :], place[:, :], ALU.add))
                dve.tensor_copy(send_to[:, tiles], row[:, :]).then_inc(rows_ready, 1)

            steps_of = dict(old=place_old, stats=norm_stats, norm=norm, gates=choose)
            for s in range(SLOTS):
                for b, name, _ in stages(s):
                    if name == "places":
                        find_rows(b)
                if s < TILES:
                    dve.wait_ge(oT_hi_done, s + 1)
                    ring = s % (LAG + 1)
                    dve.tensor_tensor(oT_lo[:, ring], oT_ps[s % 2][:, :, :], oT_hi[:, ring].bitcast(F32),
                                      ALU.subtract).then_inc(oT_lo_done, 1)
                before_it = s - LAG - 2
                if 0 <= before_it < TILES:
                    par = before_it % 2
                    dve.wait_ge(root_done, before_it + 1)
                    wait(dve, x1_done, before_it - 1)
                    dve.reciprocal(scale[:, par:par + 1], root[:, par:par + 1]).then_inc(scale_done, 1)
                for b, name, i in reversed(stages(s)):
                    if name in steps_of and i == 0:
                        steps_of[name](b)
                tile = s - LAG
                if 0 <= tile < TILES:
                    dve.wait_ge(y_ready, tile + 1)
                    dve.wait_ge(xb_done, tile // TB + 1)
                    dve.tensor_tensor(x1[:, tile, :], y_ps[tile % 2][:, :], x1[:, tile, :], ALU.add
                                      ).then_inc(z_done, 1)
                if 0 <= before_it < TILES:
                    dve.wait_ge(scale_done, before_it + 1)
                    dve.scalar_tensor_tensor(out=shift[:, par:par + 1], in0=moments[:, par, 0:1], scalar=-1.0,
                                             in1=scale[:, par:par + 1], op0=ALU.mult, op1=ALU.mult
                                             ).then_inc(shift_done, 1)
                if 0 <= tile < TILES:
                    par = tile % 2
                    dve.wait_ge(z_done, tile + 1)
                    dve.bn_stats(stats[:, par, :], x1[:, tile, :]).then_inc(stats_done, 1)
                    dve.wait_ge(stats_done, tile + 1)
                    wait(dve, shift_done, tile - 1)
                    dve.bn_aggr(moments[:, par, :], stats[:, par, :]).then_inc(moments_done, 1)


def build_experts(nc, weights, x2, send_to, xe_dram, late_sent, out, const):
    EX, D, HID = weights.W1.shape
    B, N, _ = out.shape
    KC = D // P
    HC = HID // P
    ROWL = xe_dram.shape[1]
    ID, GATE = D, D + 1
    R = B * N // EX
    RT = R // P
    TB = N // P
    PASSES = [(0, 0, EARLY_BATCHES), (0, EARLY_BATCHES, RT)] + [(e, 0, RT) for e in range(1, EX)]
    assert RT == B
    XE_RING = 3
    assert R == BANK
    ident = const[0]
    with ExitStack() as ctx:
        def sb(name, shape, dt=F32):
            return ctx.enter_context(nc.sbuf_tensor(name, shape, dt))

        def sem(name):
            return ctx.enter_context(nc.semaphore(name))

        def split_pair(name, shape):
            return sb(name + "_hi", shape, F32R), sb(name + "_lo", shape, F32R)

        w1, w2 = zip(weights.high, weights.low)
        xe = sb("xe", [P, XE_RING, RT, ROWL])
        xeT = split_pair("xeT", [P, KC, R])
        h_act = sb("h_act", [P, 2, R])
        h = split_pair("h", [P, HC, R])
        y = sb("y", [P, 2, RT, D])
        eps = sb("eps3", [P, 1])
        stats = sb("stats3", [P, 2, RT, 6])
        moments = sb("moments3", [P, 2, RT, 2])
        root = sb("root3", [P, 2, RT])
        scale = sb("scale3", [P, 2, RT])
        xeT_ps = ctx.enter_context(nc.psum_tensor("xeT_ps", [P, KC, R], F32))
        h_ps = [ctx.enter_context(nc.psum_tensor(f"h_ps{i}", [P, R], F32)) for i in range(2)]
        y_ps = [ctx.enter_context(nc.psum_tensor(f"y_ps{i}", [P, D], F32)) for i in range(RT)]

        xe_in = [sem(f"xe_in{i}") for i in range(XE_RING)]
        xe_first_in = sem("xe_first_in")
        xeT_ready = sem("xeT_ready")
        xeT_hi_done = sem("xeT_hi_done")
        xeT_done = sem("xeT_done")
        h_ready = sem("h_ready")
        gelu_done = sem("gelu_done")
        h_hi_done = sem("h_hi_done")
        h_done = sem("h_done")
        y_ready = sem("y_ready")
        z_done = sem("z3_done")
        sent = [sem(f"out_sent{i}") for i in range(2)]
        eps_set = sem("eps3_set")
        stats_done = sem("stats3_done")
        moments_done = sem("moments3_done")
        root_done = sem("root3_done")
        scale_done = sem("scale3_done")
        out_done = sem("out_done")
        block = ctx.enter_context(nc.Block())

        def wait_sent(eng, e):
            if e >= 0:
                eng.wait_ge(sent[e % 2], 16 * RT * (e // 2 + 1))

        out_rows = out.rearrange("b n d -> (b n) d")
        LAST = HC - 1
        products = ((0, 0), (0, 1), (1, 0))

        @block.sync
        def _(sp):
            def load_xe(e, tiles, done):
                wait_sent(sp, e - XE_RING)
                rows = xe_dram[e * R + tiles[0] * P:e * R + tiles[1] * P, :]
                sp.dma_start(xe[:, e % XE_RING, tiles[0]:tiles[1]], rows.rearrange("(t p) d -> p t d", p=P)
                             ).then_inc(done, 16)

            load_xe(0, (0, EARLY_BATCHES), xe_first_in)
            sp.wait_ge(late_sent, 16 * TB * (B - EARLY_BATCHES))
            load_xe(0, (EARLY_BATCHES, RT), xe_in[0])
            load_xe(1, (0, RT), xe_in[1])
            for e in range(1, EX):
                weights.wait_split(sp, 0, e - 1)
                weights.load(sp, 0, e)
                weights.wait_split(sp, 1, e - 1)
                weights.load(sp, 1, e)
                if e + 1 < EX:
                    load_xe(e + 1, (0, RT), xe_in[(e + 1) % XE_RING])

        @block.gpsimd
        def _(pool):
            def split_w1(e):
                pool.wait_ge(h_ready, HC * (e + 1))
                weights.split_low(pool, 0, e)

            def split_w2(e):
                wait(pool, y_ready, RT * e)
                weights.split_low(pool, 1, e)

            def send(e):
                for t in range(RT):
                    pool.wait_ge(out_done, RT * e + t + 1)
                    token = xe[:, e % XE_RING, t, ID:ID + 1].bitcast(mybir.dt.uint32)
                    pool.indirect_dma_start(out=out_rows, out_offset=bass.IndirectOffsetOnAxis(ap=token, axis=0),
                                            in_=y[:, e % 2, t, :], in_offset=None).then_inc(sent[e % 2], 16)

            for t in range(TB * (B - 1), TB * B):
                pool.indirect_dma_start(out=xe_dram[:, :],
                                        out_offset=bass.IndirectOffsetOnAxis(ap=send_to[:, t:t + 1], axis=0),
                                        in_=x2[:, t, :], in_offset=None).then_inc(late_sent, 16)
            for e in range(EX):
                if e > 0:
                    split_w2(e)
                if e + 1 < EX:
                    split_w1(e + 1)
                if e > 0:
                    send(e - 1)
            send(EX - 1)
            wait_sent(pool, EX - 2)
            wait_sent(pool, EX - 1)

        @block.tensor
        def _(pe):
            def transpose_rows(p):
                e, t0, t1 = PASSES[p]
                if p == 0:
                    pe.wait_ge(xe_first_in, 16)
                else:
                    pe.wait_ge(xe_in[e % XE_RING], 16 * (e // XE_RING + 1))
                wait(pe, xeT_done, p)
                for k in range(KC):
                    for t in range(t0, t1):
                        last = pe.transpose(xeT_ps[:, k, t * P:(t + 1) * P], xe[:, e % XE_RING, t, k * P:(k + 1) * P],
                                            ident[:, :])
                last.then_inc(xeT_ready, 1)

            transpose_rows(0)
            for p, (e, t0, t1) in enumerate(PASSES):
                rows = slice(t0 * P, t1 * P)
                pe.wait_ge(xeT_done, p + 1)
                weights.wait_split(pe, 0, e)
                for c in range(HC):
                    n = p * HC + c
                    wait(pe, gelu_done, n - 1)
                    for i, (a, b) in enumerate(products):
                        for k in range(KC):
                            last = pe.matmul(h_ps[n % 2][:, rows], w1[a][:, k, c * P:(c + 1) * P], xeT[b][:, k, rows],
                                             start=(i == 0 and k == 0), stop=(i == 2 and k == KC - 1))
                    last.then_inc(h_ready, 1)
                if p + 1 < len(PASSES):
                    transpose_rows(p + 1)
                if t1 < RT:
                    continue
                weights.wait_split(pe, 1, e)
                wait(pe, z_done, RT * e)
                for chunks in (range(LAST), range(LAST, HC)):
                    pe.wait_ge(h_done, HC * p + chunks[-1] + 1)
                    for t in range(RT):
                        for c in chunks:
                            for i, (a, b) in enumerate(products):
                                last = pe.matmul(y_ps[t][:, :], h[a][:, c, t * P:(t + 1) * P], w2[b][:, c, :],
                                                 start=(c == 0 and i == 0), stop=(c == LAST and i == 2))
                        if chunks[-1] == LAST:
                            last.then_inc(y_ready, 1)

        @block.scalar
        def _(act):
            def split_w1(e):
                act.wait_ge(h_ready, HC * (e + 1))
                for j in range(weights.PIECES):
                    weights.split_high(act, 0, e, j)

            def split_w2(e, j):
                wait(act, y_ready, RT * e)
                weights.split_high(act, 1, e, j)

            def rows_high(p):
                e, t0, t1 = PASSES[p]
                rows = slice(t0 * P, t1 * P)
                act.wait_ge(xeT_ready, p + 1)
                if e > 0:
                    act.wait_ge(h_ready, HC * p)
                act.activation(xeT[0][:, :, rows], xeT_ps[:, :, rows], ACT.Copy).then_inc(xeT_hi_done, 1)

            def take_root(e):
                act.wait_ge(eps_set, 1)
                act.wait_ge(moments_done, RT * (e + 1))
                wait(act, scale_done, e - 1)
                act.activation(root[:, e % 2, :], moments[:, e % 2, :, 1], ACT.Sqrt, bias=eps[:, :]
                               ).then_inc(root_done, 1)

            rows_high(0)
            for p, (e, t0, t1) in enumerate(PASSES):
                rows = slice(t0 * P, t1 * P)
                for c in range(HC):
                    n = p * HC + c
                    act.wait_ge(h_ready, n + 1)
                    wait(act, h_done, n - 1)
                    act.activation(h_act[:, n % 2, rows], h_ps[n % 2][:, rows], ACT.Gelu_apprx_tanh
                                   ).then_inc(gelu_done, 1)
                    if e > 0 and c < weights.PIECES:
                        split_w2(e, c)
                if p + 1 < len(PASSES):
                    rows_high(p + 1)
                if t1 < RT:
                    continue
                if e + 1 < EX:
                    split_w1(e + 1)
                if e > 0:
                    take_root(e - 1)
            take_root(EX - 1)

        @block.vector
        def _(dve):
            dve.memset(eps[:, :], 1e-5).then_inc(eps_set, 1)

            def rows_low(p):
                rows = slice(PASSES[p][1] * P, PASSES[p][2] * P)
                dve.wait_ge(xeT_hi_done, p + 1)
                dve.tensor_tensor(xeT[1][:, :, rows], xeT_ps[:, :, rows], xeT[0][:, :, rows].bitcast(F32),
                                  ALU.subtract).then_inc(xeT_done, 1)

            def add_rows(e):
                for t in range(RT):
                    dve.wait_ge(y_ready, RT * e + t + 1)
                    wait_sent(dve, e - 2)
                    rows = xe[:, e % XE_RING, t]
                    dve.scalar_tensor_tensor(out=y[:, e % 2, t, :], in0=y_ps[t][:, :], scalar=rows[:, GATE:GATE + 1],
                                             in1=rows[:, 0:D], op0=ALU.mult, op1=ALU.add).then_inc(z_done, 1)
                for t in range(RT):
                    dve.wait_ge(z_done, RT * e + t + 1)
                    dve.bn_stats(stats[:, e % 2, t, :], y[:, e % 2, t, :]).then_inc(stats_done, 1)
                wait(dve, out_done, RT * (e - 1))
                for t in range(RT):
                    dve.wait_ge(stats_done, RT * e + t + 1)
                    dve.bn_aggr(moments[:, e % 2, t, :], stats[:, e % 2, t, :]).then_inc(moments_done, 1)

            def norm(e):
                dve.wait_ge(root_done, e + 1)
                dve.reciprocal(scale[:, e % 2, :], root[:, e % 2, :]).then_inc(scale_done, 1)
                dve.wait_ge(scale_done, e + 1)
                for t in range(RT):
                    dve.tensor_scalar(y[:, e % 2, t, :], y[:, e % 2, t, :], moments[:, e % 2, t, 0:1],
                                      scale[:, e % 2, t:t + 1], ALU.subtract, ALU.mult).then_inc(out_done, 1)

            rows_low(0)
            for p, (e, t0, t1) in enumerate(PASSES):
                rows = slice(t0 * P, t1 * P)
                wait(dve, y_ready, RT * e)
                for c in range(HC):
                    n = p * HC + c
                    dve.wait_ge(gelu_done, n + 1)
                    dve.tensor_copy(h[0][:, c, rows], h_act[:, n % 2, rows]).then_inc(h_hi_done, 1)
                    dve.wait_ge(h_hi_done, n + 1)
                    dve.tensor_tensor(h[1][:, c, rows], h_act[:, n % 2, rows], h[0][:, c, rows].bitcast(F32),
                                      ALU.subtract).then_inc(h_done, 1)
                if p + 1 < len(PASSES):
                    rows_low(p + 1)
                if t1 < RT:
                    continue
                if e > 0:
                    norm(e - 1)
                add_rows(e)
            norm(EX - 1)


def build(nc, x, ctx_in, Wq, Wk, Wv, Wp, bp, conv_w, conv_b, Wg, W1, W2, out):
    B, N, D = x.shape
    H, _, E = Wq.shape
    HID = W1.shape[2]
    TILES = B * N // P
    ROWL = D + 4
    xT_parts = nc.dram_tensor("xT_parts", [B, P, HILO, D // P, N], F32, kind="Internal").ap()
    o_dram = nc.dram_tensor("o_tokens", [B, N, H * E], F32, kind="Internal").ap()
    xe_dram = nc.dram_tensor("expert_rows", [B * N, ROWL], F32, kind="Internal").ap()
    with ExitStack() as ctx:
        const = build_constants(nc, ctx)
        xT = ctx.enter_context(nc.sbuf_tensor("xT", [P, HILO, D // P, N], F32R))
        qk_hi = ctx.enter_context(nc.sbuf_tensor("qk_hi", [P, 2, N], F32R))
        qk_lo = ctx.enter_context(nc.sbuf_tensor("qk_lo", [P, 2, N], F32R))
        early = ForProjection(nc, ctx, xT, qk_hi, qk_lo, o_dram, Wp)
        build_attention(nc, x, xT_parts, Wq, Wk, Wv, o_dram, const, xT, qk_hi, qk_lo, early)
        weights = ExpertWeights(nc, ctx, W1, W2)
        x2 = ctx.enter_context(nc.sbuf_tensor("x2", [P, TILES, ROWL], F32))
        send_to = ctx.enter_context(nc.sbuf_tensor("send_to", [P, TILES], mybir.dt.uint32))
        late_sent = ctx.enter_context(nc.semaphore("late_sent"))
        build_project_route(nc, o_dram, x, bp, ctx_in, conv_w, conv_b, Wg, x2, send_to, xe_dram, late_sent, early,
                            weights, const)
        build_experts(nc, weights, x2, send_to, xe_dram, late_sent, out, const)


_INS = ['x', 'ctx_1024', 'L0_attn_Wq', 'L0_attn_Wk', 'L0_attn_Wv', 'L0_attn_Wp', 'L0_attn_bp',
        'L0_xattn_conv_w', 'L0_xattn_conv_b', 'L0_ffn_Wg', 'L0_ffn_W1', 'L0_ffn_W2']


def kernel(**inputs):
    import numpy as _np
    import concourse.bacc as _bacc
    from concourse import mybir as _mybir
    from concourse.bass_utils import run_bass_kernel_spmd as _run

    nc = _bacc.Bacc("TRN2", target_bir_lowering=False, num_devices=1)
    arrays, args = {}, []
    for name in _INS:
        a = _np.ascontiguousarray(inputs[name])
        arrays[f"in_{name}_dram"] = a
        args.append(nc.dram_tensor(f"in_{name}_dram", a.shape, _mybir.dt.from_np(a.dtype), kind="ExternalInput").ap())
    shape = inputs['x'].shape
    args.append(nc.dram_tensor("out_dram", shape, _mybir.dt.float32, kind="ExternalOutput").ap())
    build(nc, *args)
    r = _run(nc, [arrays], core_ids=[0])
    return r.results[0]["out_dram"]
```
